# Optimizing a Trainium2 kernel written in Bass

```python
import numpy as np
import jax
import jax.numpy as jnp

def _softmax(x, axis=-1):
    return jax.nn.softmax(x, axis=axis)

def _gelu(x):
    return jax.nn.gelu(x, approximate=True)

def _silu(x):
    return jax.nn.silu(x)

def _sigmoid(x):
    return jax.nn.sigmoid(x)

def _layernorm(x, axis=-1, eps=1e-05):
    m = jnp.mean(x, axis=axis, keepdims=True)
    v = jnp.var(x, axis=axis, keepdims=True)
    return (x - m) / jnp.sqrt(v + eps)

def _scatter_add(tgt, idx, src, axis=0):
    return tgt.at[idx].add(src)

def _segment_sum(src, seg, n):
    return jax.ops.segment_sum(src, seg, n)
kernel_name = 'mk_xattn_ffn_d1_seqx_r4_1746db'

def setup_inputs(seed: int=0):
    np.random.seed(seed)
    _w = jnp.asarray

    def _rec_inputs():
        import jax
        import jax.numpy as jnp
        _rk = jax.random.key(seed)
        x = -0.0003929 + 0.9999 * jax.random.normal(jax.random.fold_in(_rk, 1), (16, 100, 512), jnp.float32)
        _lenS = 100 - jax.random.randint(jax.random.fold_in(_rk, 7), (16,), 0, max(1, 100 // 4) + 1, jnp.int32)
        _lenS2 = 361 - jax.random.randint(jax.random.fold_in(_rk, 8), (16,), 0, max(1, 361 // 4) + 1, jnp.int32)
        _ctx_1024P = jax.random.normal(jax.random.fold_in(_rk, 11), (16, 16, 256), jnp.float32)
        _ctx_1024c = jax.random.dirichlet(jax.random.fold_in(_rk, 511), 0.3 * jnp.ones((16,), jnp.float32), (16, 361))
        _ctx_1024t = jnp.einsum('bsk,bkd->bsd', _ctx_1024c, _ctx_1024P)
        _ctx_1024t = _ctx_1024t * jax.lax.rsqrt(jnp.mean(jnp.square(_ctx_1024t)) + 1e-12) * 0.953939
        ctx_1024 = 0.000227908 + 0.99994 * (_ctx_1024t + 0.3 * jax.random.normal(jax.random.fold_in(_rk, 611), (16, 361, 256), jnp.float32))
        return (x, ctx_1024)
    x, ctx_1024 = _rec_inputs()

    def _L0_xattn_setup():
        import jax, jax.numpy as jnp
        import numpy as np
        EPS = 1e-05

        def rmsnorm(x, g, eps=EPS):
            var = jnp.mean(jnp.square(x), axis=-1, keepdims=True)
            return x * jax.lax.rsqrt(var + eps) * g
        key = jax.random.key(seed)
        ks = jax.random.split(key, 8)
        B, Sq, Skv = (2, 1024, 128)
        dim, cdim, H, D = (512, 256, 16, 128)
        inner = H * D
        s = lambda f: 1.0 / np.sqrt(f)
        return {'hidden_states': jax.random.normal(ks[0], (B, Sq, dim), jnp.float32), 'encoder_hidden_states': jax.random.normal(ks[1], (B, Skv, cdim), jnp.float32), 'Wq': jax.random.normal(ks[2], (dim, inner), jnp.float32) * s(dim), 'Wk': jax.random.normal(ks[3], (cdim, inner), jnp.float32) * s(cdim), 'Wv': jax.random.normal(ks[4], (cdim, inner), jnp.float32) * s(cdim), 'Wo': jax.random.normal(ks[5], (inner, dim), jnp.float32) * s(inner), 'gq': jnp.ones((D,), jnp.float32), 'gk': jnp.ones((D,), jnp.float32)}
    _L0_xattn_all = _L0_xattn_setup()
    _L0_xattn_in = {k: v for k, v in _L0_xattn_all.items() if k in ('Wq', 'Wk', 'Wv', 'Wo', 'gq', 'gk')}
    del _L0_xattn_all

    def _L0_ffn_setup():
        import jax, jax.numpy as jnp
        import numpy as np
        EPS = 1e-05

        def fwht(x):
            orig_shape = x.shape
            n = orig_shape[-1]
            x = x.reshape(-1, n)
            h = 1
            while h < n:
                x = x.reshape(-1, n // (2 * h), 2, h)
                a, b = (x[:, :, 0, :], x[:, :, 1, :])
                x = jnp.stack([a + b, a - b], axis=2).reshape(-1, n)
                h *= 2
            return (x * (1.0 / np.sqrt(n))).reshape(orig_shape)

        def act_quant(x):
            scale = 127.0 / jnp.clip(jnp.max(jnp.abs(x), axis=-1, keepdims=True), EPS)
            q = jnp.clip(jnp.round(x * scale), -128.0, 127.0) / scale
            return x + jax.lax.stop_gradient(q - x)

        def weight_quant(w):
            scale = jnp.clip(jnp.mean(jnp.abs(w)), EPS)
            q = jnp.clip(jnp.round(w / scale), -1.0, 1.0) * scale
            return w + jax.lax.stop_gradient(q - w)

        def h_bitlinear(x, w):
            xq = act_quant(fwht(x))
            wq = weight_quant(w)
            return jnp.einsum('bsh,oh->bso', xq, wq)
        key = jax.random.key(seed)
        k1, k2, k3, k4 = jax.random.split(key, 4)
        H, I = (512, 2048)
        B, S = (2, 512)
        hidden_states = jax.random.normal(k1, (B, S, H), dtype=jnp.float32)
        w_gate = jax.random.normal(k2, (I, H), dtype=jnp.float32) * 0.02
        w_up = jax.random.normal(k3, (I, H), dtype=jnp.float32) * 0.02
        w_down = jax.random.normal(k4, (H, I), dtype=jnp.float32) * 0.02
        return {'hidden_states': hidden_states, 'w_gate': w_gate, 'w_up': w_up, 'w_down': w_down}
    _L0_ffn_all = _L0_ffn_setup()
    _L0_ffn_in = {k: v for k, v in _L0_ffn_all.items() if k in ('w_gate', 'w_up', 'w_down')}
    del _L0_ffn_all
    return {'x': x, 'ctx_1024': ctx_1024, 'L0_xattn_Wq': _L0_xattn_in['Wq'], 'L0_xattn_Wk': _L0_xattn_in['Wk'], 'L0_xattn_Wv': _L0_xattn_in['Wv'], 'L0_xattn_Wo': _L0_xattn_in['Wo'], 'L0_xattn_gq': _L0_xattn_in['gq'], 'L0_xattn_gk': _L0_xattn_in['gk'], 'L0_ffn_w_gate': _L0_ffn_in['w_gate'], 'L0_ffn_w_up': _L0_ffn_in['w_up'], 'L0_ffn_w_down': _L0_ffn_in['w_down']}

def reference(x, ctx_1024, L0_xattn_Wq, L0_xattn_Wk, L0_xattn_Wv, L0_xattn_Wo, L0_xattn_gq, L0_xattn_gk, L0_ffn_w_gate, L0_ffn_w_up, L0_ffn_w_down):
    import jax
    import jax.numpy as jnp

    def _L0_xattn_ref(hidden_states, encoder_hidden_states, Wq, Wk, Wv, Wo, gq, gk):
        import jax, jax.numpy as jnp
        import numpy as np
        EPS = 1e-05

        def rmsnorm(x, g, eps=EPS):
            var = jnp.mean(jnp.square(x), axis=-1, keepdims=True)
            return x * jax.lax.rsqrt(var + eps) * g
        B, Sq, _ = hidden_states.shape
        Skv = encoder_hidden_states.shape[1]
        D = gq.shape[0]
        H = Wq.shape[1] // D
        scale = 1.0 / np.sqrt(D)
        q = (hidden_states @ Wq).reshape(B, Sq, H, D)
        k = (encoder_hidden_states @ Wk).reshape(B, Skv, H, D)
        v = (encoder_hidden_states @ Wv).reshape(B, Skv, H, D)
        q = rmsnorm(q, gq)
        k = rmsnorm(k, gk)
        scores = jnp.einsum('bqhd,bkhd->bhqk', q, k) * scale
        attn = jax.nn.softmax(scores, axis=-1)
        out = jnp.einsum('bhqk,bkhd->bqhd', attn, v)
        out = out.reshape(B, Sq, H * D)
        return out @ Wo

    def _L0_ffn_ref(hidden_states, w_gate, w_up, w_down):
        import jax, jax.numpy as jnp
        import numpy as np
        EPS = 1e-05

        def fwht(x):
            orig_shape = x.shape
            n = orig_shape[-1]
            x = x.reshape(-1, n)
            h = 1
            while h < n:
                x = x.reshape(-1, n // (2 * h), 2, h)
                a, b = (x[:, :, 0, :], x[:, :, 1, :])
                x = jnp.stack([a + b, a - b], axis=2).reshape(-1, n)
                h *= 2
            return (x * (1.0 / np.sqrt(n))).reshape(orig_shape)

        def act_quant(x):
            scale = 127.0 / jnp.clip(jnp.max(jnp.abs(x), axis=-1, keepdims=True), EPS)
            q = jnp.clip(jnp.round(x * scale), -128.0, 127.0) / scale
            return x + jax.lax.stop_gradient(q - x)

        def weight_quant(w):
            scale = jnp.clip(jnp.mean(jnp.abs(w)), EPS)
            q = jnp.clip(jnp.round(w / scale), -1.0, 1.0) * scale
            return w + jax.lax.stop_gradient(q - w)

        def h_bitlinear(x, w):
            xq = act_quant(fwht(x))
            wq = weight_quant(w)
            return jnp.einsum('bsh,oh->bso', xq, wq)
        gate = h_bitlinear(hidden_states, w_gate)
        up = h_bitlinear(hidden_states, w_up)
        return h_bitlinear(jax.nn.silu(gate) * up, w_down)
    x = x + _L0_xattn_ref(_layernorm(x, axis=-1), ctx_1024, L0_xattn_Wq, L0_xattn_Wk, L0_xattn_Wv, L0_xattn_Wo, L0_xattn_gq, L0_xattn_gk)
    x = x + _L0_ffn_ref(_layernorm(x, axis=-1), L0_ffn_w_gate, L0_ffn_w_up, L0_ffn_w_down)
    return x

_drawn_inputs = setup_inputs


def setup_inputs(seed=0):
    import zlib

    import numpy as np

    out = dict(_drawn_inputs(seed))
    spreads = {'L0_xattn_gq': (1.0, 0.2), 'L0_xattn_gk': (1.0, 0.2)}
    factors = {}
    for name, (base, spread) in spreads.items():
        noise = np.random.default_rng([zlib.crc32(name.encode()), seed]).standard_normal(out[name].shape)
        drawn = base * np.exp(spread * noise) if base else spread * noise
        out[name] = jnp.asarray(drawn.astype(out[name].dtype))
    for name, factor in factors.items():
        out[name] = (out[name] * factor).astype(out[name].dtype)
    return out
```

```python
import concourse.bass as bass
from concourse import mybir
from contextlib import ExitStack

F32 = mybir.dt.float32
F32R = mybir.dt.float32r
BF16 = mybir.dt.bfloat16
FP8 = mybir.dt.float8e4
ALU = mybir.AluOpType
ACT = mybir.ActivationFunctionType
AX = mybir.AxisListType

P = 128
B, SQ, DIM = 16, 100, 512
SK, CD = 361, 256
H, D = 16, 128
INNER = H * D
FF = 2048
T = B * SQ
EPS = 1e-5
SKP = SK + 1
DC, CC, FC = DIM // P, CD // P, FF // P
HG = 4
NG = H // HG
KW = [121, 120, 120]
KO = [0, 121, 241]
GB = 4
GT = GB * SQ
G = B // GB
LAST_B = B - 1
MAGIC = 1.5 * 2.0 ** 23
TT = P
TILES = -(-T // TT)
LAST_TOK = T - TT


def build(nc, x, ctxT, ctx_k, wq, wk, wv, wo, gq, gk, w_ff, ident_in, had_in, out):
    q_dram = nc.dram_tensor("q_dram", [B, D, H, SQ], F32, kind="Internal").ap()
    rk_dram = nc.dram_tensor("rk_dram", [2, HG * SK], F32, kind="Internal").ap()
    o_dram = nc.dram_tensor("o_dram", [H, D, T], F32, kind="Internal").ap()
    with ExitStack() as top:
        def sbt(ctx, name, shape, dt=F32):
            return ctx.enter_context(nc.sbuf_tensor(name, shape, dt))

        def sem(ctx, name):
            return ctx.enter_context(nc.semaphore(name))

        ident = sbt(top, "ident", [P, P])
        rq_all = sbt(top, "rq_all", [SQ, B, H])
        neg_half = sbt(top, "neg_half", [P, 1])
        with ExitStack() as ctx:
            weights = {
                "wk_hi": sbt(ctx, "wk_hi", [P, CC, INNER], F32R),
                "wk_lo": sbt(ctx, "wk_lo", [P, CC, INNER], F32R),
                "wv": sbt(ctx, "wv_sb", [P, CC, INNER]),
                "sel": sbt(ctx, "sel", [P, 2 * P - 1], F32R),
            }
            queries(nc, sbt, sem, weights, ident, rq_all, neg_half, x, wq, wk, wv, gq, gk, ident_in, q_dram)
            attention(nc, sbt, sem, weights, ident, rq_all, neg_half, ctxT, ctx_k, q_dram, rk_dram, o_dram)
        feed_forward(nc, sbt, sem, ident, neg_half, x, wo, w_ff, had_in, o_dram, out)


def wait(eng, sem, count):
    if not (isinstance(count, int) and count <= 0):
        eng.wait_ge(sem, count)


def held(eng, value):
    return value if isinstance(value, int) else eng.snap(value)


def apart(eng, passed):
    eng.sem_inc(passed, 1)


def queries(nc, sbt, sem, weights, ident, rq_all, neg_half, x, wq, wk, wv, gq, gk, ident_in, q_dram):
    wk_hi, wk_lo, wv_sb, sel = (weights[k] for k in ("wk_hi", "wk_lo", "wv", "sel"))
    QW = HG * D
    KWD = INNER // 2
    with ExitStack() as ctx:
        sb = lambda name, shape, dt=F32: sbt(ctx, name, shape, dt)
        s = lambda name: sem(ctx, name)
        wq_hi, wq_lo = sb("wq_hi", [P, DC, INNER], F32R), sb("wq_lo", [P, DC, INNER], F32R)
        stage = sb("stage", [P, 2, DC * QW])
        x_in = sb("x_in", [SQ, GB, DIM])
        xn = sb("xn", [SQ, GB, DIM])
        st, mv = sb("st", [SQ, GB, 6]), sb("mv", [SQ, GB, 2])
        ve, rstd = sb("ve", [SQ, GB]), sb("rstd", [SQ, GB])
        xT_hi, xT_lo = sb("xT_hi", [P, DC, GT], F32R), sb("xT_lo", [P, DC, GT], F32R)
        gqk, gk_sb = sb("gqk", [P, 1]), sb("gk_sb", [P, 1])
        gprod = sb("gprod", [P, 1])
        q_out = sb("q_out", [P, 2, GT])
        sq = sb("sq1", [P, 2, GT])
        sq_hi, sq_lo = sb("sq1_hi", [P, 2, GT], F32R), sb("sq1_lo", [P, 2, GT], F32R)
        ms, rqT = sb("ms1", [H, GT]), sb("rqT", [H, GT])
        psQ = [ctx.enter_context(nc.psum_tensor(f"psQ{i}", [P, 512], F32)) for i in range(2)]
        psX = [ctx.enter_context(nc.psum_tensor(f"psX{i}", [P, DC, SQ], F32)) for i in range(GB)]
        psS = ctx.enter_context(nc.psum_tensor("psS1", [P, 512], F32))
        psR = ctx.enter_context(nc.psum_tensor("psR", [P, GB, H], F32))

        d_x, d_g, d_id, d_wv = s("d1_x"), s("d1_g"), s("d1_id"), s("d1_wv")
        d_st = [s("d1_st0"), s("d1_st1")]
        d_q = [s("d1_q0"), s("d1_q1")]
        g_const, g_rstd, g_rq = s("g1_const"), s("g1_rstd"), s("g1_rq")
        v_gain, v_stat, v_agg, v_ve, v_xn = s("v1_gain"), s("v1_stat"), s("v1_agg"), s("v1_ve"), s("v1_xn")
        a_whi, v_wlo = s("a1_whi"), s("v1_wlo")
        p_xT, a_xhi, v_xlo = s("p1_xT"), s("a1_xhi"), s("v1_xlo")
        p_q, a_q, v_sqhi, v_sqlo = s("p1_q"), s("a1_q"), s("v1_sqhi"), s("v1_sqlo")
        p_ss, v_ms, p_rq, v_rq = s("p1_ss"), s("v1_ms"), s("p1_rq"), s("v1_rq")

        pieces = []
        for j in range(4):
            cols = slice(j * QW, (j + 1) * QW)
            pieces.append((wq.rearrange("(c p) n -> p c n", p=P)[:, :, cols], wq_hi[:, :, cols], wq_lo[:, :, cols]))
        for j in range(2):
            cols = slice(j * KWD, (j + 1) * KWD)
            pieces.append((wk.rearrange("(c p) n -> p c n", p=P)[:, :, cols], wk_hi[:, :, cols], wk_lo[:, :, cols]))

        def staged(i):
            c = pieces[i][1].shape[1]
            return stage[:, i % 2, :].rearrange("p (c n) -> p c n", c=c)

        SPLIT_AT = {0: 1, 2: 2, 4: 3, 8: 4, 10: 5}

        pe_passed, dve_passed = s("pe_passed1"), s("dve_passed1")
        block = ctx.enter_context(nc.Block())

        @block.sync
        def _(sp):
            xg = x.rearrange("(b q) n -> q b n", q=SQ)
            sp.dma_start(x_in[:], xg[:, 0:GB, :]).then_inc(d_x, 16)
            sp.dma_start(ident[:], ident_in).then_inc(d_id, 16)
            sp.dma_start(gqk[:], gq.rearrange("(p a) -> p a", a=1)).then_inc(d_g, 16)
            sp.dma_start(gk_sb[:], gk.rearrange("(p a) -> p a", a=1)).then_inc(d_g, 16)

            def load_piece(i):
                wait(sp, v_wlo, i - 1)
                sp.dma_start(staged(i), pieces[i][0]).then_inc(d_st[i % 2], 16)

            for i in range(4):
                load_piece(i)
            sp.dma_start(wv_sb[:], wv.rearrange("(c p) n -> p c n", p=P)).then_inc(d_wv, 16)

            def group(g, last):
                if not last:
                    nxt = held(sp, (g + 1) * GB)
                    src = xg[:, bass.ds(nxt, GB), :]
                    wait(sp, v_xn, nxt)
                    sp.dma_start(x_in[:], src).then_inc(d_x, 16)
                for h in range(H):
                    dst = q_dram[bass.ds(held(sp, g * GB), GB), :, h, :].rearrange("b d q -> d b q")
                    wait(sp, a_q, held(sp, g * H + h + 1))
                    sp.dma_start(dst, q_out[:, h % 2, :].rearrange("p (b q) -> p b q", q=SQ)).then_inc(d_q[h % 2], 16)
                    if isinstance(g, int) and g == 0 and h in (1, 3):
                        load_piece(4 + h // 2)

            group(0, False)
            with sp.Fori(1, G - 1) as g:
                group(g, False)
            group(G - 1, True)
            for i in range(2):
                sp.wait_ge(d_q[i], 16 * G * H // 2)
            sp.wait_ge(d_wv, 16)

        @block.gpsimd
        def _(pool):
            nc.gpsimd.memset(neg_half[:], -0.5).then_inc(g_const, 1)
            nc.gpsimd.memset(sel[:].bitcast(F32), 0.0).then_inc(g_const, 1)
            pool.wait_ge(g_const, 2)
            nc.gpsimd.memset(sel[:, P - 1:P].bitcast(F32), 1.0).then_inc(g_const, 1)

            def norm(g):
                wait(pool, v_ve, g + 1)
                nc.gpsimd.tensor_tensor(rstd[:], ve[:], neg_half[0:SQ, :].to_broadcast([SQ, GB]),
                                        op=ALU.pow).then_inc(g_rstd, 1)

            def rms(g):
                wait(pool, v_ms, g + 1)
                nc.gpsimd.tensor_tensor(rqT[:], ms[:], neg_half[0:H, :].to_broadcast([H, GT]),
                                        op=ALU.pow).then_inc(g_rq, 1)

            norm(0)
            norm(1)
            rms(0)
            with pool.Fori(1, G - 1) as g:
                norm(g + 1)
                rms(g)
            rms(G - 1)

        @block.tensor
        def _(pe):
            pe.wait_ge(d_id, 16)
            pe.wait_ge(g_const, 3)

            def transposes(g):
                for b in range(GB):
                    wait(pe, v_xn, g * GB + b + 1)
                    wait(pe, v_xlo, (g - 1) * GB + b + 1)
                    for c in range(DC):
                        last = nc.tensor.transpose(psX[b][:, c, :], xn[:, b, c * P:(c + 1) * P], ident[0:SQ, 0:SQ])
                    last.then_inc(p_xT, 1)

            def squares(g, h):
                wait(pe, v_sqlo, g * H + h + 1)
                if h == 0:
                    wait(pe, v_ms, g)
                for part in (sq_hi, sq_lo):
                    last = nc.tensor.matmul(psS[:, 0:GT], sel[:, P - 1 - h:2 * P - 1 - h], part[:, h % 2, :],
                                            start=(h == 0 and part is sq_hi), stop=(h == H - 1 and part is sq_lo))
                last.then_inc(p_ss, 1)

            def factors(g):
                wait(pe, g_rq, g + 1)
                wait(pe, v_rq, g)
                apart(pe, pe_passed)
                for b in range(GB):
                    last = nc.tensor.transpose(psR[0:SQ, b, :], rqT[:, b * SQ:(b + 1) * SQ], ident[0:H, 0:H])
                last.then_inc(p_rq, 1)

            def group(g, first, last_group):
                for h in range(H):
                    if first and h % HG == 0:
                        pe.wait_ge(v_wlo, h // HG + 1)
                    if h == 0:
                        wait(pe, v_xlo, (g + 1) * GB)
                    wait(pe, a_q, g * H + h - 1)
                    n = 0
                    for c in range(DC):
                        for w, m in ((wq_hi, xT_hi), (wq_hi, xT_lo), (wq_lo, xT_hi)):
                            last = nc.tensor.matmul(psQ[h % 2][:, 0:GT], w[:, c, h * D:(h + 1) * D], m[:, c, :],
                                                    start=(n == 0), stop=(n == 3 * DC - 1))
                            n += 1
                    last.then_inc(p_q, 1)
                    if h >= 1:
                        squares(g, h - 1)
                    if h == 3 and not first:
                        factors(g - 1)
                    if h == 8 and not last_group:
                        transposes(g + 1)
                squares(g, H - 1)

            transposes(0)
            group(0, True, False)
            with pe.Fori(1, G - 1) as g:
                group(g, False, False)
            group(G - 1, False, True)
            factors(G - 1)

        @block.scalar
        def _(act):
            act.wait_ge(v_gain, 1)

            def split(i):
                act.wait_ge(d_st[i % 2], 16 * (i // 2 + 1))
                nc.scalar.activation(pieces[i][1], staged(i), ACT.Copy).then_inc(a_whi, 1)

            def group(g, first):
                for b in range(GB):
                    wait(act, p_xT, g * GB + b + 1)
                    if b == 0:
                        wait(act, p_q, g * H)
                    nc.scalar.activation(xT_hi[:, :, b * SQ:(b + 1) * SQ], psX[b][:], ACT.Copy).then_inc(a_xhi, 1)
                for h in range(H):
                    if first and h in SPLIT_AT:
                        split(SPLIT_AT[h])
                    wait(act, p_q, g * H + h + 1)
                    n = (g * H + h) // 2 if isinstance(g, int) else g * (H // 2) + h // 2
                    wait(act, d_q[h % 2], n * 16)
                    nc.scalar.activation(q_out[:, h % 2, :], psQ[h % 2][:, 0:GT], ACT.Copy, scale=gprod[:])
                    wait(act, v_sqlo, g * H + h - 1)
                    nc.scalar.activation(sq[:, h % 2, :], psQ[h % 2][:, 0:GT], ACT.Square).then_inc(a_q, 1)

            split(0)
            group(0, True)
            with act.Fori(1, G) as g:
                group(g, False)

        @block.vector
        def _(dve):
            dve.wait_ge(d_g, 32)
            nc.vector.tensor_tensor(gprod[:], gqk[:], gk_sb[:], ALU.mult).then_inc(v_gain, 1)
            dve.wait_ge(g_const, 1)

            def split(i):
                dve.wait_ge(a_whi, i + 1)
                nc.vector.tensor_tensor(pieces[i][2], staged(i), pieces[i][1].bitcast(F32),
                                        ALU.subtract).then_inc(v_wlo, 1)

            def norm(g):
                wait(dve, d_x, (g + 1) * 16)
                for b in range(GB):
                    nc.vector.bn_stats(st[:, b, :], x_in[:, b, :]).then_inc(v_stat, 1)
                for b in range(GB):
                    wait(dve, v_stat, g * GB + b + 1)
                    apart(dve, dve_passed)
                    nc.vector.bn_aggr(mv[:, b, :], st[:, b, :]).then_inc(v_agg, 1)
                wait(dve, v_agg, (g + 1) * GB)
                nc.vector.tensor_scalar(ve[:], mv[:, :, 1], EPS, None, ALU.add).then_inc(v_ve, 1)
                wait(dve, g_rstd, g + 1)
                for b in range(GB):
                    wait(dve, p_xT, (g - 1) * GB + b + 1)
                    nc.vector.tensor_scalar(xn[:, b, :], x_in[:, b, :], mv[:, b, 0:1], rstd[:, b:b + 1],
                                            ALU.subtract, ALU.mult).then_inc(v_xn, 1)

            def factors(g):
                wait(dve, p_rq, g + 1)
                nc.vector.tensor_scalar(rq_all[:, bass.ds(g * GB, GB), :], psR[0:SQ, :, :], D ** -0.5, None,
                                        ALU.mult).then_inc(v_rq, 1)

            def group(g, first, last):
                for b in range(GB):
                    wait(dve, a_xhi, g * GB + b + 1)
                    nc.vector.tensor_tensor(xT_lo[:, :, b * SQ:(b + 1) * SQ], psX[b][:],
                                            xT_hi[:, :, b * SQ:(b + 1) * SQ].bitcast(F32),
                                            ALU.subtract).then_inc(v_xlo, 1)
                for h in range(H):
                    if first and h in SPLIT_AT:
                        split(SPLIT_AT[h])
                    if h == 5 and not last:
                        norm(g + 1)
                    if h == 5 and not first:
                        factors(g - 1)
                    wait(dve, a_q, g * H + h + 1)
                    wait(dve, p_ss, g * H + h - 1)
                    nc.vector.tensor_copy(sq_hi[:, h % 2, :], sq[:, h % 2, :]).then_inc(v_sqhi, 1)
                    wait(dve, v_sqhi, g * H + h + 1)
                    nc.vector.tensor_tensor(sq_lo[:, h % 2, :], sq[:, h % 2, :], sq_hi[:, h % 2, :].bitcast(F32),
                                            ALU.subtract).then_inc(v_sqlo, 1)
                wait(dve, p_ss, (g + 1) * H)
                if not first:
                    wait(dve, g_rq, g)
                nc.vector.tensor_scalar(ms[:], psS[0:H, 0:GT], 1.0 / D, EPS, ALU.mult, ALU.add).then_inc(v_ms, 1)

            norm(0)
            split(0)
            group(0, True, False)
            with dve.Fori(1, G - 1) as g:
                group(g, False, False)
            group(G - 1, False, True)
            factors(G - 1)


def attention(nc, sbt, sem, weights, ident, rq_all, neg_half, ctxT, ctx_k, q_dram, rk_dram, o_dram):
    wk_hi, wk_lo, wv_sb, sel = (weights[k] for k in ("wk_hi", "wk_lo", "wv", "sel"))
    UQ = HG * SQ
    with ExitStack() as ctx:
        sb = lambda name, shape, dt=F32: sbt(ctx, name, shape, dt)
        s = lambda name: sem(ctx, name)
        cT_in, cT_hi, cT_lo = sb("cT_in", [P, CC, SK]), sb("cT_hi", [P, CC, SKP], F32R), sb("cT_lo", [P, CC, SKP], F32R)
        cK_in, cK_hi, cK_lo = sb("cK_in", [P, 3, CD]), sb("cK_hi", [P, 3, CD], F32R), sb("cK_lo", [P, 3, CD], F32R)
        q_in = sb("q_in", [P, 2, UQ])
        q_hi, q_lo = sb("q_hi", [P, 2, UQ], F32R), sb("q_lo", [P, 2, UQ], F32R)
        rq = sb("rq", [SQ, 2, HG])
        k_hi, k_lo = sb("k_hi", [P, NG, HG, SKP], F32R), sb("k_lo", [P, NG, HG, SKP], F32R)
        sq = sb("sq2", [P, 2, SKP])
        sq_hi, sq_lo = sb("sq2_hi", [P, 2, SKP], F32R), sb("sq2_lo", [P, 2, SKP], F32R)
        ms, rkT = sb("ms2", [HG, SK]), sb("rkT", [HG, SK])
        rk = sb("rk", [SQ, 2, HG, SK])
        sc = sb("sc", [SQ, 2, SK])
        mx, nb, rs, ri = (sb(n, [SQ, 2]) for n in ("mx", "nb", "rs", "ri"))
        ex, pr = sb("ex", [SQ, 2, SK]), sb("pr", [SQ, 2, SK])
        pT_hi, pT_lo = sb("pT_hi", [P, 2, 3, UQ], F32R), sb("pT_lo", [P, 2, 3, UQ], F32R)
        z = sb("z", [P, CC, UQ])
        o = sb("o", [P, 2, UQ])
        psK = [ctx.enter_context(nc.psum_tensor(f"psK{i}", [P, 512], F32)) for i in range(2)]
        psN = ctx.enter_context(nc.psum_tensor("psN", [P, 512], F32))
        psS = ctx.enter_context(nc.psum_tensor("psS2", [P, 512], F32))
        psP = ctx.enter_context(nc.psum_tensor("psP", [P, 512], F32))
        psZ = [ctx.enter_context(nc.psum_tensor(f"psZ{i}", [P, 512], F32)) for i in range(CC)]
        psV = ctx.enter_context(nc.psum_tensor("psV", [P, 512], F32))

        d_cT, d_cK, d_rs = s("d2_cT"), s("d2_cK"), s("d2_rs")
        d_q, d_rb, d_o = ([s(f"d2_{n}{i}") for i in range(2)] for n in ("q", "rb", "o"))
        a_cT, v_cT, a_cK, v_cK, v_zero = s("a2_cT"), s("v2_cT"), s("a2_cK"), s("v2_cK"), s("v2_zero")
        a_q, v_q, v_rq = s("a2_q"), s("v2_q"), s("v2_rq")
        p_k, a_k, v_klo, v_sqhi, g_sqlo = s("p2_k"), s("a2_k"), s("v2_klo"), s("v2_sqhi"), s("g2_sqlo")
        p_ss, v_ms, g_rk = s("p2_ss"), s("v2_ms"), s("g2_rk")
        p_s, v_max, v_nb, a_ex, v_ri, v_pr = s("p2_s"), s("v2_max"), s("v2_nb"), s("a2_ex"), s("v2_ri"), s("v2_pr")
        p_t, a_pT, v_pT = s("p2_t"), s("a2_pT"), s("v2_pT")
        p_z, a_z, v_z, p_v, a_o = s("p2_z"), s("a2_z"), s("v2_z"), s("p2_v"), s("a2_o")

        sp_passed, dve_passed = s("sp_passed2"), s("dve_passed2")
        block = ctx.enter_context(nc.Block())

        def batches(eng, body):
            body(0, True, False)
            with eng.Fori(1, B - 1) as b:
                body(b, False, False)
            body(B - 1, False, True)

        @block.sync
        def _(sp):
            def load_q(b, j, split):
                src = q_dram[bass.ds(held(sp, b), 1), :, j * HG:(j + 1) * HG, :].rearrange("a d h q -> d (a h) q")
                wait(sp, v_q, held(sp, split))
                sp.dma_start(q_in[:, j % 2, :].rearrange("p (h q) -> p h q", q=SQ), src).then_inc(d_q[j % 2], 16)

            def load_cT(b):
                b = held(sp, b)
                src = ctxT[bass.ds(b, 1)].rearrange("a (c p) k -> p (a c) k", p=P)
                wait(sp, v_cT, b)
                sp.dma_start(cT_in[:], src).then_inc(d_cT, 16)

            def load_cK(b):
                b = held(sp, b)
                src = [ctx_k[bass.ds(b, 1), KO[i]:KO[i] + KW[i], :].rearrange("a k c -> k (a c)") for i in range(3)]
                wait(sp, v_cK, b)
                for i in range(3):
                    sp.dma_start(cK_in[0:KW[i], i, :], src[i]).then_inc(d_cK, 16)

            def spread_rk(slot, ready, stored):
                wait(sp, g_rk, ready)
                sp.dma_start(rk_dram[slot, :].rearrange("(h k) -> h k", k=SK), rkT[:]).then_inc(d_rs, 16)
                wait(sp, d_rs, stored)
                sp.dma_start(rk[:, slot, :, :].rearrange("p h k -> p (h k)"),
                             rk_dram[slot:slot + 1, :].to_broadcast([SQ, HG * SK])).then_inc(d_rb[slot], 16)

            load_cT(0)
            load_cK(0)
            load_q(0, 0, 0)
            load_q(0, 1, 0)
            spread_rk(0, 1, 16)

            def body(b, first, last):
                for j in range(NG):
                    u = b * NG + j
                    if j == 0 and not last:
                        load_cT(b + 1)
                    if j == 1 and not last:
                        load_cK(b + 1)
                    if not (last and j >= 2):
                        load_q(b + (j + 2) // NG, (j + 2) % NG, u + 1)
                    if not (last and j == NG - 1):
                        spread_rk((j + 1) % 2, held(sp, u + 2), held(sp, u * 16 + 32))
                    if not (first and j == 0):
                        tok = held(sp, b * SQ - (SQ if j == 0 else 0))
                        jo = (j - 1) % NG
                        dst = o_dram[jo * HG:(jo + 1) * HG, :, bass.ds(tok, SQ)].rearrange("h d t -> d h t")
                        wait(sp, a_o, held(sp, u))
                        apart(sp, sp_passed)
                        sp.dma_start(dst, o[:, (j - 1) % 2, :].rearrange("p (h q) -> p h q", q=SQ)
                                     ).then_inc(d_o[(j - 1) % 2], 16)

            batches(sp, body)
            sp.wait_ge(a_o, B * NG)
            sp.dma_start(o_dram[(NG - 1) * HG:, :, LAST_B * SQ:].rearrange("h d t -> d h t"),
                         o[:, (NG - 1) % 2, :].rearrange("p (h q) -> p h q", q=SQ)).then_inc(d_o[(NG - 1) % 2], 16)
            for i in range(2):
                sp.wait_ge(d_o[i], 16 * B * NG // 2)

        @block.gpsimd
        def _(pool):
            def low_squares(m, slot):
                wait(pool, v_sqhi, m + 1)
                nc.gpsimd.tensor_tensor(sq_lo[:, slot, :], sq[:, slot, :], sq_hi[:, slot, :].bitcast(F32),
                                        op=ALU.subtract).then_inc(g_sqlo, 1)

            def rms(u):
                wait(pool, v_ms, u + 1)
                wait(pool, d_rs, u * 16)
                nc.gpsimd.tensor_tensor(rkT[:], ms[:], neg_half[0:HG, :].to_broadcast([HG, SK]),
                                        op=ALU.pow).then_inc(g_rk, 1)

            for m in range(2 * HG):
                low_squares(m, m % 2)
                if m == HG:
                    rms(0)

            def body(b, first, last):
                for j in range(NG):
                    u = b * NG + j
                    for h in range(HG):
                        if not (last and j >= 2):
                            low_squares(u * HG + 2 * HG + h, h % 2)
                        if h == 0 and not (last and j == NG - 1):
                            rms(u + 1)

            batches(pool, body)

        @block.tensor
        def _(pe):
            def keys(m, j, h):
                wait(pe, v_klo, m - 1)
                n = 0
                for c in range(CC):
                    col = (j * HG + h) * D
                    for w, x in ((wk_hi, cT_hi), (wk_hi, cT_lo), (wk_lo, cT_hi)):
                        last = nc.tensor.matmul(psK[h % 2][:, 0:SKP], w[:, c, col:col + D], x[:, c, :],
                                                start=(n == 0), stop=(n == 3 * CC - 1))
                        n += 1
                last.then_inc(p_k, 1)

            def squares(m, u, h):
                wait(pe, g_sqlo, m + 1)
                if h == 0:
                    wait(pe, v_ms, u)
                for part in (sq_hi, sq_lo):
                    last = nc.tensor.matmul(psN[:, 0:SKP], sel[:, P - 1 - h:2 * P - 1 - h], part[:, h % 2, :],
                                            start=(h == 0 and part is sq_hi), stop=(h == HG - 1 and part is sq_lo))
                last.then_inc(p_ss, 1)

            def scores(n, j, h):
                wait(pe, v_max, n)
                cols = slice(h * SQ, (h + 1) * SQ)
                for i, (w, x) in enumerate(((q_hi, k_hi), (q_hi, k_lo), (q_lo, k_hi))):
                    last = nc.tensor.matmul(psS[0:SQ, 0:SKP], w[:, j % 2, cols], x[:, j, h, :],
                                            start=(i == 0), stop=(i == 2))
                last.then_inc(p_s, 1)

            def transposes(n, h):
                wait(pe, v_pr, n + 1)
                wait(pe, v_pT, n)
                for i in range(3):
                    last = nc.tensor.transpose(psP[0:KW[i], i * SQ:(i + 1) * SQ],
                                               pr[:, h % 2, KO[i]:KO[i] + KW[i]], ident[0:SQ, 0:SQ])
                last.then_inc(p_t, 1)

            def gather(u, b_next, j):
                wait(pe, v_pT, u * HG + HG)
                if j == 0:
                    wait(pe, v_cK, b_next)
                wait(pe, a_z, u)
                wait(pe, v_z, u)
                for c in range(CC):
                    n = 0
                    for i in range(3):
                        for w, x in ((cK_hi, pT_hi), (cK_hi, pT_lo), (cK_lo, pT_hi)):
                            last = nc.tensor.matmul(psZ[c][:, 0:UQ], w[0:KW[i], i, c * P:(c + 1) * P],
                                                    x[0:KW[i], j % 2, i, :], start=(n == 0), stop=(n == 8))
                            n += 1
                last.then_inc(p_z, 1)

            def values(u, j):
                wait(pe, a_z, u + 1)
                wait(pe, v_z, u + 1)
                wait(pe, a_o, u)
                for h in range(HG):
                    col = (j * HG + h) * D
                    for c in range(CC):
                        last = nc.tensor.matmul(psV[:, h * SQ:(h + 1) * SQ], wv_sb[:, c, col:col + D],
                                                z[:, c, h * SQ:(h + 1) * SQ], start=(c == 0), stop=(c == CC - 1))
                last.then_inc(p_v, 1)

            pe.wait_ge(v_zero, 1)
            pe.wait_ge(v_cT, 1)
            for m in range(2 * HG):
                keys(m, m // HG, m % HG)
                if m >= 1:
                    squares(m - 1, (m - 1) // HG, (m - 1) % HG)

            def body(b, first, last):
                for j in range(NG):
                    u = b * NG + j
                    n0 = u * HG
                    before = not (first and j == 0)
                    ahead = not (last and j >= 2)
                    for h in range(HG):
                        n, m = n0 + h, n0 + 2 * HG + h
                        if h == 0:
                            wait(pe, v_q, u + 1)
                            wait(pe, v_klo, n0 + HG)
                        scores(n, j, h)
                        if ahead:
                            if h == 0 and j == 2:
                                wait(pe, v_cT, b + 2)
                            keys(m, (j + 2) % NG, h)
                        if h > 0 and ahead:
                            squares(m - 1, u + 2, h - 1)
                        if h == 0 and not (last and j == NG - 1):
                            squares(m - 1, u + 1, HG - 1)
                        if h > 0:
                            transposes(n - 1, h - 1)
                        elif before:
                            transposes(n0 - 1, HG - 1)
                        if h == 1 and before:
                            gather(u - 1, b if j == 0 else b + 1, (j - 1) % NG)
                        if h == 2 and before:
                            values(u - 1, (j - 1) % NG)

            batches(pe, body)
            transposes(B * H - 1, HG - 1)
            gather(B * NG - 1, B, NG - 1)
            values(B * NG - 1, NG - 1)

        @block.scalar
        def _(act):
            def high_cT(b_next):
                wait(act, d_cT, b_next * 16)
                nc.scalar.activation(cT_hi[:, :, 0:SK], cT_in[:], ACT.Copy).then_inc(a_cT, 1)

            def high_cK(b_next):
                wait(act, d_cK, b_next * 48)
                for i in range(3):
                    nc.scalar.activation(cK_hi[0:KW[i], i, :], cK_in[0:KW[i], i, :], ACT.Copy).then_inc(a_cK, 1)

            def high_q(u, count, j):
                wait(act, d_q[j % 2], count)
                nc.scalar.activation(q_hi[:, j % 2, :], q_in[:, j % 2, :], ACT.Copy).then_inc(a_q, 1)

            def high_k(m, j, h):
                wait(act, p_k, m + 1)
                nc.scalar.activation(k_hi[:, j, h, :], psK[h % 2][:, 0:SKP], ACT.Copy)
                wait(act, g_sqlo, m - 1)
                nc.scalar.activation(sq[:, h % 2, :], psK[h % 2][:, 0:SKP], ACT.Square).then_inc(a_k, 1)

            def high_pT(n, j, h):
                wait(act, p_t, n + 1)
                nc.scalar.activation(pT_hi[0:KW[0], j % 2, :, h * SQ:(h + 1) * SQ],
                                     psP[0:KW[0], 0:3 * SQ].rearrange("p (i q) -> p i q", q=SQ),
                                     ACT.Copy).then_inc(a_pT, 1)

            def copy_z(u):
                wait(act, p_z, u + 1)
                wait(act, p_v, u)
                nc.scalar.activation(z[:, 0, :], psZ[0][:, 0:UQ], ACT.Copy).then_inc(a_z, 1)

            def copy_o(u, count, j):
                wait(act, p_v, u + 1)
                wait(act, d_o[j % 2], count)
                nc.scalar.activation(o[:, j % 2, :], psV[:, 0:UQ], ACT.Copy).then_inc(a_o, 1)

            act.wait_ge(v_zero, 1)
            high_cT(1)
            high_q(0, 16, 0)
            high_cK(1)
            for m in range(2 * HG):
                high_k(m, m // HG, m % HG)

            def body(b, first, last):
                for j in range(NG):
                    u = b * NG + j
                    n0 = u * HG
                    before = not (first and j == 0)
                    ahead = not (last and j >= 2)
                    half = b * 2 + j // 2
                    for h in range(HG):
                        n, m = n0 + h, n0 + 2 * HG + h
                        wait(act, v_nb, n + 1)
                        nc.scalar.activation(ex[:, h % 2, :], sc[:, h % 2, :], ACT.Exp, bias=nb[:, h % 2:h % 2 + 1],
                                             scale=rq[:, j % 2, h:h + 1], accum_out=rs[:, h % 2:h % 2 + 1]
                                             ).then_inc(a_ex, 1)
                        if ahead:
                            high_k(m, (j + 2) % NG, h)
                        if h > 0:
                            high_pT(n - 1, j, h - 1)
                        elif before:
                            high_pT(n0 - 1, j - 1, HG - 1)
                        if h == 2 and before:
                            copy_z(u - 1)
                        if h == 2 and not (last and j == NG - 1):
                            wait(act, p_s, n0)
                            high_q(u + 1, (b * 2 + (j + 1) // 2 + 1) * 16, j + 1)
                        if h == 3 and before:
                            copy_o(u - 1, (b * 2 + (j - 1) // 2) * 16, j - 1)
                    if j == 1 and not last:
                        wait(act, p_k, (b + 1) * H)
                        high_cT(b + 2)
                    if j == 0 and not first:
                        wait(act, p_z, u)
                        high_cK(b + 1)

            batches(act, body)
            high_pT(B * H - 1, NG - 1, HG - 1)
            copy_z(B * NG - 1)
            copy_o(B * NG - 1, (B * NG // 2 - 1) * 16, NG - 1)

        @block.vector
        def _(dve):
            nc.vector.memset(cT_hi[:, :, SK:SKP].bitcast(F32), 0.0).then_inc(v_zero, 1)
            nc.vector.memset(cT_lo[:, :, SK:SKP].bitcast(F32), 0.0).then_inc(v_zero, 1)
            nc.vector.memset(psP[:], 0.0).then_inc(v_zero, 1)

            def low_cT(b_next):
                wait(dve, a_cT, b_next)
                nc.vector.tensor_tensor(cT_lo[:, :, 0:SK], cT_in[:], cT_hi[:, :, 0:SK].bitcast(F32),
                                        ALU.subtract).then_inc(v_cT, 1)

            def low_cK(b_next):
                wait(dve, a_cK, b_next * 3)
                for i in range(3):
                    last = nc.vector.tensor_tensor(cK_lo[0:KW[i], i, :], cK_in[0:KW[i], i, :],
                                                   cK_hi[0:KW[i], i, :].bitcast(F32), ALU.subtract)
                last.then_inc(v_cK, 1)

            def low_q(b, j, u):
                wait(dve, a_q, u + 1)
                nc.vector.tensor_tensor(q_lo[:, j % 2, :], q_in[:, j % 2, :], q_hi[:, j % 2, :].bitcast(F32),
                                        ALU.subtract).then_inc(v_q, 1)
                nc.vector.tensor_copy(rq[:, j % 2, :],
                                      rq_all[:, bass.ds(b, 1), (j % NG) * HG:(j % NG + 1) * HG]
                                      .rearrange("p a h -> p (a h)")).then_inc(v_rq, 1)

            def low_k(m, j, h):
                wait(dve, a_k, m + 1)
                nc.vector.tensor_tensor(k_lo[:, j, h, :], psK[h % 2][:, 0:SKP], k_hi[:, j, h, :].bitcast(F32),
                                        ALU.subtract).then_inc(v_klo, 1)
                wait(dve, p_ss, m - 1)
                nc.vector.tensor_copy(sq_hi[:, h % 2, :], sq[:, h % 2, :]).then_inc(v_sqhi, 1)

            def mean_squares(u):
                wait(dve, p_ss, u * HG + HG)
                wait(dve, g_rk, u)
                nc.vector.tensor_scalar(ms[:], psN[0:HG, 0:SK], 1.0 / D, EPS, ALU.mult, ALU.add).then_inc(v_ms, 1)

            def low_pT(n, j, h):
                wait(dve, a_pT, n + 1)
                nc.vector.tensor_tensor(pT_lo[0:KW[0], j % 2, :, h * SQ:(h + 1) * SQ],
                                        psP[0:KW[0], 0:3 * SQ].rearrange("p (i q) -> p i q", q=SQ),
                                        pT_hi[0:KW[0], j % 2, :, h * SQ:(h + 1) * SQ].bitcast(F32),
                                        ALU.subtract).then_inc(v_pT, 1)

            low_cT(1)
            low_q(0, 0, 0)
            low_cK(1)
            for m in range(2 * HG):
                low_k(m, m // HG, m % HG)
                if m == HG:
                    mean_squares(0)

            def copy_z(u):
                wait(dve, p_z, u + 1)
                wait(dve, p_v, u)
                nc.vector.tensor_copy(z[:, 1, :], psZ[1][:, 0:UQ]).then_inc(v_z, 1)

            def body(b, first, last):
                for j in range(NG):
                    u = b * NG + j
                    n0 = u * HG
                    before = not (first and j == 0)
                    ahead = not (last and j >= 2)
                    for h in range(HG):
                        n, m = n0 + h, n0 + 2 * HG + h
                        k = slice(h % 2, h % 2 + 1)
                        if h == 0:
                            wait(dve, d_rb[j % 2], (b * 2 + j // 2 + 1) * 16)
                        wait(dve, a_ex, n - 1)
                        wait(dve, p_s, n + 1)
                        if h == 0:
                            wait(dve, v_rq, u + 1)
                        apart(dve, dve_passed)
                        nc.vector.tensor_tensor_reduce(out=sc[:, h % 2, :], in0=psS[0:SQ, 0:SK], in1=rk[:, j % 2, h, :],
                                                       scale=1.0, scalar=-3.0e38, op0=ALU.mult, op1=ALU.max,
                                                       accum_out=mx[:, k]).then_inc(v_max, 1)
                        wait(dve, v_max, n + 1)
                        nc.vector.tensor_scalar(nb[:, k], mx[:, k], rq[:, j % 2, h:h + 1], -1.0, ALU.mult,
                                                ALU.mult).then_inc(v_nb, 1)
                        if h == 0 and not (last and j == NG - 1):
                            mean_squares(u + 1)
                        wait(dve, a_ex, n + 1)
                        nc.vector.reciprocal(ri[:, k], rs[:, k]).then_inc(v_ri, 1)
                        wait(dve, p_t, n - 1)
                        wait(dve, v_ri, n + 1)
                        nc.vector.tensor_scalar(pr[:, h % 2, :], ex[:, h % 2, :], ri[:, k], None,
                                                ALU.mult).then_inc(v_pr, 1)
                        if ahead:
                            low_k(m, (j + 2) % NG, h)
                        if h > 0:
                            low_pT(n - 1, j, h - 1)
                        elif before:
                            low_pT(n0 - 1, j - 1, HG - 1)
                        if h == 2 and before:
                            copy_z(u - 1)
                        if h == 2 and not (last and j == NG - 1):
                            low_q(b + (j + 1) // NG, j + 1, u + 1)
                    if j == 1 and not last:
                        low_cT(b + 2)
                    if j == 0 and not first:
                        low_cK(b + 1)

            batches(dve, body)
            low_pT(B * H - 1, NG - 1, HG - 1)
            copy_z(B * NG - 1)


def feed_forward(nc, sbt, sem, ident, neg_half, x, wo, w_ff, had_in, o_dram, out):
    WC = 4
    NB = FF // DIM
    with ExitStack() as ctx:
        sb = lambda name, shape, dt=F32: sbt(ctx, name, shape, dt)
        s = lambda name: sem(ctx, name)
        wo_hi, wo_lo = sb("wo_hi", [P, H, DIM], F32R), sb("wo_lo", [P, H, DIM], F32R)
        wt = sb("wt", [P, 3, WC, FF], FP8)
        stage = sb("stage3", [P, 2, FF])
        below = sb("below", [P, FF], BF16)
        had = sb("had", [P, DC, DIM], F32R)
        ones = sb("ones", [P, P])
        asum, asums = sb("asum", [P, 3, WC]), sb("asums", [P, 3])
        wsc, half, nhalf, w127 = (sb(n, [P, 3]) for n in ("wsc", "half", "nhalf", "w127"))
        o_in = sb("o_in", [P, H, TT])
        o_hi, o_lo = sb("o_hi", [P, H, TT], F32R), sb("o_lo", [P, H, TT], F32R)
        x_in, x1, x1_old, xn = (sb(n, [P, DIM]) for n in ("x_in3", "x1", "x1_old", "xn3"))
        st, mv, ve, rstd = sb("st3", [P, 6]), sb("mv3", [P, 2]), sb("ve3", [P, 1]), sb("rstd3", [P, 1])
        xT_hi, xT_lo = sb("xT3_hi", [P, DC, TT], F32R), sb("xT3_lo", [P, DC, TT], F32R)
        mx, am, rc, sq = (sb(n, [P, 2]) for n in ("mx3", "am3", "rc3", "sq3"))
        al, ald = sb("al", [P, 2]), sb("ald", [P, 1])
        mag1, mag2 = sb("mag1", [P, DIM]), sb("mag2", [P, FF])
        q1, q1T = sb("q1", [P, DIM], BF16), sb("q1T", [P, DC, TT], BF16)
        q2, q2T = sb("q2", [P, FF], BF16), sb("q2T", [P, FC, TT], BF16)
        sil = sb("sil", [P, 2, DIM])
        hid = stage[:, 0, :].rearrange("p (n j) -> p n j", j=DIM)
        half_rot = stage[:, 1, :].rearrange("p (n j) -> p n j", j=DIM)
        hT_hi, hT_lo = sb("hT_hi", [P, FC, TT], F32R), sb("hT_lo", [P, FC, TT], F32R)
        y = sb("y", [P, DIM])
        ident_b = sb("ident_b", [P, P], BF16)
        psB = ctx.enter_context(nc.psum_tensor("psB", [P, NB, DIM], F32))
        psA = ctx.enter_context(nc.psum_tensor("psA", [P, DIM], F32))
        psF = ctx.enter_context(nc.psum_tensor("psF", [P, DIM], F32))
        psT = [ctx.enter_context(nc.psum_tensor(f"psT{i}", [P, DIM], F32)) for i in range(2)]
        psTb = [t[:].bitcast(BF16) for t in psT]

        d_st = [s("d3_st0"), s("d3_st1")]
        d_o, d_x, d_out, d_had = s("d3_o"), s("d3_x"), s("d3_out"), s("d3_had")
        a_w, v_w, v_sum, v_sums, p_sum, v_mean, v_thr = (s(n) for n in ("a3_w", "v3_w", "v3_sum", "v3_sums", "p3_sum",
                                                                         "v3_mean", "v3_thr"))
        v_below, v_wt, v_had, g_ones = s("v3_below"), s("v3_wt"), s("v3_had"), s("g3_ones")
        a_o, v_o = s("a3_o"), s("v3_o")
        p1, p2, p3, p4, p5, p6, p7, p8, p9 = (s(f"p3_{i}") for i in range(1, 10))
        v_x1, v_st, v_ag, v_ve, g_rs, v_xn = (s(n) for n in ("v3_x1", "v3_st", "v3_ag", "v3_ve", "g3_rs", "v3_xn"))
        a_xT, v_xT = s("a3_xT"), s("v3_xT")
        v_mx, v_am, v_rc, v_sq, v_al = ([s(f"v3_{n}{i}") for i in range(2)] for n in ("mx", "am", "rc", "sq", "al"))
        a_mag, v_q = ([s(f"{n}{i}") for i in range(2)] for n in ("a3_mag", "v3_q"))
        a_q1T, a_q2T, a_sil, v_h, v_r1, v_r2 = (s(n) for n in ("a3_q1T", "a3_q2T", "a3_sil", "v3_h", "v3_r1", "v3_r2"))
        a_hT, v_hT, v_y, v_old = s("a3_hT"), s("v3_hT"), s("v3_y"), s("v3_old")

        wo_v = wo.rearrange("(j h d) n -> j d h n", d=D, h=HG)
        jobs = [("wo", j) for j in range(NG)] + [("had", 0)]
        jobs += [("sum", w, c) for w in range(3) for c in range(WC)]
        jobs += [("round", w, c) for w in range(3) for c in range(WC)]
        FREED = len(jobs)

        pe_passed, dve_passed = s("pe_passed3"), s("dve_passed3")
        block = ctx.enter_context(nc.Block())

        def tiles(eng, body):
            body(0, True, False)
            with eng.Fori(1, TILES - 1) as t:
                body(t, False, False)
            body(TILES - 1, False, True)

        @block.sync
        def _(sp):
            def load_o(t, tok):
                src = o_dram[:, :, bass.ds(tok, TT)].rearrange("h d t -> d h t")
                wait(sp, v_o, t)
                sp.dma_start(o_in[:], src).then_inc(d_o, 16)

            def load_x(t, tok):
                src = x[bass.ds(tok, TT), :]
                wait(sp, v_x1, t)
                sp.dma_start(x_in[:], src).then_inc(d_x, 16)

            def store(tok, count):
                dst = out[bass.ds(tok, TT), :]
                wait(sp, v_y, count)
                sp.dma_start(dst, y[:]).then_inc(d_out, 16)

            def front_loads(t, tok):
                load_o(t, tok)
                load_x(t, tok)

            for i, job in enumerate(jobs):
                if i >= 2:
                    sp.wait_ge(v_w, i - 1)
                if job[0] == "wo":
                    src, dst = wo_v[job[1]], stage[:, i % 2, :].rearrange("p (h n) -> p h n", h=HG)
                elif job[0] == "had":
                    src, dst = had_in.rearrange("(c p) n -> p c n", p=P), stage[:, i % 2, :].rearrange("p (c n) -> p c n", c=DC)
                else:
                    src, dst = w_ff[job[1], job[2]], stage[:, i % 2, :]
                sp.dma_start(dst, src).then_inc(d_st[i % 2], 16)
                if i == 1:
                    load_o(0, 0)
                    load_x(0, 0)
            front_loads(1, TT)
            with sp.Fori(1, TILES - 2) as t:
                front_loads(sp.snap(t + 1), sp.snap(t * TT + TT))
                store(sp.snap(t * TT - TT), sp.snap(t))
            front_loads(TILES - 1, LAST_TOK)
            store((TILES - 3) * TT, TILES - 2)
            store((TILES - 2) * TT, TILES - 1)
            store(LAST_TOK, TILES)
            sp.wait_ge(d_out, 16 * TILES)

        @block.gpsimd
        def _(pool):
            nc.gpsimd.memset(ones[:], 1.0).then_inc(g_ones, 1)

            def body(t, first, last):
                wait(pool, v_ve, t + 1)
                nc.gpsimd.tensor_tensor(rstd[:], ve[:], neg_half[:], op=ALU.pow).then_inc(g_rs, 1)

            tiles(pool, body)

        @block.tensor
        def _(pe):
            pe.wait_ge(g_ones, 1)
            pe.wait_ge(v_sums, 1)
            nc.tensor.matmul(psF[:, 0:3], ones[:], asums[:], start=True, stop=True).then_inc(p_sum, 1)

            def out_proj(t):
                wait(pe, v_o, t + 1)
                wait(pe, v_y, t - 1)
                n = 0
                for h in range(H):
                    for w, m in ((o_hi, wo_hi), (o_hi, wo_lo), (o_lo, wo_hi)):
                        last = nc.tensor.matmul(psA[:], w[:, h, :], m[:, h, :], start=(n == 0), stop=(n == 3 * H - 1))
                        n += 1
                last.then_inc(p1, 1)

            def norm_T(t):
                wait(pe, v_xn, t + 1)
                wait(pe, v_hT, t * NB)
                for c in range(DC):
                    last = nc.tensor.transpose(psT[0][:, c * P:(c + 1) * P], xn[:, c * P:(c + 1) * P], ident[:])
                last.then_inc(p2, 1)

            def rotate_in(t):
                wait(pe, v_xT, t + 1)
                wait(pe, a_mag[0], t)
                for c in range(DC):
                    for m in (xT_hi, xT_lo):
                        last = nc.tensor.matmul(psF[:], m[:, c, :], had[:, c, :], start=(c == 0 and m is xT_hi),
                                                stop=(c == DC - 1 and m is xT_lo))
                last.then_inc(p3, 1)

            def q1_T(t):
                wait(pe, v_q[0], t + 1)
                wait(pe, a_q2T, 2 * t)
                wait(pe, v_hT, t * NB)
                for c in range(DC):
                    last = nc.tensor.transpose(psTb[1][:, c * P:(c + 1) * P], q1[:, c * P:(c + 1) * P], ident_b[:])
                last.then_inc(p4, 1)

            def gate_up(t, first):
                wait(pe, a_q1T, t + 1)
                if first:
                    pe.wait_ge(v_wt, 2 * WC)
                wait(pe, a_mag[1], t)
                for j in range(NB):
                    wait(pe, v_h, t * NB + j - 1)
                    apart(pe, pe_passed)
                    for k in range(2):
                        for c in range(DC):
                            last = nc.tensor.matmul(psB[:, 2 * (j % 2) + k, :], q1T[:, c, :],
                                                    wt[:, k, c, j * DIM:(j + 1) * DIM], start=(c == 0), stop=(c == DC - 1))
                    last.then_inc(p5, 1)

            def hidden_T(t):
                wait(pe, v_r2, 2 * t + 2)
                for n in range(NB):
                    if n == 0:
                        wait(pe, a_q2T, 2 * t)
                        wait(pe, a_q1T, t + 1)
                    else:
                        wait(pe, v_hT, t * NB + n - 1)
                    for c in range(DC):
                        last = nc.tensor.transpose(psT[n % 2][:, c * P:(c + 1) * P], hid[:, n, c * P:(c + 1) * P], ident[:])
                    last.then_inc(p6, 1)

            def rotate_hidden(t, blocks):
                for n in blocks:
                    wait(pe, v_hT, t * NB + n + 1)
                    if n == 0:
                        wait(pe, v_h, t * NB + NB)
                    for c in range(DC):
                        for m in (hT_hi, hT_lo):
                            last = nc.tensor.matmul(psB[:, n, :], m[:, n * DC + c, :], had[:, c, :],
                                                    start=(c == 0 and m is hT_hi), stop=(c == DC - 1 and m is hT_lo))
                    last.then_inc(p7, 1)

            def q2_T(t, front):
                wait(pe, v_q[1], t + 1)
                if front:
                    wait(pe, v_xT, t + 2)
                wait(pe, v_hT, t * NB + NB)
                for k in range(2):
                    for c in range(FC // 2):
                        i = k * FC // 2 + c
                        last = nc.tensor.transpose(psTb[k][:, c * P:(c + 1) * P], q2[:, i * P:(i + 1) * P], ident_b[:])
                    last.then_inc(p8, 1)

            def down(t, part, front):
                if part == 0 and front:
                    wait(pe, v_x1, t + 2)
                wait(pe, a_q2T, 2 * t + part + 1)
                apart(pe, pe_passed)
                for i in range(part * FC // 2, (part + 1) * FC // 2):
                    last = nc.tensor.matmul(psA[:], q2T[:, i, :], wt[:, 2, i // WC, (i % WC) * DIM:(i % WC + 1) * DIM],
                                            start=(i == 0), stop=(i == FC - 1))
                if part == 1:
                    last.then_inc(p9, 1)

            pe.wait_ge(v_had, 2)

            def body(t, first, last):
                if first:
                    pe.wait_ge(v_w, NG)
                out_proj(t)
                if not first:
                    hidden_T(t - 1)
                    rotate_hidden(t - 1, range(0, NB // 2))
                norm_T(t)
                if not first:
                    rotate_hidden(t - 1, range(NB // 2, NB))
                rotate_in(t)
                if not first:
                    q2_T(t - 1, True)
                    down(t - 1, 0, True)
                q1_T(t)
                if not first:
                    down(t - 1, 1, True)
                gate_up(t, first)

            body(0, True, False)
            pe.wait_ge(v_wt, 3 * WC)
            with pe.Fori(1, TILES - 1) as t:
                body(t, False, False)
            body(TILES - 1, False, True)
            hidden_T(TILES - 1)
            rotate_hidden(TILES - 1, range(NB))
            q2_T(TILES - 1, False)
            down(TILES - 1, 0, False)
            down(TILES - 1, 1, False)

        @block.scalar
        def _(act):
            def high_o(t):
                wait(act, d_o, t * 16 + 16)
                wait(act, p1, t)
                nc.scalar.activation(o_hi[:], o_in[:], ACT.Copy).then_inc(a_o, 1)

            for i in range(NG):
                act.wait_ge(d_st[i % 2], 16 * (i // 2 + 1))
                nc.scalar.activation(wo_hi[:, i * HG:(i + 1) * HG, :].rearrange("p h n -> p (h n)"), stage[:, i % 2, :],
                                     ACT.Copy).then_inc(a_w, 1)
                if i == 1:
                    high_o(0)

            def high_hT(t):
                for n in range(NB):
                    wait(act, p6, t * NB + n + 1)
                    if n == 0:
                        wait(act, p7, t * NB)
                    nc.scalar.activation(hT_hi[:, n * DC:(n + 1) * DC, :].rearrange("p c t -> p (c t)"),
                                         psT[n % 2][:], ACT.Copy).then_inc(a_hT, 1)

            def high_xT(t):
                wait(act, p2, t + 1)
                nc.scalar.activation(xT_hi[:].rearrange("p c t -> p (c t)"), psT[0][:], ACT.Copy).then_inc(a_xT, 1)

            def round1(t):
                wait(act, v_sq[0], t + 1)
                wait(act, v_q[0], t)
                nc.scalar.activation(mag1[:], psF[:], ACT.Copy, bias=MAGIC, scale=sq[:, 0:1]).then_inc(a_mag[0], 1)

            def round2(t):
                wait(act, v_sq[1], t + 1)
                wait(act, v_q[1], t)
                nc.scalar.activation(mag2[:], psB[:].rearrange("p n j -> p (n j)"), ACT.Copy, bias=MAGIC,
                                     scale=sq[:, 1:2]).then_inc(a_mag[1], 1)

            def copy_q2T(t):
                for k in range(2):
                    wait(act, p8, 2 * t + k + 1)
                    if k == 0:
                        wait(act, p9, t)
                    nc.scalar.activation(q2T[:, k * FC // 2:(k + 1) * FC // 2, :].rearrange("p c t -> p (c t)"),
                                         psTb[k][:, 0:FC // 2 * TT], ACT.Copy).then_inc(a_q2T, 1)

            def copy_q1T(t):
                wait(act, p4, t + 1)
                wait(act, p5, t * NB)
                nc.scalar.activation(q1T[:].rearrange("p c t -> p (c t)"), psTb[1][:, 0:DIM], ACT.Copy).then_inc(a_q1T, 1)

            def silus(t):
                wait(act, v_al[0], t + 1)
                for j in range(NB):
                    wait(act, p5, t * NB + j + 1)
                    wait(act, v_h, t * NB + j - 1)
                    nc.scalar.activation(sil[:, j % 2, :], psB[:, 2 * (j % 2), :], ACT.Silu, scale=al[:, 0:1]
                                         ).then_inc(a_sil, 1)

            def body(t, first, last):
                if not first:
                    high_hT(t - 1)
                high_xT(t)
                if not first:
                    round2(t - 1)
                round1(t)
                if not last:
                    high_o(t + 1)
                if not first:
                    copy_q2T(t - 1)
                copy_q1T(t)
                silus(t)

            tiles(act, body)
            high_hT(TILES - 1)
            round2(TILES - 1)
            copy_q2T(TILES - 1)

        @block.vector
        def _(dve):
            def low_o(t):
                wait(dve, a_o, t + 1)
                nc.vector.tensor_tensor(o_lo[:], o_in[:], o_hi[:].bitcast(F32), ALU.subtract).then_inc(v_o, 1)

            nc.vector.tensor_copy(ident_b[:], ident[:]).then_inc(v_had, 1)
            for i, job in enumerate(jobs):
                piece = stage[:, i % 2, :]
                arrived = 16 * (i // 2 + 1)
                if job[0] == "wo":
                    j = job[1]
                    dve.wait_ge(a_w, j + 1)
                    part = wo_hi[:, j * HG:(j + 1) * HG, :].rearrange("p h n -> p (h n)").bitcast(F32)
                    nc.vector.tensor_tensor(wo_lo[:, j * HG:(j + 1) * HG, :].rearrange("p h n -> p (h n)"), piece, part,
                                            ALU.subtract).then_inc(v_w, 1)
                    if j == 1:
                        low_o(0)
                elif job[0] == "had":
                    dve.wait_ge(d_st[i % 2], arrived)
                    nc.vector.tensor_copy(had[:].rearrange("p c n -> p (c n)"), piece).then_inc(v_w, 1)
                    dve.wait_ge(v_w, i + 1)
                    nc.vector.memset(mx[:], 0.0).then_inc(v_had, 1)
                elif job[0] == "sum":
                    _, w, c = job
                    dve.wait_ge(d_st[i % 2], arrived)
                    nc.vector.tensor_reduce(asum[:, w, c:c + 1], piece, axis=AX.X, op=ALU.add,
                                            apply_absolute_value=True).then_inc(v_w, 1)
                    if (w, c) == (2, WC - 1):
                        dve.wait_ge(v_w, i + 1)
                        nc.vector.tensor_reduce(asums[:], asum[:], axis=AX.X, op=ALU.add).then_inc(v_sums, 1)
                        dve.wait_ge(p_sum, 1)
                        nc.vector.tensor_scalar(wsc[:], psF[:, 0:3], 1.0 / (DIM * FF), EPS, ALU.mult, ALU.max).then_inc(v_mean, 1)
                        dve.wait_ge(v_mean, 1)
                        nc.vector.tensor_scalar(half[:], wsc[:], 0.5, None, ALU.mult).then_inc(v_thr, 1)
                        nc.vector.tensor_scalar(nhalf[:], wsc[:], -0.5, None, ALU.mult).then_inc(v_thr, 1)
                        nc.vector.tensor_scalar(w127[:], wsc[:], 1.0 / 127.0, None, ALU.mult).then_inc(v_thr, 1)
                        dve.wait_ge(v_thr, 3)
                else:
                    _, w, c = job
                    k = w * WC + c
                    dve.wait_ge(d_st[i % 2], arrived)
                    nc.vector.tensor_scalar(below[:], piece, nhalf[:, w:w + 1], None, ALU.is_lt).then_inc(v_below, 1)
                    dve.wait_ge(v_below, k + 1)
                    nc.vector.scalar_tensor_tensor(wt[:, w, c, :], piece, half[:, w:w + 1], below[:], ALU.is_gt,
                                                   ALU.subtract, saturate=False).then_inc(v_wt, 1)
                    dve.wait_ge(v_wt, k + 1)
                    nc.vector.memset(mx[:], 0.0).then_inc(v_w, 1)

            def rotate4(t):
                wait(dve, v_h, t * NB + NB)
                pairs = hid.rearrange("p (a b) j -> p a b j", b=2)
                halves = half_rot.rearrange("p (a b) j -> p a b j", b=2)
                for b, op in enumerate((ALU.add, ALU.subtract)):
                    nc.vector.tensor_tensor(halves[:, :, b, :], pairs[:, :, 0, :], pairs[:, :, 1, :], op).then_inc(v_r1, 1)
                wait(dve, v_r1, 2 * t + 2)
                for a, op in enumerate((ALU.add, ALU.subtract)):
                    nc.vector.tensor_tensor(pairs[:, a, :, :], halves[:, 0, :, :], halves[:, 1, :, :], op).then_inc(v_r2, 1)

            def keep(t):
                wait(dve, v_y, t)
                nc.vector.tensor_copy(x1_old[:], x1[:]).then_inc(v_old, 1)

            def low_hT(t, n):
                wait(dve, a_hT, t * NB + n + 1)
                nc.vector.tensor_tensor(hT_lo[:, n * DC:(n + 1) * DC, :].rearrange("p c t -> p (c t)"), psT[n % 2][:],
                                        hT_hi[:, n * DC:(n + 1) * DC, :].rearrange("p c t -> p (c t)").bitcast(F32),
                                        ALU.subtract).then_inc(v_hT, 1)

            def residual(t):
                wait(dve, p1, t + 1)
                wait(dve, d_x, t * 16 + 16)
                wait(dve, v_old, t)
                nc.vector.tensor_tensor(x1[:], psA[:], x_in[:], ALU.add).then_inc(v_x1, 1)
                wait(dve, v_x1, t + 1)
                nc.vector.bn_stats(st[:], x1[:]).then_inc(v_st, 1)
                wait(dve, v_st, t + 1)
                apart(dve, dve_passed)
                nc.vector.bn_aggr(mv[:], st[:]).then_inc(v_ag, 1)
                wait(dve, v_ag, t + 1)
                nc.vector.tensor_scalar(ve[:], mv[:, 1:2], EPS, None, ALU.add).then_inc(v_ve, 1)

            def norm(t):
                wait(dve, g_rs, t + 1)
                wait(dve, p2, t)
                nc.vector.tensor_scalar(xn[:], x1[:], mv[:, 0:1], rstd[:], ALU.subtract, ALU.mult).then_inc(v_xn, 1)

            def low_xT(t):
                wait(dve, a_xT, t + 1)
                nc.vector.tensor_tensor(xT_lo[:].rearrange("p c t -> p (c t)"), psT[0][:],
                                        xT_hi[:].rearrange("p c t -> p (c t)").bitcast(F32), ALU.subtract).then_inc(v_xT, 1)

            def scales(i, t, ps, n, factor, weight):
                c = slice(i, i + 1)
                norm_n = float(n) ** -0.5
                nc.vector.tensor_reduce(mx[:, c], ps, axis=AX.X, op=ALU.max, apply_absolute_value=True).then_inc(v_mx[i], 1)
                wait(dve, v_mx[i], t + 1)
                nc.vector.tensor_scalar(am[:, c], mx[:, c], norm_n, EPS, ALU.mult, ALU.max).then_inc(v_am[i], 1)
                wait(dve, v_am[i], t + 1)
                nc.vector.reciprocal(rc[:, c], am[:, c]).then_inc(v_rc[i], 1)
                wait(dve, v_rc[i], t + 1)
                nc.vector.tensor_scalar(sq[:, c], rc[:, c], 127.0 * norm_n, None, ALU.mult).then_inc(v_sq[i], 1)
                nc.vector.tensor_scalar(factor, weight, am[:, c], None, ALU.mult).then_inc(v_al[i], 1)

            def to_int(i, t, q, mag):
                wait(dve, a_mag[i], t + 1)
                nc.vector.tensor_scalar(q, mag, MAGIC, 127.0, ALU.subtract, ALU.min).then_inc(v_q[i], 1)

            def hidden(t):
                for j in range(NB):
                    wait(dve, a_sil, t * NB + j + 1)
                    nc.vector.scalar_tensor_tensor(hid[:, j, :], psB[:, 2 * (j % 2) + 1, :], al[:, 1:2], sil[:, j % 2, :],
                                                   ALU.mult, ALU.mult).then_inc(v_h, 1)

            def result(t):
                wait(dve, p9, t + 1)
                wait(dve, d_out, t * 16)
                wait(dve, v_al[1], t + 1)
                nc.vector.scalar_tensor_tensor(y[:], psA[:], ald[:], x1_old[:], ALU.mult, ALU.add).then_inc(v_y, 1)

            def back_scales(t):
                wait(dve, p7, t * NB + NB)
                wait(dve, p8, 2 * t)
                scales(1, t, psB[:].rearrange("p n j -> p (n j)"), FF, ald[:], w127[:, 2:3])

            def body(t, first, last):
                if not first:
                    rotate4(t - 1)
                    keep(t - 1)
                    low_hT(t - 1, 0)
                    low_hT(t - 1, 1)
                residual(t)
                if not first:
                    low_hT(t - 1, 2)
                    low_hT(t - 1, 3)
                norm(t)
                low_xT(t)
                if not first:
                    back_scales(t - 1)
                wait(dve, p3, t + 1)
                wait(dve, p4, t)
                scales(0, t, psF[:], DIM, al[:], w127[:, 0:2])
                if not first:
                    to_int(1, t - 1, q2[:], mag2[:])
                to_int(0, t, q1[:], mag1[:])
                if not last:
                    low_o(t + 1)
                if not first:
                    result(t - 1)
                hidden(t)

            tiles(dve, body)
            t = TILES - 1
            rotate4(t)
            keep(t)
            for n in range(NB):
                low_hT(t, n)
            back_scales(t)
            to_int(1, t, q2[:], mag2[:])
            result(t)


def kernel(x, ctx_1024, L0_xattn_Wq, L0_xattn_Wk, L0_xattn_Wv, L0_xattn_Wo, L0_xattn_gq, L0_xattn_gk,
           L0_ffn_w_gate, L0_ffn_w_up, L0_ffn_w_down):
    import numpy as np
    import concourse.bacc as bacc
    from concourse.bass_utils import run_bass_kernel_spmd

    x2 = np.asarray(x).reshape(T, DIM)
    ctx = np.asarray(ctx_1024)
    rows = lambda w: np.asarray(w).T.reshape(4, P, FF)
    down = np.asarray(L0_ffn_w_down).T.reshape(4, 4, P, DIM).transpose(0, 2, 1, 3).reshape(4, P, FF)
    had = np.ones((1, 1), np.float32)
    while had.shape[0] < DIM:
        had = np.block([[had, had], [had, -had]])
    arrays = {
        "x": x2, "ctxT": ctx.transpose(0, 2, 1), "ctx_k": ctx, "wq": L0_xattn_Wq, "wk": L0_xattn_Wk, "wv": L0_xattn_Wv,
        "wo": L0_xattn_Wo, "gq": L0_xattn_gq, "gk": L0_xattn_gk,
        "w_ff": np.stack([rows(L0_ffn_w_gate), rows(L0_ffn_w_up), down]),
        "ident": np.eye(P, dtype=np.float32), "had": had,
    }
    arrays = {"in_" + k: np.ascontiguousarray(v) for k, v in arrays.items()}
    nc = bacc.Bacc("TRN2", target_bir_lowering=False, num_devices=1)
    args = [nc.dram_tensor(k, a.shape, F32, kind="ExternalInput").ap() for k, a in arrays.items()]
    out = nc.dram_tensor("out", [T, DIM], F32, kind="ExternalOutput").ap()
    build(nc, *args, out)
    r = run_bass_kernel_spmd(nc, [arrays], core_ids=[0])
    return r.results[0]["out"].reshape(B, SQ, DIM)
```

```python
import concourse.bass as bass
from concourse import mybir
from contextlib import ExitStack

F32 = mybir.dt.float32
F32R = mybir.dt.float32r
BF16 = mybir.dt.bfloat16
FP8 = mybir.dt.float8e4
ALU = mybir.AluOpType
ACT = mybir.ActivationFunctionType
AX = mybir.AxisListType

P = 128
B, SQ, DIM = 16, 100, 512
SK, CD = 361, 256
H, D = 16, 128
INNER = H * D
FF = 2048
T = B * SQ
EPS = 1e-5
SKR = 19
SKP = SK + 1
DC, CC, FC = DIM // P, CD // P, FF // P
HG = 4
NG = H // HG
KW = [121, 120, 120]
KO = [0, 121, 241]
GB = 4
GT = GB * SQ
G = B // GB
LAST_B = B - 1
MAGIC = 1.5 * 2.0 ** 23
TT = P
TILES = -(-T // TT)
LAST_TOK = T - TT


def build(nc, x, ctxT, ctx_k, wq, wk, wv, wo, gq, gk, w_ff, ident_in, had_in, out):
    q_dram = nc.dram_tensor("q_dram", [B, D, H, SQ], F32, kind="Internal").ap()
    rk_dram = nc.dram_tensor("rk_dram", [2, HG * SK], F32, kind="Internal").ap()
    o_dram = nc.dram_tensor("o_dram", [H, D, T], F32, kind="Internal").ap()
    with ExitStack() as top:
        def sbt(ctx, name, shape, dt=F32):
            return ctx.enter_context(nc.sbuf_tensor(name, shape, dt))

        def sem(ctx, name):
            return ctx.enter_context(nc.semaphore(name))

        ident = sbt(top, "ident", [P, P])
        rq_all = sbt(top, "rq_all", [SQ, B, H])
        neg_half = sbt(top, "neg_half", [P, 1])
        with ExitStack() as ctx:
            weights = {
                "wk_hi": sbt(ctx, "wk_hi", [P, CC, INNER], F32R),
                "wk_lo": sbt(ctx, "wk_lo", [P, CC, INNER], F32R),
                "wv": sbt(ctx, "wv_sb", [P, CC, INNER]),
                "sel": sbt(ctx, "sel", [P, 2 * P - 1], F32R),
            }
            queries(nc, sbt, sem, weights, ident, rq_all, neg_half, x, wq, wk, wv, gq, gk, ident_in, q_dram)
            attention(nc, sbt, sem, weights, ident, rq_all, neg_half, ctxT, ctx_k, q_dram, rk_dram, o_dram)
        feed_forward(nc, sbt, sem, ident, neg_half, x, wo, w_ff, had_in, o_dram, out)


def wait(eng, sem, count):
    if not (isinstance(count, int) and count <= 0):
        eng.wait_ge(sem, count)


def held(eng, value):
    return value if isinstance(value, int) else eng.snap(value)


def apart(eng, passed):
    eng.sem_inc(passed, 1)


def query_factors(nc, rq_all, neg_half, g):
    rows = rq_all[:, bass.ds(g * GB, GB), :]
    return nc.gpsimd.tensor_tensor(rows, rows, neg_half[0:SQ, :].unsqueeze(2).to_broadcast([SQ, GB, H]), op=ALU.pow)


def queries(nc, sbt, sem, weights, ident, rq_all, neg_half, x, wq, wk, wv, gq, gk, ident_in, q_dram):
    wk_hi, wk_lo, wv_sb, sel = (weights[k] for k in ("wk_hi", "wk_lo", "wv", "sel"))
    QW = HG * D
    KWD = INNER // 2
    with ExitStack() as ctx:
        sb = lambda name, shape, dt=F32: sbt(ctx, name, shape, dt)
        s = lambda name: sem(ctx, name)
        wq_hi, wq_lo = sb("wq_hi", [P, DC, INNER], F32R), sb("wq_lo", [P, DC, INNER], F32R)
        stage = sb("stage", [P, 2, DC * QW])
        x_in = sb("x_in", [SQ, GB, DIM])
        xn = sb("xn", [SQ, GB, DIM])
        st, mv = sb("st", [SQ, GB, 6]), sb("mv", [SQ, GB, 2])
        ve, rstd = sb("ve", [SQ, GB]), sb("rstd", [SQ, GB])
        xT_hi, xT_lo = sb("xT_hi", [P, DC, GT], F32R), sb("xT_lo", [P, DC, GT], F32R)
        gqk, gk_sb = sb("gqk", [P, 1]), sb("gk_sb", [P, 1])
        gprod = sb("gprod", [P, 1])
        q_out = sb("q_out", [P, 2, GT])
        sq = sb("sq1", [P, 2, GT])
        sq_hi, sq_lo = sb("sq1_hi", [P, 2, GT], F32R), sb("sq1_lo", [P, 2, GT], F32R)
        ms = sb("ms1", [H, GT])
        psQ = [ctx.enter_context(nc.psum_tensor(f"psQ{i}", [P, 512], F32)) for i in range(2)]
        psX = [ctx.enter_context(nc.psum_tensor(f"psX{i}", [P, DC, SQ], F32)) for i in range(GB)]
        psS = ctx.enter_context(nc.psum_tensor("psS1", [P, 512], F32))
        psR = ctx.enter_context(nc.psum_tensor("psR", [P, GB, H], F32))

        d_x, d_g, d_id, d_wv = s("d1_x"), s("d1_g"), s("d1_id"), s("d1_wv")
        d_st = [s("d1_st0"), s("d1_st1")]
        d_q = [s("d1_q0"), s("d1_q1")]
        g_const, g_rstd, g_rq = s("g1_const"), s("g1_rstd"), s("g1_rq")
        v_gain, v_stat, v_agg, v_ve, v_xn = s("v1_gain"), s("v1_stat"), s("v1_agg"), s("v1_ve"), s("v1_xn")
        a_whi, v_wlo = s("a1_whi"), s("v1_wlo")
        p_xT, a_xhi, v_xlo = s("p1_xT"), s("a1_xhi"), s("v1_xlo")
        p_q, a_q, v_sqhi, v_sqlo = s("p1_q"), s("a1_q"), s("v1_sqhi"), s("v1_sqlo")
        p_ss, v_ms, p_rq, v_rq = s("p1_ss"), s("v1_ms"), s("p1_rq"), s("v1_rq")

        pieces = []
        for j in range(4):
            cols = slice(j * QW, (j + 1) * QW)
            pieces.append((wq.rearrange("(c p) n -> p c n", p=P)[:, :, cols], wq_hi[:, :, cols], wq_lo[:, :, cols]))
        for j in range(2):
            cols = slice(j * KWD, (j + 1) * KWD)
            pieces.append((wk.rearrange("(c p) n -> p c n", p=P)[:, :, cols], wk_hi[:, :, cols], wk_lo[:, :, cols]))

        def staged(i):
            c = pieces[i][1].shape[1]
            return stage[:, i % 2, :].rearrange("p (c n) -> p c n", c=c)

        SPLIT_AT = {0: 1, 2: 2, 4: 3, 8: 4, 10: 5}

        pe_passed, dve_passed = s("pe_passed1"), s("dve_passed1")
        block = ctx.enter_context(nc.Block())

        @block.sync
        def _(sp):
            xg = x.rearrange("(b q) n -> q b n", q=SQ)
            sp.dma_start(x_in[:], xg[:, 0:GB, :]).then_inc(d_x, 16)
            sp.dma_start(ident[:], ident_in).then_inc(d_id, 16)
            sp.dma_start(gqk[:], gq.rearrange("(p a) -> p a", a=1)).then_inc(d_g, 16)
            sp.dma_start(gk_sb[:], gk.rearrange("(p a) -> p a", a=1)).then_inc(d_g, 16)

            def load_piece(i):
                wait(sp, v_wlo, i - 1)
                sp.dma_start(staged(i), pieces[i][0]).then_inc(d_st[i % 2], 16)

            for i in range(4):
                load_piece(i)
            sp.dma_start(wv_sb[:], wv.rearrange("(c p) n -> p c n", p=P)).then_inc(d_wv, 16)

            def group(g, last):
                if not last:
                    nxt = held(sp, (g + 1) * GB)
                    src = xg[:, bass.ds(nxt, GB), :]
                    wait(sp, v_xn, nxt)
                    sp.dma_start(x_in[:], src).then_inc(d_x, 16)
                for h in range(H):
                    dst = q_dram[bass.ds(held(sp, g * GB), GB), :, h, :].rearrange("b d q -> d b q")
                    wait(sp, a_q, held(sp, g * H + h + 1))
                    sp.dma_start(dst, q_out[:, h % 2, :].rearrange("p (b q) -> p b q", q=SQ)).then_inc(d_q[h % 2], 16)
                    if isinstance(g, int) and g == 0 and h in (1, 3):
                        load_piece(4 + h // 2)

            group(0, False)
            with sp.Fori(1, G - 1) as g:
                group(g, False)
            group(G - 1, True)
            for i in range(2):
                sp.wait_ge(d_q[i], 16 * G * H // 2)
            sp.wait_ge(d_wv, 16)

        @block.gpsimd
        def _(pool):
            nc.gpsimd.memset(neg_half[:], -0.5).then_inc(g_const, 1)
            nc.gpsimd.memset(sel[:].bitcast(F32), 0.0).then_inc(g_const, 1)
            pool.wait_ge(g_const, 2)
            nc.gpsimd.memset(sel[:, P - 1:P].bitcast(F32), 1.0).then_inc(g_const, 1)

            def norm(g):
                wait(pool, v_ve, g + 1)
                nc.gpsimd.tensor_tensor(rstd[:], ve[:], neg_half[0:SQ, :].to_broadcast([SQ, GB]),
                                        op=ALU.pow).then_inc(g_rstd, 1)

            def rms(g):
                wait(pool, v_rq, g + 1)
                query_factors(nc, rq_all, neg_half, g).then_inc(g_rq, 1)

            norm(0)
            norm(1)
            with pool.Fori(0, G - 2) as g:
                norm(g + 2)
                rms(g)
            rms(G - 2)

        @block.tensor
        def _(pe):
            pe.wait_ge(d_id, 16)
            pe.wait_ge(g_const, 3)

            def transposes(g):
                for b in range(GB):
                    wait(pe, v_xn, g * GB + b + 1)
                    wait(pe, v_xlo, (g - 1) * GB + b + 1)
                    for c in range(DC):
                        last = nc.tensor.transpose(psX[b][:, c, :], xn[:, b, c * P:(c + 1) * P], ident[0:SQ, 0:SQ])
                    last.then_inc(p_xT, 1)

            def squares(g, h):
                wait(pe, v_sqlo, g * H + h + 1)
                if h == 0:
                    wait(pe, v_ms, g)
                for part in (sq_hi, sq_lo):
                    last = nc.tensor.matmul(psS[:, 0:GT], sel[:, P - 1 - h:2 * P - 1 - h], part[:, h % 2, :],
                                            start=(h == 0 and part is sq_hi), stop=(h == H - 1 and part is sq_lo))
                last.then_inc(p_ss, 1)

            def factors(g):
                wait(pe, v_ms, g + 1)
                wait(pe, v_rq, g)
                apart(pe, pe_passed)
                for b in range(GB):
                    last = nc.tensor.transpose(psR[0:SQ, b, :], ms[:, b * SQ:(b + 1) * SQ], ident[0:H, 0:H])
                last.then_inc(p_rq, 1)

            def group(g, first, last_group):
                for h in range(H):
                    if first and h % HG == 0:
                        pe.wait_ge(v_wlo, h // HG + 1)
                    if h == 0:
                        wait(pe, v_xlo, (g + 1) * GB)
                    wait(pe, a_q, g * H + h - 1)
                    n = 0
                    for c in range(DC):
                        for w, m in ((wq_hi, xT_hi), (wq_hi, xT_lo), (wq_lo, xT_hi)):
                            last = nc.tensor.matmul(psQ[h % 2][:, 0:GT], w[:, c, h * D:(h + 1) * D], m[:, c, :],
                                                    start=(n == 0), stop=(n == 3 * DC - 1))
                            n += 1
                    last.then_inc(p_q, 1)
                    if h >= 1:
                        squares(g, h - 1)
                    if h == 3 and not first:
                        factors(g - 1)
                    if h == 8 and not last_group:
                        transposes(g + 1)
                squares(g, H - 1)

            transposes(0)
            group(0, True, False)
            with pe.Fori(1, G - 1) as g:
                group(g, False, False)
            group(G - 1, False, True)
            factors(G - 1)

        @block.scalar
        def _(act):
            act.wait_ge(v_gain, 1)

            def split(i):
                act.wait_ge(d_st[i % 2], 16 * (i // 2 + 1))
                nc.scalar.activation(pieces[i][1], staged(i), ACT.Copy).then_inc(a_whi, 1)

            def group(g, first):
                for b in range(GB):
                    wait(act, p_xT, g * GB + b + 1)
                    if b == 0:
                        wait(act, p_q, g * H)
                    nc.scalar.activation(xT_hi[:, :, b * SQ:(b + 1) * SQ], psX[b][:], ACT.Copy).then_inc(a_xhi, 1)
                for h in range(H):
                    if first and h in SPLIT_AT:
                        split(SPLIT_AT[h])
                    wait(act, p_q, g * H + h + 1)
                    n = (g * H + h) // 2 if isinstance(g, int) else g * (H // 2) + h // 2
                    wait(act, d_q[h % 2], n * 16)
                    nc.scalar.activation(q_out[:, h % 2, :], psQ[h % 2][:, 0:GT], ACT.Copy, scale=gprod[:])
                    wait(act, v_sqlo, g * H + h - 1)
                    nc.scalar.activation(sq[:, h % 2, :], psQ[h % 2][:, 0:GT], ACT.Square).then_inc(a_q, 1)

            split(0)
            group(0, True)
            with act.Fori(1, G) as g:
                group(g, False)

        @block.vector
        def _(dve):
            dve.wait_ge(d_g, 32)
            nc.vector.tensor_tensor(gprod[:], gqk[:], gk_sb[:], ALU.mult).then_inc(v_gain, 1)
            dve.wait_ge(g_const, 1)

            def split(i):
                dve.wait_ge(a_whi, i + 1)
                nc.vector.tensor_tensor(pieces[i][2], staged(i), pieces[i][1].bitcast(F32),
                                        ALU.subtract).then_inc(v_wlo, 1)

            def norm(g):
                wait(dve, d_x, (g + 1) * 16)
                for b in range(GB):
                    nc.vector.bn_stats(st[:, b, :], x_in[:, b, :]).then_inc(v_stat, 1)
                for b in range(GB):
                    wait(dve, v_stat, g * GB + b + 1)
                    apart(dve, dve_passed)
                    nc.vector.bn_aggr(mv[:, b, :], st[:, b, :]).then_inc(v_agg, 1)
                wait(dve, v_agg, (g + 1) * GB)
                nc.vector.tensor_scalar(ve[:], mv[:, :, 1], EPS, None, ALU.add).then_inc(v_ve, 1)
                wait(dve, g_rstd, g + 1)
                for b in range(GB):
                    wait(dve, p_xT, (g - 1) * GB + b + 1)
                    nc.vector.tensor_scalar(xn[:, b, :], x_in[:, b, :], mv[:, b, 0:1], rstd[:, b:b + 1],
                                            ALU.subtract, ALU.mult).then_inc(v_xn, 1)

            def factors(g):
                wait(dve, p_rq, g + 1)
                nc.vector.tensor_copy(rq_all[:, bass.ds(g * GB, GB), :], psR[0:SQ, :, :]).then_inc(v_rq, 1)

            def group(g, first, last):
                for b in range(GB):
                    wait(dve, a_xhi, g * GB + b + 1)
                    nc.vector.tensor_tensor(xT_lo[:, :, b * SQ:(b + 1) * SQ], psX[b][:],
                                            xT_hi[:, :, b * SQ:(b + 1) * SQ].bitcast(F32),
                                            ALU.subtract).then_inc(v_xlo, 1)
                for h in range(H):
                    if first and h in SPLIT_AT:
                        split(SPLIT_AT[h])
                    if h == 5 and not last:
                        norm(g + 1)
                    if h == 5 and not first:
                        factors(g - 1)
                    wait(dve, a_q, g * H + h + 1)
                    wait(dve, p_ss, g * H + h - 1)
                    nc.vector.tensor_copy(sq_hi[:, h % 2, :], sq[:, h % 2, :]).then_inc(v_sqhi, 1)
                    wait(dve, v_sqhi, g * H + h + 1)
                    nc.vector.tensor_tensor(sq_lo[:, h % 2, :], sq[:, h % 2, :], sq_hi[:, h % 2, :].bitcast(F32),
                                            ALU.subtract).then_inc(v_sqlo, 1)
                wait(dve, p_ss, (g + 1) * H)
                wait(dve, p_rq, g)
                nc.vector.tensor_scalar(ms[:], psS[0:H, 0:GT], D * EPS, None, ALU.add).then_inc(v_ms, 1)

            norm(0)
            split(0)
            group(0, True, False)
            with dve.Fori(1, G - 1) as g:
                group(g, False, False)
            group(G - 1, False, True)
            factors(G - 1)


def attention(nc, sbt, sem, weights, ident, rq_all, neg_half, ctxT, ctx_k, q_dram, rk_dram, o_dram):
    wk_hi, wk_lo, wv_sb, sel = (weights[k] for k in ("wk_hi", "wk_lo", "wv", "sel"))
    UQ = HG * SQ
    LEAD = 11
    HEADS, UNITS = B * H, B * NG
    with ExitStack() as ctx:
        sb = lambda name, shape, dt=F32: sbt(ctx, name, shape, dt)
        s = lambda name: sem(ctx, name)
        cT_in, cT_hi, cT_lo = sb("cT_in", [P, CC, SK]), sb("cT_hi", [P, 2, CC, SKP], F32R), sb("cT_lo", [P, 2, CC, SKP], F32R)
        cK_in, cK_hi, cK_lo = sb("cK_in", [P, 3, CD]), sb("cK_hi", [P, 2, 3, CD], F32R), sb("cK_lo", [P, 2, 3, CD], F32R)
        q_in = sb("q_in", [P, 2, UQ])
        q_hi, q_lo = sb("q_hi", [P, 2, UQ], F32R), sb("q_lo", [P, 2, UQ], F32R)
        rq = sb("rq", [SQ, 2, HG])
        k_hi, k_lo = sb("k_hi", [P, NG, HG, SKP], F32R), sb("k_lo", [P, NG, HG, SKP], F32R)
        sq = sb("sq2", [P, 2, SKP])
        sq_hi, sq_lo = sb("sq2_hi", [P, 2, SKP], F32R), sb("sq2_lo", [P, 2, SKP], F32R)
        ms = sb("ms2", [HG, SK])
        ms_sp, rk_sp = sb("ms_sp", [HG * SKR, SK // SKR]), sb("rk_sp", [HG * SKR, SK // SKR])
        rk = sb("rk", [SQ, 2, HG, SK])
        sc = sb("sc", [SQ, 2, SK])
        mx, nb, rs, ri = (sb(n, [SQ, 2]) for n in ("mx", "nb", "rs", "ri"))
        ex, pr = sb("ex", [SQ, 2, SK]), sb("pr", [SQ, 2, SK])
        pT_hi, pT_lo = sb("pT_hi", [P, 2, 3, UQ], F32R), sb("pT_lo", [P, 2, 3, UQ], F32R)
        z = sb("z", [P, CC, UQ])
        o = sb("o", [P, 2, UQ])
        psK = [ctx.enter_context(nc.psum_tensor(f"psK{i}", [P, 512], F32)) for i in range(2)]
        psN = ctx.enter_context(nc.psum_tensor("psN", [P, 512], F32))
        psS = ctx.enter_context(nc.psum_tensor("psS2", [P, 512], F32))
        psP = ctx.enter_context(nc.psum_tensor("psP", [P, 512], F32))
        psZ = [ctx.enter_context(nc.psum_tensor(f"psZ{i}", [P, 512], F32)) for i in range(CC)]
        psV = ctx.enter_context(nc.psum_tensor("psV", [P, 512], F32))

        d_cT, d_cK, d_ms, d_rs = s("d2_cT"), s("d2_cK"), s("d2_ms"), s("d2_rs")
        d_q, d_rb, d_o = ([s(f"d2_{n}{i}") for i in range(2)] for n in ("q", "rb", "o"))
        a_cT, v_cT, a_cK, v_cK, v_zero = s("a2_cT"), s("v2_cT"), s("a2_cK"), s("v2_cK"), s("v2_zero")
        a_q, v_q, v_rq = s("a2_q"), s("v2_q"), s("v2_rq")
        p_k, a_k, v_klo, v_sqhi, g_sqlo = s("p2_k"), s("a2_k"), s("v2_klo"), s("v2_sqhi"), s("g2_sqlo")
        p_ss, v_ms, g_rk, g_rq = s("p2_ss"), s("v2_ms"), s("g2_rk"), s("g2_rq")
        p_s, v_max, v_nb, a_ex, v_ri, a_pr = s("p2_s"), s("v2_max"), s("v2_nb"), s("a2_ex"), s("v2_ri"), s("a2_pr")
        p_t, a_pT, v_pT = s("p2_t"), s("a2_pT"), s("v2_pT")
        p_z, a_z, v_z, p_v, a_o = s("p2_z"), s("a2_z"), s("v2_z"), s("p2_v"), s("a2_o")
        sp_passed, dve_passed = s("sp_passed2"), s("dve_passed2")

        def real(i, count):
            return not isinstance(i, int) or 0 <= i < count

        def pipeline(eng, unit):
            def batch(b, par):
                for j in range(NG):
                    unit(b * NG + j, b, j, par)

            batch(-1, 1)
            batch(0, 0)
            batch(1, 1)
            with eng.Fori(1, B // 2 - 1) as pair:
                batch(pair * 2, 0)
                batch(pair * 2 + 1, 1)
            batch(B - 2, 0)
            batch(B - 1, 1)
            for j in range(2):
                unit(UNITS + j, B, j, 0)

        def ahead(j, h):
            return divmod((j * HG + h) % H, HG)

        block = ctx.enter_context(nc.Block())

        @block.sync
        def _(sp):
            def load_q(u, b, j):
                src = q_dram[bass.ds(held(sp, b), 1), :, j * HG:(j + 1) * HG, :].rearrange("a d h q -> d (a h) q")
                wait(sp, v_q, held(sp, u - 1))
                sp.dma_start(q_in[:, j % 2, :].rearrange("p (h q) -> p h q", q=SQ), src).then_inc(d_q[j % 2], 16)

            def load_cT(b):
                b = held(sp, b)
                src = ctxT[bass.ds(b, 1)].rearrange("a (c p) k -> p (a c) k", p=P)
                wait(sp, v_cT, b)
                sp.dma_start(cT_in[:], src).then_inc(d_cT, 16)

            def load_cK(b):
                b = held(sp, b)
                src = [ctx_k[bass.ds(b, 1), KO[i]:KO[i] + KW[i], :].rearrange("a k c -> k (a c)") for i in range(3)]
                wait(sp, v_cK, b)
                for i in range(3):
                    sp.dma_start(cK_in[0:KW[i], i, :], src[i]).then_inc(d_cK, 16)

            def spread_rk(u, slot):
                done = held(sp, u + 1)
                stored = held(sp, u * 16 + 16)
                used = held(sp, u * HG - HG)
                wait(sp, v_ms, done)
                sp.dma_start(ms_sp[:], ms[:].rearrange("h (i k) -> h i k", i=SKR)).then_inc(d_ms, 16)
                wait(sp, g_rk, done)
                sp.dma_start(rk_dram[slot, :].rearrange("(i k) -> i k", i=HG * SKR), rk_sp[:]).then_inc(d_rs, 16)
                wait(sp, d_rs, stored)
                wait(sp, v_max, used)
                sp.dma_start(rk[:, slot, :, :].rearrange("p h k -> p (h k)"),
                             rk_dram[slot:slot + 1, :].to_broadcast([SQ, HG * SK])).then_inc(d_rb[slot], 16)

            def store_o(u, b, j):
                tok = held(sp, b * SQ)
                dst = o_dram[j * HG:(j + 1) * HG, :, bass.ds(tok, SQ)].rearrange("h d t -> d h t")
                wait(sp, a_o, held(sp, u + 1))
                apart(sp, sp_passed)
                sp.dma_start(dst, o[:, j % 2, :].rearrange("p (h q) -> p h q", q=SQ)).then_inc(d_o[j % 2], 16)

            def unit(u, b, j, par):
                if j == 0 and real(b + 1, B):
                    load_cK(b + 1)
                if j == 1 and real(b + 2, B):
                    load_cT(b + 2)
                if real(u + 2, UNITS):
                    load_q(u + 2, b + (j + 2) // NG, (j + 2) % NG)
                    spread_rk(u + 2, j % 2)
                if real(u - 2, UNITS):
                    store_o(u - 2, b + (j - 2) // NG, (j - 2) % NG)

            load_cT(0)
            pipeline(sp, unit)
            for i in range(2):
                sp.wait_ge(d_o[i], 16 * UNITS // 2)

        @block.gpsimd
        def _(pool):
            def low_squares(m, h):
                wait(pool, v_sqhi, m + 1)
                nc.gpsimd.tensor_tensor(sq_lo[:, h % 2, :], sq[:, h % 2, :], sq_hi[:, h % 2, :].bitcast(F32),
                                        op=ALU.subtract).then_inc(g_sqlo, 1)

            def rms(u):
                wait(pool, d_ms, u * 16 + 16)
                wait(pool, d_rs, u * 16)
                nc.gpsimd.tensor_tensor(rk_sp[:], ms_sp[:], neg_half[0:HG * SKR, :].to_broadcast([HG * SKR, SK // SKR]),
                                        op=ALU.pow).then_inc(g_rk, 1)

            def unit(u, b, j, par):
                for h in range(HG):
                    m = u * HG + h + LEAD
                    if real(m - 1, HEADS):
                        low_squares(m - 1, (h + LEAD - 1) % HG)
                    if h == 3 and real(u + 2, UNITS):
                        rms(u + 2)

            query_factors(nc, rq_all, neg_half, G - 1).then_inc(g_rq, 1)
            pipeline(pool, unit)

        @block.tensor
        def _(pe):
            def keys(m, j, h, slot):
                wait(pe, v_klo, m - 1)
                n = 0
                for c in range(CC):
                    col = (j * HG + h) * D
                    for w, x in ((wk_hi, cT_hi), (wk_hi, cT_lo), (wk_lo, cT_hi)):
                        last = nc.tensor.matmul(psK[h % 2][:, 0:SKP], w[:, c, col:col + D], x[:, slot, c, :],
                                                start=(n == 0), stop=(n == 3 * CC - 1))
                        n += 1
                last.then_inc(p_k, 1)

            def squares(m, h, v_ms_count):
                wait(pe, g_sqlo, m + 1)
                if h == 0:
                    wait(pe, v_ms, v_ms_count)
                for part in (sq_hi, sq_lo):
                    last = nc.tensor.matmul(psN[:, 0:SKP], sel[:, P - 1 - h:2 * P - 1 - h], part[:, h % 2, :],
                                            start=(h == 0 and part is sq_hi), stop=(h == HG - 1 and part is sq_lo))
                last.then_inc(p_ss, 1)

            def scores(n, u, j, h):
                if h == 0:
                    wait(pe, v_q, u + 1)
                wait(pe, v_klo, n + 1)
                wait(pe, v_max, n)
                cols = slice(h * SQ, (h + 1) * SQ)
                for i, (w, x) in enumerate(((q_hi, k_hi), (q_hi, k_lo), (q_lo, k_hi))):
                    last = nc.tensor.matmul(psS[0:SQ, 0:SKP], w[:, j % 2, cols], x[:, j, h, :],
                                            start=(i == 0), stop=(i == 2))
                last.then_inc(p_s, 1)

            def transposes(n, h):
                wait(pe, a_pr, n + 1)
                wait(pe, v_pT, n)
                for i in range(3):
                    last = nc.tensor.transpose(psP[0:KW[i], i * SQ:(i + 1) * SQ],
                                               pr[:, h % 2, KO[i]:KO[i] + KW[i]], ident[0:SQ, 0:SQ])
                last.then_inc(p_t, 1)

            def gather(u, j, slot, c):
                wait(pe, v_pT, u * HG + HG)
                wait(pe, v_z if c else a_z, u)
                n = 0
                for i in range(3):
                    for w, x in ((cK_hi, pT_hi), (cK_hi, pT_lo), (cK_lo, pT_hi)):
                        last = nc.tensor.matmul(psZ[c][:, 0:UQ], w[0:KW[i], slot, i, c * P:(c + 1) * P],
                                                x[0:KW[i], j % 2, i, :], start=(n == 0), stop=(n == 8))
                        n += 1
                last.then_inc(p_z, 1)

            def values(u, j, heads):
                for h in heads:
                    if h == 0:
                        wait(pe, a_z, u + 1)
                        wait(pe, v_z, u + 1)
                        wait(pe, a_o, u)
                    col = (j * HG + h) * D
                    for c in range(CC):
                        last = nc.tensor.matmul(psV[:, h * SQ:(h + 1) * SQ], wv_sb[:, c, col:col + D],
                                                z[:, c, h * SQ:(h + 1) * SQ], start=(c == 0), stop=(c == CC - 1))
                    if h == HG - 1:
                        last.then_inc(p_v, 1)

            def unit(u, b, j, par):
                for h in range(HG):
                    n = u * HG + h
                    m = n + LEAD
                    if real(n, HEADS):
                        scores(n, u, j, h)
                    if real(m, HEADS):
                        jm, hm = ahead(j, h + LEAD)
                        if jm == 0 and hm == 0:
                            wait(pe, v_cT, b + 2)
                        keys(m, jm, hm, 1 - par if j * HG + h + LEAD >= H else par)
                    if real(m - 2, HEADS):
                        hs = (h + LEAD - 2) % HG
                        squares(m - 2, hs, u + (h + LEAD - 2) // HG)
                    if real(n - 2, HEADS):
                        transposes(n - 2, (h - 2) % HG)
                    if h < 2 and real(u - 2, UNITS):
                        values(u - 2, (j - 2) % NG, (2 * h, 2 * h + 1))
                    if h >= 2 and real(u - 1, UNITS):
                        if j == 1 and h == 2:
                            wait(pe, v_cK, b + 1)
                        gather(u - 1, (j - 1) % NG, par if j else 1 - par, h - 2)

            pe.wait_ge(v_zero, 3)
            pipeline(pe, unit)

        @block.scalar
        def _(act):
            def high_cT(b, slot):
                wait(act, d_cT, b * 16 + 16)
                wait(act, p_k, b * H - H)
                nc.scalar.activation(cT_hi[:, slot, :, 0:SK], cT_in[:], ACT.Copy).then_inc(a_cT, 1)

            def high_cK(b, slot):
                wait(act, d_cK, b * 48 + 48)
                wait(act, p_z, (b - 1) * NG * CC)
                for i in range(3):
                    nc.scalar.activation(cK_hi[0:KW[i], slot, i, :], cK_in[0:KW[i], i, :], ACT.Copy).then_inc(a_cK, 1)

            def high_q(u, count, j):
                wait(act, d_q[j % 2], count)
                wait(act, p_s, u * HG - HG)
                nc.scalar.activation(q_hi[:, j % 2, :], q_in[:, j % 2, :], ACT.Copy).then_inc(a_q, 1)

            def high_k(m, j, h):
                wait(act, p_k, m + 1)
                wait(act, p_s, m - H + 1)
                nc.scalar.activation(k_hi[:, j, h, :], psK[h % 2][:, 0:SKP], ACT.Copy)

            def square_k(m, h):
                wait(act, g_sqlo, m - 1)
                nc.scalar.activation(sq[:, h % 2, :], psK[h % 2][:, 0:SKP], ACT.Square).then_inc(a_k, 1)

            def exponential(n, j, h):
                wait(act, v_nb, n + 1)
                wait(act, a_pr, n - 1)
                nc.scalar.activation(ex[:, h % 2, :], sc[:, h % 2, :], ACT.Exp, bias=nb[:, h % 2:h % 2 + 1],
                                     scale=rq[:, j % 2, h:h + 1], accum_out=rs[:, h % 2:h % 2 + 1]).then_inc(a_ex, 1)

            def normalise(n, h):
                wait(act, v_ri, n + 1)
                wait(act, p_t, n - 1)
                nc.scalar.activation(pr[:, h % 2, :], ex[:, h % 2, :], ACT.Copy, scale=ri[:, h % 2:h % 2 + 1]
                                     ).then_inc(a_pr, 1)

            def high_pT(n, u, j, h):
                wait(act, p_t, n + 1)
                if h == 0:
                    wait(act, p_z, (u - 1) * CC)
                nc.scalar.activation(pT_hi[0:KW[0], j % 2, :, h * SQ:(h + 1) * SQ],
                                     psP[0:KW[0], 0:3 * SQ].rearrange("p (i q) -> p i q", q=SQ),
                                     ACT.Copy).then_inc(a_pT, 1)

            def copy_z(u):
                wait(act, p_z, u * CC + 1)
                wait(act, p_v, u)
                nc.scalar.activation(z[:, 0, :], psZ[0][:, 0:UQ], ACT.Copy).then_inc(a_z, 1)

            def copy_o(u, count, j):
                wait(act, p_v, u + 1)
                wait(act, d_o[j % 2], count)
                nc.scalar.activation(o[:, j % 2, :], psV[:, 0:UQ], ACT.Copy).then_inc(a_o, 1)

            def unit(u, b, j, par):
                for h in range(HG):
                    n = u * HG + h
                    m = n + LEAD
                    jm, hm = ahead(j, h + LEAD)
                    if real(n - 1, HEADS):
                        normalise(n - 1, (h - 1) % HG)
                    if j == 0 and h == 1 and real(b + 1, B):
                        high_cT(b + 1, 1 - par)
                    if j == 2 and h == 0 and real(b + 1, B):
                        high_cK(b + 1, 1 - par)
                    if h == 1 and real(u + 1, UNITS):
                        high_q(u + 1, (b * 2 + (j + 1) // 2 + 1) * 16, (j + 1) % NG)
                    if h == 2 and real(u - 2, UNITS):
                        copy_o(u - 2, (b * 2 + (j - 2) // 2) * 16, (j - 2) % NG)
                    if h == 3 and real(u - 1, UNITS):
                        copy_z(u - 1)
                    if real(m, HEADS):
                        high_k(m, jm, hm)
                    if real(n, HEADS):
                        exponential(n, j, h)
                    if real(m, HEADS):
                        square_k(m, hm)
                    if real(n - 2, HEADS):
                        high_pT(n - 2, u + (h - 2) // HG, (j + (h - 2) // HG) % NG, (h - 2) % HG)

            act.wait_ge(v_zero, 3)
            pipeline(act, unit)

        @block.vector
        def _(dve):
            nc.vector.memset(cT_hi[:, :, :, SK:SKP].bitcast(F32), 0.0).then_inc(v_zero, 1)
            nc.vector.memset(cT_lo[:, :, :, SK:SKP].bitcast(F32), 0.0).then_inc(v_zero, 1)
            nc.vector.memset(psP[:], 0.0).then_inc(v_zero, 1)

            def low_cT(b, slot):
                wait(dve, a_cT, b + 1)
                nc.vector.tensor_tensor(cT_lo[:, slot, :, 0:SK], cT_in[:], cT_hi[:, slot, :, 0:SK].bitcast(F32),
                                        ALU.subtract).then_inc(v_cT, 1)

            def low_cK(b, slot):
                wait(dve, a_cK, b * 3 + 3)
                for i in range(3):
                    last = nc.vector.tensor_tensor(cK_lo[0:KW[i], slot, i, :], cK_in[0:KW[i], i, :],
                                                   cK_hi[0:KW[i], slot, i, :].bitcast(F32), ALU.subtract)
                last.then_inc(v_cK, 1)

            def low_q(u, b, j):
                wait(dve, a_q, u + 1)
                nc.vector.tensor_tensor(q_lo[:, j % 2, :], q_in[:, j % 2, :], q_hi[:, j % 2, :].bitcast(F32),
                                        ALU.subtract).then_inc(v_q, 1)
                nc.vector.tensor_copy(rq[:, j % 2, :], rq_all[:, bass.ds(b, 1), j * HG:(j + 1) * HG]
                                      .rearrange("p a h -> p (a h)")).then_inc(v_rq, 1)

            def low_k(m, j, h):
                wait(dve, a_k, m + 1)
                nc.vector.tensor_tensor(k_lo[:, j, h, :], psK[h % 2][:, 0:SKP], k_hi[:, j, h, :].bitcast(F32),
                                        ALU.subtract).then_inc(v_klo, 1)

            def high_squares(m, h):
                wait(dve, p_ss, m - 1)
                nc.vector.tensor_copy(sq_hi[:, h % 2, :], sq[:, h % 2, :]).then_inc(v_sqhi, 1)

            def mean_squares(u):
                wait(dve, p_ss, u * HG + HG)
                wait(dve, d_ms, u * 16)
                nc.vector.tensor_scalar(ms[:], psN[0:HG, 0:SK], 1.0 / D, EPS, ALU.mult, ALU.add).then_inc(v_ms, 1)

            def low_pT(n, j, h):
                wait(dve, a_pT, n + 1)
                nc.vector.tensor_tensor(pT_lo[0:KW[0], j % 2, :, h * SQ:(h + 1) * SQ],
                                        psP[0:KW[0], 0:3 * SQ].rearrange("p (i q) -> p i q", q=SQ),
                                        pT_hi[0:KW[0], j % 2, :, h * SQ:(h + 1) * SQ].bitcast(F32),
                                        ALU.subtract).then_inc(v_pT, 1)

            def invert_sum(n, h):
                k = slice(h % 2, h % 2 + 1)
                wait(dve, a_ex, n + 1)
                wait(dve, a_pr, n - 1)
                nc.vector.reciprocal(ri[:, k], rs[:, k]).then_inc(v_ri, 1)

            def scale_scores(n, u, b, j, h):
                if h == 0:
                    wait(dve, d_rb[j % 2], (b * 2 + j // 2 + 1) * 16)
                    wait(dve, v_rq, u + 1)
                wait(dve, a_ex, n - 1)
                wait(dve, p_s, n + 1)
                apart(dve, dve_passed)
                nc.vector.tensor_tensor_reduce(out=sc[:, h % 2, :], in0=psS[0:SQ, 0:SK], in1=rk[:, j % 2, h, :],
                                               scale=1.0, scalar=-3.0e38, op0=ALU.mult, op1=ALU.max,
                                               accum_out=mx[:, h % 2:h % 2 + 1]).then_inc(v_max, 1)

            def negate_max(n, j, h):
                k = slice(h % 2, h % 2 + 1)
                wait(dve, v_max, n + 1)
                nc.vector.tensor_scalar(nb[:, k], mx[:, k], rq[:, j % 2, h:h + 1], -1.0, ALU.mult,
                                        ALU.mult).then_inc(v_nb, 1)

            def copy_z(u):
                wait(dve, p_z, u * CC + 2)
                wait(dve, p_v, u)
                nc.vector.tensor_copy(z[:, 1, :], psZ[1][:, 0:UQ]).then_inc(v_z, 1)

            def unit(u, b, j, par):
                for h in range(HG):
                    n = u * HG + h
                    m = n + LEAD
                    if real(n - 1, HEADS):
                        invert_sum(n - 1, (h - 1) % HG)
                    if h == 3 and real(u + 2, UNITS):
                        mean_squares(u + 2)
                    if real(n - 3, HEADS):
                        low_pT(n - 3, (j + (h - 3) // HG) % NG, (h - 3) % HG)
                    if h == 0 and real(u - 2, UNITS):
                        copy_z(u - 2)
                    if real(n, HEADS):
                        scale_scores(n, u, b, j, h)
                    if real(m - 1, HEADS):
                        low_k(m - 1, *ahead(j, h + LEAD - 1))
                    if real(n, HEADS):
                        negate_max(n, j, h)
                    if real(m - 1, HEADS):
                        high_squares(m - 1, (h + LEAD - 1) % HG)
                    if j == 0 and h == 2 and real(b + 1, B):
                        low_cT(b + 1, 1 - par)
                    if j == 2 and h == 1 and real(b + 1, B):
                        low_cK(b + 1, 1 - par)
                    if h == 2 and real(u + 1, UNITS):
                        low_q(u + 1, b + (j + 1) // NG, (j + 1) % NG)

            pipeline(dve, unit)


def feed_forward(nc, sbt, sem, ident, neg_half, x, wo, w_ff, had_in, o_dram, out):
    WC = 4
    NB = FF // DIM
    with ExitStack() as ctx:
        sb = lambda name, shape, dt=F32: sbt(ctx, name, shape, dt)
        s = lambda name: sem(ctx, name)
        wo_hi, wo_lo = sb("wo_hi", [P, H, DIM], F32R), sb("wo_lo", [P, H, DIM], F32R)
        wt = sb("wt", [P, 3, WC, FF], FP8)
        stage = sb("stage3", [P, 2, FF])
        below = sb("below", [P, FF], BF16)
        had = sb("had", [P, DC, DIM], F32R)
        ones = sb("ones", [P, P])
        asum, asums = sb("asum", [P, 3, WC]), sb("asums", [P, 3])
        wsc, half, nhalf, w127 = (sb(n, [P, 3]) for n in ("wsc", "half", "nhalf", "w127"))
        o_in = sb("o_in", [P, H, TT])
        o_hi, o_lo = sb("o_hi", [P, H, TT], F32R), sb("o_lo", [P, H, TT], F32R)
        x_in, x1, x1_old, xn = (sb(n, [P, DIM]) for n in ("x_in3", "x1", "x1_old", "xn3"))
        st, mv, ve, rstd = sb("st3", [P, 6]), sb("mv3", [P, 2]), sb("ve3", [P, 1]), sb("rstd3", [P, 1])
        xT_hi, xT_lo = sb("xT3_hi", [P, DC, TT], F32R), sb("xT3_lo", [P, DC, TT], F32R)
        mx, am, rc, sq = (sb(n, [P, 2]) for n in ("mx3", "am3", "rc3", "sq3"))
        al, ald = sb("al", [P, 2]), sb("ald", [P, 1])
        mag1, mag2 = sb("mag1", [P, DIM]), sb("mag2", [P, FF])
        q1, q1T = sb("q1", [P, DIM], BF16), sb("q1T", [P, DC, TT], BF16)
        q2, q2T = sb("q2", [P, FF], BF16), sb("q2T", [P, FC, TT], BF16)
        sil = sb("sil", [P, 2, DIM])
        hid = stage[:, 0, :].rearrange("p (n j) -> p n j", j=DIM)
        half_rot = stage[:, 1, :].rearrange("p (n j) -> p n j", j=DIM)
        hT_hi, hT_lo = sb("hT_hi", [P, FC, TT], F32R), sb("hT_lo", [P, FC, TT], F32R)
        y = sb("y", [P, DIM])
        ident_b = sb("ident_b", [P, P], BF16)
        psB = ctx.enter_context(nc.psum_tensor("psB", [P, NB, DIM], F32))
        psA = ctx.enter_context(nc.psum_tensor("psA", [P, DIM], F32))
        psF = ctx.enter_context(nc.psum_tensor("psF", [P, DIM], F32))
        psT = [ctx.enter_context(nc.psum_tensor(f"psT{i}", [P, DIM], F32)) for i in range(2)]
        psTb = [t[:].bitcast(BF16) for t in psT]

        d_st = [s("d3_st0"), s("d3_st1")]
        d_o, d_x, d_out, d_had = s("d3_o"), s("d3_x"), s("d3_out"), s("d3_had")
        a_w, v_w, v_sum, v_sums, p_sum, v_mean, v_thr = (s(n) for n in ("a3_w", "v3_w", "v3_sum", "v3_sums", "p3_sum",
                                                                         "v3_mean", "v3_thr"))
        v_below, v_wt, v_had, g_ones = s("v3_below"), s("v3_wt"), s("v3_had"), s("g3_ones")
        a_o, v_o = s("a3_o"), s("v3_o")
        p1, p2, p3, p4, p5, p6, p7, p8, p9 = (s(f"p3_{i}") for i in range(1, 10))
        v_x1, v_st, v_ag, v_ve, g_rs, v_xn = (s(n) for n in ("v3_x1", "v3_st", "v3_ag", "v3_ve", "g3_rs", "v3_xn"))
        a_xT, v_xT = s("a3_xT"), s("v3_xT")
        v_mx, v_am, v_rc, v_sq, v_al = ([s(f"v3_{n}{i}") for i in range(2)] for n in ("mx", "am", "rc", "sq", "al"))
        a_mag, v_q = ([s(f"{n}{i}") for i in range(2)] for n in ("a3_mag", "v3_q"))
        a_q1T, a_q2T, a_sil, v_h, v_r1, v_r2 = (s(n) for n in ("a3_q1T", "a3_q2T", "a3_sil", "v3_h", "v3_r1", "v3_r2"))
        a_hT, v_hT, v_y, v_old = s("a3_hT"), s("v3_hT"), s("v3_y"), s("v3_old")

        wo_v = wo.rearrange("(j h d) n -> j d h n", d=D, h=HG)
        jobs = [("wo", j) for j in range(NG)] + [("had", 0)]
        jobs += [("sum", w, c) for w in range(3) for c in range(WC)]
        jobs += [("round", w, c) for w in range(3) for c in range(WC)]
        FREED = len(jobs)

        pe_passed, dve_passed = s("pe_passed3"), s("dve_passed3")
        block = ctx.enter_context(nc.Block())

        def tiles(eng, body):
            body(0, True, False)
            with eng.Fori(1, TILES - 1) as t:
                body(t, False, False)
            body(TILES - 1, False, True)

        @block.sync
        def _(sp):
            def load_o(t, tok):
                src = o_dram[:, :, bass.ds(tok, TT)].rearrange("h d t -> d h t")
                wait(sp, v_o, t)
                sp.dma_start(o_in[:], src).then_inc(d_o, 16)

            def load_x(t, tok):
                src = x[bass.ds(tok, TT), :]
                wait(sp, v_x1, t)
                sp.dma_start(x_in[:], src).then_inc(d_x, 16)

            def store(tok, count):
                dst = out[bass.ds(tok, TT), :]
                wait(sp, v_y, count)
                sp.dma_start(dst, y[:]).then_inc(d_out, 16)

            def front_loads(t, tok):
                load_o(t, tok)
                load_x(t, tok)

            for i, job in enumerate(jobs):
                if i >= 2:
                    sp.wait_ge(v_w, i - 1)
                if job[0] == "wo":
                    src, dst = wo_v[job[1]], stage[:, i % 2, :].rearrange("p (h n) -> p h n", h=HG)
                elif job[0] == "had":
                    src, dst = had_in.rearrange("(c p) n -> p c n", p=P), stage[:, i % 2, :].rearrange("p (c n) -> p c n", c=DC)
                else:
                    src, dst = w_ff[job[1], job[2]], stage[:, i % 2, :]
                sp.dma_start(dst, src).then_inc(d_st[i % 2], 16)
                if i == 1:
                    load_o(0, 0)
                    load_x(0, 0)
            front_loads(1, TT)
            with sp.Fori(1, TILES - 2) as t:
                front_loads(sp.snap(t + 1), sp.snap(t * TT + TT))
                store(sp.snap(t * TT - TT), sp.snap(t))
            front_loads(TILES - 1, LAST_TOK)
            store((TILES - 3) * TT, TILES - 2)
            store((TILES - 2) * TT, TILES - 1)
            store(LAST_TOK, TILES)
            sp.wait_ge(d_out, 16 * TILES)

        @block.gpsimd
        def _(pool):
            nc.gpsimd.memset(ones[:], 1.0).then_inc(g_ones, 1)

            def body(t, first, last):
                wait(pool, v_ve, t + 1)
                nc.gpsimd.tensor_tensor(rstd[:], ve[:], neg_half[:], op=ALU.pow).then_inc(g_rs, 1)

            tiles(pool, body)

        @block.tensor
        def _(pe):
            pe.wait_ge(g_ones, 1)
            pe.wait_ge(v_sums, 1)
            nc.tensor.matmul(psF[:, 0:3], ones[:], asums[:], start=True, stop=True).then_inc(p_sum, 1)

            def out_proj(t):
                wait(pe, v_o, t + 1)
                wait(pe, v_y, t - 1)
                n = 0
                for h in range(H):
                    for w, m in ((o_hi, wo_hi), (o_hi, wo_lo), (o_lo, wo_hi)):
                        last = nc.tensor.matmul(psA[:], w[:, h, :], m[:, h, :], start=(n == 0), stop=(n == 3 * H - 1))
                        n += 1
                last.then_inc(p1, 1)

            def norm_T(t):
                wait(pe, v_xn, t + 1)
                wait(pe, v_hT, t * NB)
                for c in range(DC):
                    last = nc.tensor.transpose(psT[0][:, c * P:(c + 1) * P], xn[:, c * P:(c + 1) * P], ident[:])
                last.then_inc(p2, 1)

            def rotate_in(t):
                wait(pe, v_xT, t + 1)
                wait(pe, a_mag[0], t)
                for c in range(DC):
                    for m in (xT_hi, xT_lo):
                        last = nc.tensor.matmul(psF[:], m[:, c, :], had[:, c, :], start=(c == 0 and m is xT_hi),
                                                stop=(c == DC - 1 and m is xT_lo))
                last.then_inc(p3, 1)

            def q1_T(t):
                wait(pe, v_q[0], t + 1)
                wait(pe, a_q2T, 2 * t)
                wait(pe, v_hT, t * NB)
                for c in range(DC):
                    last = nc.tensor.transpose(psTb[1][:, c * P:(c + 1) * P], q1[:, c * P:(c + 1) * P], ident_b[:])
                last.then_inc(p4, 1)

            def gate_up(t, first):
                wait(pe, a_q1T, t + 1)
                if first:
                    pe.wait_ge(v_wt, 2 * WC)
                wait(pe, a_mag[1], t)
                for j in range(NB):
                    wait(pe, v_h, t * NB + j - 1)
                    apart(pe, pe_passed)
                    for k in range(2):
                        for c in range(DC):
                            last = nc.tensor.matmul(psB[:, 2 * (j % 2) + k, :], q1T[:, c, :],
                                                    wt[:, k, c, j * DIM:(j + 1) * DIM], start=(c == 0), stop=(c == DC - 1))
                    last.then_inc(p5, 1)

            def hidden_T(t):
                wait(pe, v_r2, 2 * t + 2)
                for n in range(NB):
                    if n == 0:
                        wait(pe, a_q2T, 2 * t)
                        wait(pe, a_q1T, t + 1)
                    else:
                        wait(pe, v_hT, t * NB + n - 1)
                    for c in range(DC):
                        last = nc.tensor.transpose(psT[n % 2][:, c * P:(c + 1) * P], hid[:, n, c * P:(c + 1) * P], ident[:])
                    last.then_inc(p6, 1)

            def rotate_hidden(t, blocks):
                for n in blocks:
                    wait(pe, v_hT, t * NB + n + 1)
                    if n == 0:
                        wait(pe, v_h, t * NB + NB)
                    for c in range(DC):
                        for m in (hT_hi, hT_lo):
                            last = nc.tensor.matmul(psB[:, n, :], m[:, n * DC + c, :], had[:, c, :],
                                                    start=(c == 0 and m is hT_hi), stop=(c == DC - 1 and m is hT_lo))
                    last.then_inc(p7, 1)

            def q2_T(t, front):
                wait(pe, v_q[1], t + 1)
                if front:
                    wait(pe, v_xT, t + 2)
                wait(pe, v_hT, t * NB + NB)
                for k in range(2):
                    for c in range(FC // 2):
                        i = k * FC // 2 + c
                        last = nc.tensor.transpose(psTb[k][:, c * P:(c + 1) * P], q2[:, i * P:(i + 1) * P], ident_b[:])
                    last.then_inc(p8, 1)

            def down(t, part, front):
                if part == 0 and front:
                    wait(pe, v_x1, t + 2)
                wait(pe, a_q2T, 2 * t + part + 1)
                apart(pe, pe_passed)
                for i in range(part * FC // 2, (part + 1) * FC // 2):
                    last = nc.tensor.matmul(psA[:], q2T[:, i, :], wt[:, 2, i // WC, (i % WC) * DIM:(i % WC + 1) * DIM],
                                            start=(i == 0), stop=(i == FC - 1))
                if part == 1:
                    last.then_inc(p9, 1)

            pe.wait_ge(v_had, 2)

            def body(t, first, last):
                if first:
                    pe.wait_ge(v_w, NG)
                out_proj(t)
                if not first:
                    hidden_T(t - 1)
                    rotate_hidden(t - 1, range(0, NB // 2))
                norm_T(t)
                if not first:
                    rotate_hidden(t - 1, range(NB // 2, NB))
                rotate_in(t)
                if not first:
                    q2_T(t - 1, True)
                    down(t - 1, 0, True)
                q1_T(t)
                if not first:
                    down(t - 1, 1, True)
                gate_up(t, first)

            body(0, True, False)
            pe.wait_ge(v_wt, 3 * WC)
            with pe.Fori(1, TILES - 1) as t:
                body(t, False, False)
            body(TILES - 1, False, True)
            hidden_T(TILES - 1)
            rotate_hidden(TILES - 1, range(NB))
            q2_T(TILES - 1, False)
            down(TILES - 1, 0, False)
            down(TILES - 1, 1, False)

        @block.scalar
        def _(act):
            def high_o(t):
                wait(act, d_o, t * 16 + 16)
                wait(act, p1, t)
                nc.scalar.activation(o_hi[:], o_in[:], ACT.Copy).then_inc(a_o, 1)

            for i in range(NG):
                act.wait_ge(d_st[i % 2], 16 * (i // 2 + 1))
                nc.scalar.activation(wo_hi[:, i * HG:(i + 1) * HG, :].rearrange("p h n -> p (h n)"), stage[:, i % 2, :],
                                     ACT.Copy).then_inc(a_w, 1)
                if i == 1:
                    high_o(0)

            def high_hT(t):
                for n in range(NB):
                    wait(act, p6, t * NB + n + 1)
                    if n == 0:
                        wait(act, p7, t * NB)
                    nc.scalar.activation(hT_hi[:, n * DC:(n + 1) * DC, :].rearrange("p c t -> p (c t)"),
                                         psT[n % 2][:], ACT.Copy).then_inc(a_hT, 1)

            def high_xT(t):
                wait(act, p2, t + 1)
                nc.scalar.activation(xT_hi[:].rearrange("p c t -> p (c t)"), psT[0][:], ACT.Copy).then_inc(a_xT, 1)

            def round1(t):
                wait(act, v_sq[0], t + 1)
                wait(act, v_q[0], t)
                nc.scalar.activation(mag1[:], psF[:], ACT.Copy, bias=MAGIC, scale=sq[:, 0:1]).then_inc(a_mag[0], 1)

            def round2(t):
                wait(act, v_sq[1], t + 1)
                wait(act, v_q[1], t)
                nc.scalar.activation(mag2[:], psB[:].rearrange("p n j -> p (n j)"), ACT.Copy, bias=MAGIC,
                                     scale=sq[:, 1:2]).then_inc(a_mag[1], 1)

            def copy_q2T(t):
                for k in range(2):
                    wait(act, p8, 2 * t + k + 1)
                    if k == 0:
                        wait(act, p9, t)
                    nc.scalar.activation(q2T[:, k * FC // 2:(k + 1) * FC // 2, :].rearrange("p c t -> p (c t)"),
                                         psTb[k][:, 0:FC // 2 * TT], ACT.Copy).then_inc(a_q2T, 1)

            def copy_q1T(t):
                wait(act, p4, t + 1)
                wait(act, p5, t * NB)
                nc.scalar.activation(q1T[:].rearrange("p c t -> p (c t)"), psTb[1][:, 0:DIM], ACT.Copy).then_inc(a_q1T, 1)

            def silus(t):
                wait(act, v_al[0], t + 1)
                for j in range(NB):
                    wait(act, p5, t * NB + j + 1)
                    wait(act, v_h, t * NB + j - 1)
                    nc.scalar.activation(sil[:, j % 2, :], psB[:, 2 * (j % 2), :], ACT.Silu, scale=al[:, 0:1]
                                         ).then_inc(a_sil, 1)

            def body(t, first, last):
                if not first:
                    high_hT(t - 1)
                high_xT(t)
                if not first:
                    round2(t - 1)
                round1(t)
                if not last:
                    high_o(t + 1)
                if not first:
                    copy_q2T(t - 1)
                copy_q1T(t)
                silus(t)

            tiles(act, body)
            high_hT(TILES - 1)
            round2(TILES - 1)
            copy_q2T(TILES - 1)

        @block.vector
        def _(dve):
            def low_o(t):
                wait(dve, a_o, t + 1)
                nc.vector.tensor_tensor(o_lo[:], o_in[:], o_hi[:].bitcast(F32), ALU.subtract).then_inc(v_o, 1)

            nc.vector.tensor_copy(ident_b[:], ident[:]).then_inc(v_had, 1)
            for i, job in enumerate(jobs):
                piece = stage[:, i % 2, :]
                arrived = 16 * (i // 2 + 1)
                if job[0] == "wo":
                    j = job[1]
                    dve.wait_ge(a_w, j + 1)
                    part = wo_hi[:, j * HG:(j + 1) * HG, :].rearrange("p h n -> p (h n)").bitcast(F32)
                    nc.vector.tensor_tensor(wo_lo[:, j * HG:(j + 1) * HG, :].rearrange("p h n -> p (h n)"), piece, part,
                                            ALU.subtract).then_inc(v_w, 1)
                    if j == 1:
                        low_o(0)
                elif job[0] == "had":
                    dve.wait_ge(d_st[i % 2], arrived)
                    nc.vector.tensor_copy(had[:].rearrange("p c n -> p (c n)"), piece).then_inc(v_w, 1)
                    dve.wait_ge(v_w, i + 1)
                    nc.vector.memset(mx[:], 0.0).then_inc(v_had, 1)
                elif job[0] == "sum":
                    _, w, c = job
                    dve.wait_ge(d_st[i % 2], arrived)
                    nc.vector.tensor_reduce(asum[:, w, c:c + 1], piece, axis=AX.X, op=ALU.add,
                                            apply_absolute_value=True).then_inc(v_w, 1)
                    if (w, c) == (2, WC - 1):
                        dve.wait_ge(v_w, i + 1)
                        nc.vector.tensor_reduce(asums[:], asum[:], axis=AX.X, op=ALU.add).then_inc(v_sums, 1)
                        dve.wait_ge(p_sum, 1)
                        nc.vector.tensor_scalar(wsc[:], psF[:, 0:3], 1.0 / (DIM * FF), EPS, ALU.mult, ALU.max).then_inc(v_mean, 1)
                        dve.wait_ge(v_mean, 1)
                        nc.vector.tensor_scalar(half[:], wsc[:], 0.5, None, ALU.mult).then_inc(v_thr, 1)
                        nc.vector.tensor_scalar(nhalf[:], wsc[:], -0.5, None, ALU.mult).then_inc(v_thr, 1)
                        nc.vector.tensor_scalar(w127[:], wsc[:], 1.0 / 127.0, None, ALU.mult).then_inc(v_thr, 1)
                        dve.wait_ge(v_thr, 3)
                else:
                    _, w, c = job
                    k = w * WC + c
                    dve.wait_ge(d_st[i % 2], arrived)
                    nc.vector.tensor_scalar(below[:], piece, nhalf[:, w:w + 1], None, ALU.is_lt).then_inc(v_below, 1)
                    dve.wait_ge(v_below, k + 1)
                    nc.vector.scalar_tensor_tensor(wt[:, w, c, :], piece, half[:, w:w + 1], below[:], ALU.is_gt,
                                                   ALU.subtract, saturate=False).then_inc(v_wt, 1)
                    dve.wait_ge(v_wt, k + 1)
                    nc.vector.memset(mx[:], 0.0).then_inc(v_w, 1)

            def rotate4(t):
                wait(dve, v_h, t * NB + NB)
                pairs = hid.rearrange("p (a b) j -> p a b j", b=2)
                halves = half_rot.rearrange("p (a b) j -> p a b j", b=2)
                for b, op in enumerate((ALU.add, ALU.subtract)):
                    nc.vector.tensor_tensor(halves[:, :, b, :], pairs[:, :, 0, :], pairs[:, :, 1, :], op).then_inc(v_r1, 1)
                wait(dve, v_r1, 2 * t + 2)
                for a, op in enumerate((ALU.add, ALU.subtract)):
                    nc.vector.tensor_tensor(pairs[:, a, :, :], halves[:, 0, :, :], halves[:, 1, :, :], op).then_inc(v_r2, 1)

            def keep(t):
                wait(dve, v_y, t)
                nc.vector.tensor_copy(x1_old[:], x1[:]).then_inc(v_old, 1)

            def low_hT(t, n):
                wait(dve, a_hT, t * NB + n + 1)
                nc.vector.tensor_tensor(hT_lo[:, n * DC:(n + 1) * DC, :].rearrange("p c t -> p (c t)"), psT[n % 2][:],
                                        hT_hi[:, n * DC:(n + 1) * DC, :].rearrange("p c t -> p (c t)").bitcast(F32),
                                        ALU.subtract).then_inc(v_hT, 1)

            def residual(t):
                wait(dve, p1, t + 1)
                wait(dve, d_x, t * 16 + 16)
                wait(dve, v_old, t)
                nc.vector.tensor_tensor(x1[:], psA[:], x_in[:], ALU.add).then_inc(v_x1, 1)
                wait(dve, v_x1, t + 1)
                nc.vector.bn_stats(st[:], x1[:]).then_inc(v_st, 1)
                wait(dve, v_st, t + 1)
                apart(dve, dve_passed)
                nc.vector.bn_aggr(mv[:], st[:]).then_inc(v_ag, 1)
                wait(dve, v_ag, t + 1)
                nc.vector.tensor_scalar(ve[:], mv[:, 1:2], EPS, None, ALU.add).then_inc(v_ve, 1)

            def norm(t):
                wait(dve, g_rs, t + 1)
                wait(dve, p2, t)
                nc.vector.tensor_scalar(xn[:], x1[:], mv[:, 0:1], rstd[:], ALU.subtract, ALU.mult).then_inc(v_xn, 1)

            def low_xT(t):
                wait(dve, a_xT, t + 1)
                nc.vector.tensor_tensor(xT_lo[:].rearrange("p c t -> p (c t)"), psT[0][:],
                                        xT_hi[:].rearrange("p c t -> p (c t)").bitcast(F32), ALU.subtract).then_inc(v_xT, 1)

            def scales(i, t, ps, n, factor, weight):
                c = slice(i, i + 1)
                norm_n = float(n) ** -0.5
                nc.vector.tensor_reduce(mx[:, c], ps, axis=AX.X, op=ALU.max, apply_absolute_value=True).then_inc(v_mx[i], 1)
                wait(dve, v_mx[i], t + 1)
                nc.vector.tensor_scalar(am[:, c], mx[:, c], norm_n, EPS, ALU.mult, ALU.max).then_inc(v_am[i], 1)
                wait(dve, v_am[i], t + 1)
                nc.vector.reciprocal(rc[:, c], am[:, c]).then_inc(v_rc[i], 1)
                wait(dve, v_rc[i], t + 1)
                nc.vector.tensor_scalar(sq[:, c], rc[:, c], 127.0 * norm_n, None, ALU.mult).then_inc(v_sq[i], 1)
                nc.vector.tensor_scalar(factor, weight, am[:, c], None, ALU.mult).then_inc(v_al[i], 1)

            def to_int(i, t, q, mag):
                wait(dve, a_mag[i], t + 1)
                nc.vector.tensor_scalar(q, mag, MAGIC, 127.0, ALU.subtract, ALU.min).then_inc(v_q[i], 1)

            def hidden(t):
                for j in range(NB):
                    wait(dve, a_sil, t * NB + j + 1)
                    nc.vector.scalar_tensor_tensor(hid[:, j, :], psB[:, 2 * (j % 2) + 1, :], al[:, 1:2], sil[:, j % 2, :],
                                                   ALU.mult, ALU.mult).then_inc(v_h, 1)

            def result(t):
                wait(dve, p9, t + 1)
                wait(dve, d_out, t * 16)
                wait(dve, v_al[1], t + 1)
                nc.vector.scalar_tensor_tensor(y[:], psA[:], ald[:], x1_old[:], ALU.mult, ALU.add).then_inc(v_y, 1)

            def back_scales(t):
                wait(dve, p7, t * NB + NB)
                wait(dve, p8, 2 * t)
                scales(1, t, psB[:].rearrange("p n j -> p (n j)"), FF, ald[:], w127[:, 2:3])

            def body(t, first, last):
                if not first:
                    rotate4(t - 1)
                    keep(t - 1)
                    low_hT(t - 1, 0)
                    low_hT(t - 1, 1)
                residual(t)
                if not first:
                    low_hT(t - 1, 2)
                    low_hT(t - 1, 3)
                norm(t)
                low_xT(t)
                if not first:
                    back_scales(t - 1)
                wait(dve, p3, t + 1)
                wait(dve, p4, t)
                scales(0, t, psF[:], DIM, al[:], w127[:, 0:2])
                if not first:
                    to_int(1, t - 1, q2[:], mag2[:])
                to_int(0, t, q1[:], mag1[:])
                if not last:
                    low_o(t + 1)
                if not first:
                    result(t - 1)
                hidden(t)

            tiles(dve, body)
            t = TILES - 1
            rotate4(t)
            keep(t)
            for n in range(NB):
                low_hT(t, n)
            back_scales(t)
            to_int(1, t, q2[:], mag2[:])
            result(t)


def kernel(x, ctx_1024, L0_xattn_Wq, L0_xattn_Wk, L0_xattn_Wv, L0_xattn_Wo, L0_xattn_gq, L0_xattn_gk,
           L0_ffn_w_gate, L0_ffn_w_up, L0_ffn_w_down):
    import numpy as np
    import concourse.bacc as bacc
    from concourse.bass_utils import run_bass_kernel_spmd

    x2 = np.asarray(x).reshape(T, DIM)
    ctx = np.asarray(ctx_1024)
    rows = lambda w: np.asarray(w).T.reshape(4, P, FF)
    down = np.asarray(L0_ffn_w_down).T.reshape(4, 4, P, DIM).transpose(0, 2, 1, 3).reshape(4, P, FF)
    had = np.ones((1, 1), np.float32)
    while had.shape[0] < DIM:
        had = np.block([[had, had], [had, -had]])
    arrays = {
        "x": x2, "ctxT": ctx.transpose(0, 2, 1), "ctx_k": ctx, "wq": L0_xattn_Wq, "wk": L0_xattn_Wk, "wv": L0_xattn_Wv,
        "wo": L0_xattn_Wo, "gq": L0_xattn_gq, "gk": L0_xattn_gk,
        "w_ff": np.stack([rows(L0_ffn_w_gate), rows(L0_ffn_w_up), down]),
        "ident": np.eye(P, dtype=np.float32), "had": had,
    }
    arrays = {"in_" + k: np.ascontiguousarray(v) for k, v in arrays.items()}
    nc = bacc.Bacc("TRN2", target_bir_lowering=False, num_devices=1)
    args = [nc.dram_tensor(k, a.shape, F32, kind="ExternalInput").ap() for k, a in arrays.items()]
    out = nc.dram_tensor("out", [T, DIM], F32, kind="ExternalOutput").ap()
    build(nc, *args, out)
    r = run_bass_kernel_spmd(nc, [arrays], core_ids=[0])
    return r.results[0]["out"].reshape(B, SQ, DIM)
```

```python
import concourse.bass as bass
from concourse import mybir
from contextlib import ExitStack

F32 = mybir.dt.float32
F32R = mybir.dt.float32r
BF16 = mybir.dt.bfloat16
FP8 = mybir.dt.float8e4
ALU = mybir.AluOpType
ACT = mybir.ActivationFunctionType
AX = mybir.AxisListType

P = 128
B, SQ, DIM = 16, 100, 512
SK, CD = 361, 256
H, D = 16, 128
INNER = H * D
FF = 2048
T = B * SQ
EPS = 1e-5
SKR = 19
SKP = SK + 1
DC, CC, FC = DIM // P, CD // P, FF // P
HG = 4
NG = H // HG
KW = [121, 120, 120]
KO = [0, 121, 241]
QS = 4
GB = 4
GT = GB * SQ
G = B // GB
LAST_B = B - 1
MAGIC = 1.5 * 2.0 ** 23
WC = 4
HB, HC = 256, 2
NB = FF // DIM
TT = P
TILES = -(-T // TT)
LAST_TOK = T - TT


def build(nc, x, ctxT, ctx_k, wq, wk, wv, wo, gq, gk, w_ff, ident_in, had_in, out):
    q_dram = nc.dram_tensor("q_dram", [B, D, H, SQ], F32, kind="Internal").ap()
    rk_dram = nc.dram_tensor("rk_dram", [2, HG * SK], F32, kind="Internal").ap()
    o_dram = nc.dram_tensor("o_dram", [H, D, T], F32, kind="Internal").ap()
    wt_dram = nc.dram_tensor("wt_dram", [3 * WC, P, FF // 2], BF16, kind="Internal").ap()
    with ExitStack() as top:
        def sbt(ctx, name, shape, dt=F32):
            return ctx.enter_context(nc.sbuf_tensor(name, shape, dt))

        def sem(name):
            return top.enter_context(nc.semaphore(name))

        d_q = [sem(f"d1_q{i}") for i in range(QS)]
        d_o = [sem(f"d2_o{i}") for i in range(2)]
        d_first = sem("d2_first")
        d_wo = [sem(f"d_wo{i}") for i in range(4)]
        passed = {e: sem(e + "_passed") for e in ("sp", "act", "dve", "pe", "pool")}
        ident = sbt(top, "ident", [P, P])
        rq_all = sbt(top, "rq_all", [SQ, B, H])
        neg_half = sbt(top, "neg_half", [P, 1])
        asums = sbt(top, "asums", [P, 3])
        w127 = sbt(top, "w127", [P, 3])
        o_in = sbt(top, "o_in", [P, H, TT])
        wk_hi = sbt(top, "wk_hi", [P, CC, INNER], F32R)
        wk_lo = sbt(top, "wk_lo", [P, CC, INNER], F32R)
        wo_first = [w[:].rearrange("p c n -> p (c n)").rearrange("p (h n) -> p h n", n=DIM) for w in (wk_hi, wk_lo)]
        with ExitStack() as ctx:
            weights = {
                "wk_hi": wk_hi,
                "wk_lo": wk_lo,
                "wv": sbt(ctx, "wv_sb", [P, CC, INNER]),
                "sel": sbt(ctx, "sel", [P, 2 * P - 1], F32R),
                "cT_in": sbt(ctx, "cT_in", [P, CC, SK]),
                "cK_in": sbt(ctx, "cK_in", [P, 3, CD]),
                "cT_hi": sbt(ctx, "cT_hi", [P, 2, CC, SKP], F32R),
                "cT_lo": sbt(ctx, "cT_lo", [P, 2, CC, SKP], F32R),
                "ones": sbt(ctx, "ones", [P, P]),
            }
            queries(nc, sbt, sem, passed, weights, ident, rq_all, neg_half, asums, d_q, x, wq, wk, wv, gq, gk, w_ff,
                    ctxT, ctx_k, ident_in, q_dram)
            attention(nc, sbt, sem, passed, weights, ident, rq_all, neg_half, asums, w127, d_q, d_o, d_first, ctxT, ctx_k, w_ff,
                      q_dram, rk_dram, o_dram, o_in, wt_dram, wo, d_wo, wo_first)
        feed_forward(nc, sbt, sem, passed, ident, neg_half, w127, o_in, d_o, d_first, x, wo, d_wo, wo_first, had_in, o_dram,
                     wt_dram, out)


def due(count):
    return not isinstance(count, int) or count > 0


def held(eng, value):
    return value if isinstance(value, int) else eng.snap(value)


def apart(eng, passed):
    eng.sem_inc(passed, 1)


def query_factors(nc, rq_all, neg_half, g, part):
    rows = rq_all[:, bass.ds(g * GB, GB), 2 * part:2 * part + 2]
    return nc.gpsimd.tensor_tensor(rows, rows, neg_half[0:SQ, :].unsqueeze(2).to_broadcast([SQ, GB, 2]), op=ALU.pow)


def queries(nc, sbt, sem, passed, weights, ident, rq_all, neg_half, asums, d_q, x, wq, wk, wv, gq, gk, w_ff, ctxT,
            ctx_k, ident_in, q_dram):
    wk_hi, wk_lo, wv_sb, sel = (weights[k] for k in ("wk_hi", "wk_lo", "wv", "sel"))
    cT_in, cT_hi, cT_lo = (weights[k] for k in ("cT_in", "cT_hi", "cT_lo"))
    QW = HG * D
    KWD = INNER // 2
    with ExitStack() as ctx:
        sb = lambda name, shape, dt=F32: sbt(ctx, name, shape, dt)
        s = sem
        wq_hi, wq_lo = sb("wq_hi", [P, DC, INNER], F32R), sb("wq_lo", [P, DC, INNER], F32R)
        stage = sb("stage", [P, 2, DC * QW])
        x_in = sb("x_in", [SQ, GB, DIM])
        xn = sb("xn", [SQ, GB, DIM])
        st, mv = sb("st", [SQ, GB, 6]), sb("mv", [SQ, GB, 2])
        ve, rstd = sb("ve", [SQ, GB]), sb("rstd", [SQ, GB])
        xT_hi, xT_lo = sb("xT_hi", [P, DC, GT], F32R), sb("xT_lo", [P, DC, GT], F32R)
        gqk, gk_sb = sb("gqk", [P, 1]), sb("gk_sb", [P, 1])
        gprod = sb("gprod", [P, 1])
        asum = sb("asum", [P, 2 * WC])
        warm = sb("warm", [P, 1])
        q_out = sb("q_out", [P, QS, GT])
        sq = sb("sq1", [P, 2, GT])
        sq_hi, sq_lo = sb("sq1_hi", [P, 2, GT], F32R), sb("sq1_lo", [P, 2, GT], F32R)
        ms = sb("ms1", [H, GT])
        psQ = [ctx.enter_context(nc.psum_tensor(f"psQ{i}", [P, 512], F32)) for i in range(2)]
        psX = [ctx.enter_context(nc.psum_tensor(f"psX{c}", [P, 512], F32)) for c in range(DC)]
        psS = ctx.enter_context(nc.psum_tensor("psS1", [P, 512], F32))
        psR = ctx.enter_context(nc.psum_tensor("psR", [P, GB, H], F32))

        d_x = [s(f"d1_x{b}") for b in range(GB)]
        d_g, d_id, d_wv, d_c, d_cK = s("d1_g"), s("d1_id"), s("d1_wv"), s("d1_c"), s("d1_cK")
        a_c = s("a1_c")
        d_st = [s("d1_st0"), s("d1_st1")]
        g_const, g_rstd, g_rq = s("g1_const"), s("g1_rstd"), s("g1_rq")
        v_gain, v_stat, v_agg, v_ve, v_xn = s("v1_gain"), s("v1_stat"), s("v1_agg"), s("v1_ve"), s("v1_xn")
        a_first, v_first, a_whi, v_asum = s("a1_first"), s("v1_first"), s("a1_whi"), s("v1_asum")
        used = [s("used1_0"), s("used1_1")]
        p_xT, p_read, a_xhi, v_xlo = s("p1_xT"), s("p1_read"), s("a1_xhi"), s("v1_xlo")
        p_q, a_q, v_sqhi, g_sqlo = s("p1_q"), s("a1_q"), s("v1_sqhi"), s("g1_sqlo")
        p_ss, v_ms, p_rq, v_rq = s("p1_ss"), s("v1_ms"), s("p1_rq"), s("v1_rq")

        pieces = []
        for j in range(4):
            cols = slice(j * QW, (j + 1) * QW)
            pieces.append((wq.rearrange("(c p) n -> p c n", p=P)[:, :, cols], wq_hi[:, :, cols], wq_lo[:, :, cols]))
        for j in range(2):
            cols = slice(j * KWD, (j + 1) * KWD)
            pieces.append((wk.rearrange("(c p) n -> p c n", p=P)[:, :, cols], wk_hi[:, :, cols], wk_lo[:, :, cols]))

        halves = [slice(k * QW // 2, (k + 1) * QW // 2) for k in range(2)]

        def staged(i):
            c = pieces[i][1].shape[1]
            return stage[:, i % 2, :].rearrange("p (c n) -> p c n", c=c)

        SPLIT_AT = {0: 1, 2: 2, 4: 3, 8: 4, 10: 5}

        sp_passed, pe_passed, dve_passed = (passed[e] for e in ("sp", "pe", "dve"))
        LOAD_AT = {0: 0, 3: 1, 7: 2, 10: 3}
        SUM_AT = {4: 0, 5: 1, 7: 2, 8: 3, 10: 4, 11: 5, 13: 6, 14: 7}

        block = ctx.enter_context(nc.Block())

        @block.sync
        def _(sp):
            xg = x.rearrange("(b q) n -> q b n", q=SQ)
            for b in range(GB):
                sp.dma_start(x_in[:, b, :], xg[:, b, :]).then_inc(d_x[b], 16)
            sp.dma_start(ident[:], ident_in).then_inc(d_id, 16)
            sp.dma_start(gqk[:], gq.rearrange("(p a) -> p a", a=1)).then_inc(d_g, 16)
            sp.dma_start(gk_sb[:], gk.rearrange("(p a) -> p a", a=1)).then_inc(d_g, 16)

            def load_piece(i):
                if due(i // 2):
                    sp.wait_ge(used[i % 2], i // 2)
                sp.dma_start(staged(i), pieces[i][0]).then_inc(d_st[i % 2], 16)

            def load_ff(g, c):
                src = w_ff[bass.ds(held(sp, g - 1), 1), c].rearrange("a p n -> p (a n)")
                sp.wait_ge(used[c % 2], held(sp, g * 2 + (1 + c // 2)))
                apart(sp, sp_passed)
                sp.dma_start(stage[:, c % 2, :], src).then_inc(d_st[c % 2], 16)

            for i in range(4):
                load_piece(i)

            def group(g, last):
                for h in range(H):
                    if h == 1 and not last:
                        nxt = held(sp, (g + 1) * GB)
                        sp.wait_ge(v_xn, nxt)
                        for b in range(GB):
                            sp.dma_start(x_in[:, b, :], xg[:, bass.ds(held(sp, nxt + b), 1), :].rearrange("q a n -> q (a n)")
                                         ).then_inc(d_x[b], 16)
                    dst = q_dram[bass.ds(held(sp, g * GB), GB), :, h, :].rearrange("b d q -> d b q")
                    sp.wait_ge(a_q, held(sp, g * H + h + 1))
                    sp.dma_start(dst, q_out[:, h % QS, :].rearrange("p (b q) -> p b q", q=SQ)).then_inc(d_q[h % QS], 16)
                    if isinstance(g, int) and g == 0:
                        if h in (1, 3):
                            load_piece(4 + h // 2)
                        if h == 9:
                            sp.dma_start(wv_sb[:], wv.rearrange("(c p) n -> p c n", p=P)).then_inc(d_wv, 16)
                    elif h in LOAD_AT:
                        load_ff(g, LOAD_AT[h])

            group(0, False)
            with sp.Fori(1, G - 1) as g:
                group(g, False)
            sp.dma_start(weights["cT_in"][:], ctxT[0].rearrange("(c p) k -> p c k", p=P)).then_inc(d_c, 16)
            for i in range(3):
                sp.dma_start(weights["cK_in"][0:KW[i], i, :], ctx_k[0, KO[i]:KO[i] + KW[i], :]).then_inc(d_cK, 16)
            group(G - 1, True)
            sp.wait_ge(d_wv, 16)
            sp.wait_ge(d_c, 16)
            sp.wait_ge(d_cK, 48)

        @block.gpsimd
        def _(pool):
            nc.gpsimd.memset(neg_half[:], -0.5).then_inc(g_const, 1)
            nc.gpsimd.memset(sel[:].bitcast(F32), 0.0).then_inc(g_const, 1)
            pool.wait_ge(g_const, 2)
            nc.gpsimd.memset(sel[:, P - 1:P].bitcast(F32), 1.0).then_inc(g_const, 1)
            nc.gpsimd.memset(weights["ones"][:], 1.0)
            for part in (cT_hi, cT_lo):
                nc.gpsimd.memset(part[:, :, :, SK:SKP].bitcast(F32), 0.0)

            def norm(g):
                pool.wait_ge(v_ve, g + 1)
                nc.gpsimd.tensor_tensor(rstd[:], ve[:], neg_half[0:SQ, :].to_broadcast([SQ, GB]),
                                        op=ALU.pow).then_inc(g_rstd, 1)

            def low_squares(g, h):
                pool.wait_ge(v_sqhi, g * H + h + 1)
                nc.gpsimd.tensor_tensor(sq_lo[:, h % 2, :], sq[:, h % 2, :], sq_hi[:, h % 2, :].bitcast(F32),
                                        op=ALU.subtract).then_inc(g_sqlo, 1)

            def rms(g, part):
                pool.wait_ge(v_rq, g + 1)
                query_factors(nc, rq_all, neg_half, g, part).then_inc(g_rq, 1)

            def group(g, first, last):
                for h in range(H - 2 if last else H):
                    low_squares(g, h)
                    if h == 5 and not last:
                        norm(g + 1)
                    if 6 <= h < 14 and not first:
                        rms(g - 1, h - 6)

            norm(0)
            group(0, True, False)
            with pool.Fori(1, G - 1) as g:
                group(g, False, False)
            group(G - 1, False, True)

        @block.tensor
        def _(pe):
            pe.wait_ge(d_id, 16)
            pe.wait_ge(g_const, 3)

            def transposes(g):
                if due(g * DC):
                    pe.wait_ge(v_xlo, g * DC)
                for b in range(GB):
                    pe.wait_ge(v_xn, g * GB + b + 1)
                    for c in range(DC):
                        last = nc.tensor.transpose(psX[c][:, b * SQ:(b + 1) * SQ], xn[:, b, c * P:(c + 1) * P], ident[0:SQ, 0:SQ])
                    last.then_inc(p_xT, 1)

            def squares(g, h):
                pe.wait_ge(g_sqlo, g * H + h + 1)
                if h == 0:
                    if due(g):
                        pe.wait_ge(v_ms, g)
                for part in (sq_hi, sq_lo):
                    last = nc.tensor.matmul(psS[:, 0:GT], sel[:, P - 1 - h:2 * P - 1 - h], part[:, h % 2, :],
                                            start=(h == 0 and part is sq_hi), stop=(h == H - 1 and part is sq_lo))
                last.then_inc(p_ss, 1)

            def factors(g):
                pe.wait_ge(v_ms, g + 1)
                pe.wait_ge(v_rq, g)
                apart(pe, pe_passed)
                for b in range(GB):
                    last = nc.tensor.transpose(psR[0:SQ, b, :], ms[:, b * SQ:(b + 1) * SQ], ident[0:H, 0:H])
                last.then_inc(p_rq, 1)

            def group(g, first, last_group):
                for h in range(H):
                    if first and h == 0:
                        pe.wait_ge(v_first, 1)
                    elif first and h % HG == 0:
                        pe.wait_ge(used[h // HG % 2], h // HG // 2 + 1)
                    if first and h == 2:
                        pe.wait_ge(used[0], 1)
                    if due(g * H + h - 1):
                        pe.wait_ge(a_q, g * H + h - 1)
                    n = 0
                    for c in range(DC):
                        if h == 0:
                            pe.wait_ge(v_xlo, g * DC + c + 1)
                            apart(pe, pe_passed)
                        for w, m in ((wq_hi, xT_hi), (wq_hi, xT_lo), (wq_lo, xT_hi)):
                            last = nc.tensor.matmul(psQ[h % 2][:, 0:GT], w[:, c, h * D:(h + 1) * D], m[:, c, :],
                                                    start=(n == 0), stop=(n == 3 * DC - 1))
                            n += 1
                        if h == H - 1 and c < DC - 1:
                            last.then_inc(p_read, 1)
                    last.then_inc(p_q, 1)
                    if h >= 2:
                        squares(g, h - 2)
                    elif not first:
                        squares(g - 1, H - 2 + h)
                    if h == 4 and not first:
                        factors(g - 1)
                    if h == 10 and not last_group:
                        transposes(g + 1)

            transposes(0)
            group(0, True, False)
            with pe.Fori(1, G - 1) as g:
                group(g, False, False)
            group(G - 1, False, True)
            squares(G - 1, H - 2)
            squares(G - 1, H - 1)
            factors(G - 1)

        @block.scalar
        def _(act):
            act.wait_ge(g_const, 1)
            nc.scalar.activation(warm[:], neg_half[:], ACT.Copy)
            act.wait_ge(v_gain, 1)

            def split(i):
                act.wait_ge(d_st[i % 2], 16 * (i // 2 + 1))
                nc.scalar.activation(pieces[i][1], staged(i), ACT.Copy).then_inc(a_whi, 1)

            def split_first(k):
                act.wait_ge(d_st[0], 16)
                nc.scalar.activation(pieces[0][1][:, :, halves[k]], staged(0)[:, :, halves[k]], ACT.Copy).then_inc((a_first, a_whi)[k], 1)

            def sum_ff(g, i):
                c, k = i // 2, i % 2
                if k == 0:
                    act.wait_ge(d_st[c % 2], g * 32 + (c // 2 * 16 + 32))
                if i == 0:
                    act.wait_ge(v_asum, g)
                half = stage[:, c % 2, k * FF // 2:(k + 1) * FF // 2]
                total = nc.scalar.activation(half, half, ACT.Abs, accum_out=asum[:, i:i + 1])
                if k == 1:
                    total.then_inc(used[c % 2], 1)

            def high_xT(g):
                act.wait_ge(p_xT, g * GB + GB)
                for c in range(DC):
                    if c < DC - 1:
                        if due((g - 1) * (DC - 1) + c + 1):
                            act.wait_ge(p_read, (g - 1) * (DC - 1) + c + 1)
                    else:
                        if due(g * H):
                            act.wait_ge(p_q, g * H)
                    nc.scalar.activation(xT_hi[:, c, :], psX[c][:, 0:GT], ACT.Copy).then_inc(a_xhi, 1)

            def group(g, first, last):
                for h in range(H):
                    if h == H - 1 and not last:
                        high_xT(g + 1)
                    if first and h in SPLIT_AT:
                        split(SPLIT_AT[h])
                    if not first and h in SUM_AT:
                        sum_ff(g, SUM_AT[h])
                    act.wait_ge(p_q, g * H + h + 1)
                    if due(g * (H // QS * 16) + h // QS * 16):
                        act.wait_ge(d_q[h % QS], g * (H // QS * 16) + h // QS * 16)
                    nc.scalar.activation(q_out[:, h % QS, :], psQ[h % 2][:, 0:GT], ACT.Copy, scale=gprod[:])
                    if due(g * H + h - 1):
                        act.wait_ge(g_sqlo, g * H + h - 1)
                    nc.scalar.activation(sq[:, h % 2, :], psQ[h % 2][:, 0:GT], ACT.Square).then_inc(a_q, 1)

            split_first(0)
            high_xT(0)
            split_first(1)
            group(0, True, False)
            with act.Fori(1, G - 1) as g:
                group(g, False, False)
            group(G - 1, False, True)
            act.wait_ge(d_c, 16)
            nc.scalar.activation(cT_hi[:, 0, :, 0:SK], cT_in[:], ACT.Copy).then_inc(a_c, 1)

        @block.vector
        def _(dve):

            def split(i):
                dve.wait_ge(a_whi, i + 1)
                nc.vector.tensor_tensor(pieces[i][2], staged(i), pieces[i][1].bitcast(F32),
                                        ALU.subtract).then_inc(used[i % 2], 1)

            def split_first(k):
                dve.wait_ge((a_first, a_whi)[k], 1)
                nc.vector.tensor_tensor(pieces[0][2][:, :, halves[k]], staged(0)[:, :, halves[k]],
                                              pieces[0][1][:, :, halves[k]].bitcast(F32), ALU.subtract).then_inc((v_first, used[0])[k], 1)

            def sum_pieces(g):
                for i in range(2):
                    dve.wait_ge(used[i], g * 2 + 3)
                nc.vector.tensor_reduce(asums[:, bass.ds(g - 1, 1)], asum[:], axis=AX.X, op=ALU.add).then_inc(v_asum, 1)

            def statistics(g, batches):
                for b in batches:
                    dve.wait_ge(d_x[b], (g + 1) * 16)
                    nc.vector.bn_stats(st[:, b, :], x_in[:, b, :]).then_inc(v_stat, 1)
                for b in batches:
                    dve.wait_ge(v_stat, g * GB + b + 1)
                    apart(dve, dve_passed)
                    nc.vector.bn_aggr(mv[:, b, :], st[:, b, :]).then_inc(v_agg, 1)
                if GB - 1 in batches:
                    dve.wait_ge(v_agg, (g + 1) * GB)
                    nc.vector.tensor_scalar(ve[:], mv[:, :, 1], EPS, None, ALU.add).then_inc(v_ve, 1)

            def norm(g, batches):
                dve.wait_ge(g_rstd, g + 1)
                for b in batches:
                    if due((g - 1) * GB + b + 1):
                        dve.wait_ge(p_xT, (g - 1) * GB + b + 1)
                    nc.vector.tensor_scalar(xn[:, b, :], x_in[:, b, :], mv[:, b, 0:1], rstd[:, b:b + 1],
                                            ALU.subtract, ALU.mult).then_inc(v_xn, 1)

            def factors(g):
                dve.wait_ge(p_rq, g + 1)
                nc.vector.tensor_copy(rq_all[:, bass.ds(g * GB, GB), :], psR[0:SQ, :, :]).then_inc(v_rq, 1)

            def mean_squares(g):
                dve.wait_ge(p_ss, (g + 1) * H)
                dve.wait_ge(p_rq, g)
                nc.vector.tensor_scalar(ms[:], psS[0:H, 0:GT], D * EPS, None, ALU.add).then_inc(v_ms, 1)

            def low_xT(g):
                for c in range(DC):
                    dve.wait_ge(a_xhi, g * DC + c + 1)
                    nc.vector.tensor_tensor(xT_lo[:, c, :], psX[c][:, 0:GT],
                                            xT_hi[:, c, :].bitcast(F32),
                                            ALU.subtract).then_inc(v_xlo, 1)

            def group(g, first, last):
                for h in range(H):
                    if h == H - 1 and not last:
                        low_xT(g + 1)
                    if first and h in SPLIT_AT:
                        split(SPLIT_AT[h])
                    if not last:
                        if h in (3, 4):
                            statistics(g + 1, range(2 * (h - 3), 2 * (h - 3) + 2))
                        if h in (7, 8):
                            norm(g + 1, range(2 * (h - 7), 2 * (h - 7) + 2))
                    dve.wait_ge(a_q, g * H + h + 1)
                    if due(g * H + h - 1):
                        dve.wait_ge(p_ss, g * H + h - 1)
                    nc.vector.tensor_copy(sq_hi[:, h % 2, :], sq[:, h % 2, :]).then_inc(v_sqhi, 1)
                    if last and h >= H - 2:
                        dve.wait_ge(v_sqhi, g * H + h + 1)
                        dve.wait_ge(g_sqlo, g * H + H - 2)
                        nc.vector.tensor_tensor(sq_lo[:, h % 2, :], sq[:, h % 2, :], sq_hi[:, h % 2, :].bitcast(F32),
                                                ALU.subtract).then_inc(g_sqlo, 1)
                    if h == 1 and not first:
                        mean_squares(g - 1)
                    if h == 5 and not first:
                        factors(g - 1)
                if not first and not last:
                    sum_pieces(g)

            nc.vector.memset(asums[:], 0.0).then_inc(v_asum, 1)
            statistics(0, range(GB))
            dve.wait_ge(d_g, 32)
            nc.vector.tensor_tensor(gprod[:], gqk[:], gk_sb[:], ALU.mult).then_inc(v_gain, 1)
            norm(0, range(GB))
            split_first(0)
            low_xT(0)
            split_first(1)
            group(0, True, False)
            with dve.Fori(1, G - 1) as g:
                group(g, False, False)
            group(G - 1, False, True)
            dve.wait_ge(a_c, 1)
            nc.vector.tensor_tensor(cT_lo[:, 0, :, 0:SK], cT_in[:], cT_hi[:, 0, :, 0:SK].bitcast(F32), ALU.subtract)
            mean_squares(G - 1)
            sum_pieces(G - 1)
            factors(G - 1)


def attention(nc, sbt, sem, passed, weights, ident, rq_all, neg_half, asums, w127, d_stored, d_o, d_first, ctxT, ctx_k, w_ff,
              q_dram, rk_dram, o_dram, o_in, wt_dram, wo, d_wo, wo_first):
    wk_hi, wk_lo, wv_sb, sel = (weights[k] for k in ("wk_hi", "wk_lo", "wv", "sel"))
    UQ = HG * SQ
    LEAD = 11
    HEADS, UNITS = B * H, B * NG
    CHUNKS = 3 * WC * FF // DIM
    with ExitStack() as ctx:
        sb = lambda name, shape, dt=F32: sbt(ctx, name, shape, dt)
        s = sem
        cT_in, cK_in = weights["cT_in"], weights["cK_in"]
        cT_hi, cT_lo, ones = (weights[k] for k in ("cT_hi", "cT_lo", "ones"))
        cK_hi, cK_lo = sb("cK_hi", [P, 2, 3, CD], F32R), sb("cK_lo", [P, 2, 3, CD], F32R)
        q_in = sb("q_in", [P, 2, UQ])
        q_hi, q_lo = sb("q_hi", [P, 2, UQ], F32R), sb("q_lo", [P, 2, UQ], F32R)
        rq = sb("rq", [SQ, 2, HG])
        k_hi, k_lo = sb("k_hi", [P, NG, HG, SKP], F32R), sb("k_lo", [P, NG, HG, SKP], F32R)
        sq = sb("sq2", [P, 2, SKP])
        sq_hi, sq_lo = sb("sq2_hi", [P, 2, SKP], F32R), sb("sq2_lo", [P, 2, SKP], F32R)
        ms = sb("ms2", [HG, SK])
        ms_sp, rk_sp = sb("ms_sp", [HG * SKR, SK // SKR]), sb("rk_sp", [HG * SKR, SK // SKR])
        rk = sb("rk", [SQ, 2, HG, SK])
        sc = sb("sc", [SQ, 2, SK])
        mx, nb, rs, ri = (sb(n, [SQ, 2]) for n in ("mx", "nb", "rs", "ri"))
        ex, pr = sb("ex", [SQ, 2, SK]), sb("pr", [SQ, 2, SK])
        pT_hi, pT_lo = sb("pT_hi", [P, 2, 3, UQ], F32R), sb("pT_lo", [P, 2, 3, UQ], F32R)
        z = sb("z", [P, CC, UQ])
        o = sb("o", [P, 2, UQ])
        wsc = sb("wsc", [P, 3])
        bounds = sb("bounds", [P, 3 * WC, 2])
        bound = sb("bound", [P, 2])
        w_in, below = sb("w_in", [P, 2, DIM]), sb("below", [P, DIM], BF16)
        w_out = sb("w_out", [P, 2, DIM], FP8)
        psK = [ctx.enter_context(nc.psum_tensor(f"psK{i}", [P, 512], F32)) for i in range(2)]
        psN = ctx.enter_context(nc.psum_tensor("psN", [P, 512], F32))
        psS = ctx.enter_context(nc.psum_tensor("psS2", [P, 512], F32))
        psP = ctx.enter_context(nc.psum_tensor("psP", [P, 512], F32))
        psZ = [ctx.enter_context(nc.psum_tensor(f"psZ{i}", [P, 512], F32)) for i in range(CC)]
        psV = ctx.enter_context(nc.psum_tensor("psV", [P, 512], F32))

        d_cT, d_cK, d_ms, d_rs = s("d2_cT"), s("d2_cK"), s("d2_ms"), s("d2_rs")
        d_q, d_rb = ([s(f"d2_{n}{i}") for i in range(2)] for n in ("q", "rb"))
        a_cT, v_cT, a_cK, v_cK, v_zero = s("a2_cT"), s("v2_cT"), s("a2_cK"), s("v2_cK"), s("v2_zero")
        a_q, v_q, v_rq = s("a2_q"), s("v2_q"), s("v2_rq")
        p_k, a_k, v_klo, v_sqhi, g_sqlo = s("p2_k"), s("a2_k"), s("v2_klo"), s("v2_sqhi"), s("g2_sqlo")
        p_ss, v_ms, g_rk, g_rq = s("p2_ss"), s("v2_ms"), s("g2_rk"), s("g2_rq")
        p_s, v_max, v_nb, a_ex, v_ri, a_pr = s("p2_s"), s("v2_max"), s("v2_nb"), s("a2_ex"), s("v2_ri"), s("a2_pr")
        p_t, a_pT, v_pT = s("p2_t"), s("a2_pT"), s("v2_pT")
        p_z, a_z, v_z, p_v, a_o = s("p2_z"), s("a2_z"), s("v2_z"), s("p2_v"), s("a2_o")
        p_sum, v_mean, v_bounds, v_bound = (s(n) for n in ("p2_sum", "v2_mean", "v2_bounds", "v2_bound"))
        v_below, v_wt = s("v2_below"), s("v2_wt")
        wo_slots = [w_in[:, 0, :], w_in[:, 1, :], cT_in[:].rearrange("p c k -> p (c k)")[:, 0:DIM],
                    cK_in[:].rearrange("p i c -> p (i c)")[:, 0:DIM]]
        WO_AT = {(UNITS - 2 + i // HG, i % HG): i for i in range(H // 2)}
        g_whi, g_wlo = s("g2_whi"), s("g2_wlo")
        d_w, d_wt = ([s(f"d2_{n}{i}") for i in range(2)] for n in ("w", "wt"))
        sp_passed, act_passed, dve_passed = (passed[e] for e in ("sp", "act", "dve"))

        def real(i, count):
            return not isinstance(i, int) or 0 <= i < count

        def pipeline(eng, unit):
            def batch(b, par):
                for j in range(NG):
                    unit(b * NG + j, b, j, par)

            for b in range(-1, 4):
                batch(b, b % 2)
            with eng.Fori(2, B // 2 - 1) as pair:
                batch(pair * 2, 0)
                batch(pair * 2 + 1, 1)
            batch(B - 2, 0)
            batch(B - 1, 1)
            for j in range(2):
                unit(UNITS + j, B, j, 0)

        def early(m):
            return isinstance(m, int) and m < LEAD - 1

        def first_batch(b):
            return isinstance(b, int) and b == 0

        def ahead(j, h):
            return divmod((j * HG + h) % H, HG)

        block = ctx.enter_context(nc.Block())

        @block.sync
        def _(sp):
            def load_q(u, b, j):
                src = q_dram[bass.ds(held(sp, b), 1), :, j * HG:(j + 1) * HG, :].rearrange("a d h q -> d (a h) q")
                if due(held(sp, u - 1)):
                    sp.wait_ge(v_q, held(sp, u - 1))
                sp.dma_start(q_in[:, j % 2, :].rearrange("p (h q) -> p h q", q=SQ), src).then_inc(d_q[j % 2], 16)

            def load_cT(b):
                b = held(sp, b)
                src = ctxT[bass.ds(b, 1)].rearrange("a (c p) k -> p (a c) k", p=P)
                if due(b - 1):
                    sp.wait_ge(v_cT, b - 1)
                sp.dma_start(cT_in[:], src).then_inc(d_cT, 16)

            def load_cK(b):
                b = held(sp, b)
                src = [ctx_k[bass.ds(b, 1), KO[i]:KO[i] + KW[i], :].rearrange("a k c -> k (a c)") for i in range(3)]
                sp.wait_ge(v_cK, b)
                for i in range(3):
                    sp.dma_start(cK_in[0:KW[i], i, :], src[i]).then_inc(d_cK, 16)

            def spread_rk(u, slot):
                done = held(sp, u + 1)
                powers = held(sp, u * 2 + 2)
                stored = held(sp, u * 16 + 16)
                used = held(sp, u * HG - HG)
                sp.wait_ge(v_ms, done)
                sp.dma_start(ms_sp[:], ms[:].rearrange("h (i k) -> h i k", i=SKR)).then_inc(d_ms, 16)
                sp.wait_ge(g_rk, powers)
                sp.dma_start(rk_dram[slot, :].rearrange("(i k) -> i k", i=HG * SKR), rk_sp[:]).then_inc(d_rs, 16)
                sp.wait_ge(d_rs, stored)
                if due(used):
                    sp.wait_ge(v_max, used)
                sp.dma_start(rk[:, slot, :, :].rearrange("p h k -> p (h k)"),
                             rk_dram[slot:slot + 1, :].to_broadcast([SQ, HG * SK])).then_inc(d_rb[slot], 16)

            def store_o(u, b, j):
                tok = held(sp, b * SQ)
                dst = o_dram[j * HG:(j + 1) * HG, :, bass.ds(tok, SQ)].rearrange("h d t -> d h t")
                sp.wait_ge(a_o, held(sp, u + 1))
                apart(sp, sp_passed)
                sp.dma_start(dst, o[:, j % 2, :].rearrange("p (h q) -> p h q", q=SQ)).then_inc(d_o[j % 2], 16)

            def unit(u, b, j, par):
                if j == 0 and real(b, B - 1):
                    load_cK(b + 1)
                if j == 1 and real(b + 2, B):
                    load_cT(b + 2)
                if isinstance(u, int) and u == -2:
                    for i in range(QS):
                        sp.wait_ge(d_stored[i], 16 * G * H // QS)
                if isinstance(u, int) and u == UNITS - 4:
                    for i in range(2):
                        sp.wait_ge(d_o[i], 16 * NG)
                    sp.dma_start(o_in[:], o_dram[:, :, 0:TT].rearrange("h d t -> d h t")).then_inc(d_first, 16)
                if real(u + 2, UNITS):
                    load_q(u + 2, b + (j + 2) // NG, (j + 2) % NG)
                    spread_rk(u + 2, j % 2)
                if real(u - 2, UNITS):
                    store_o(u - 2, b + (j - 2) // NG, (j - 2) % NG)
                if real(u - 8, CHUNKS):
                    store_w(u - 8, b - 2, j)
                if isinstance(u, int) and u == UNITS - 4:
                    sp.wait_ge(v_wt, CHUNKS)
                    sp.wait_ge(v_cT, B - 1)
                    sp.wait_ge(v_cK, B)
                    for i in range(4):
                        sp.dma_start(wo_slots[i], wo[i * D:(i + 1) * D, :]).then_inc(d_wo[i], 16)
                if isinstance(u, int) and u == UNITS - 2:
                    for i in range(4):
                        sp.wait_ge(g_wlo, i + 1)
                        sp.dma_start(wo_slots[i], wo[(i + 4) * D:(i + 5) * D, :]).then_inc(d_wo[i], 16)

            def store_w(k, piece, j):
                cols = slice(j * DIM // 2, (j + 1) * DIM // 2)
                dst = wt_dram[bass.ds(held(sp, piece), 1), :, cols].rearrange("a p n -> p (a n)")
                sp.wait_ge(v_wt, held(sp, k + 1))
                apart(sp, sp_passed)
                sp.dma_start(dst, w_out[:, j % 2, :].bitcast(BF16)).then_inc(d_wt[j % 2], 16)

            pipeline(sp, unit)
            for i in range(2):
                sp.wait_ge(d_wt[i], 16 * CHUNKS // 2)

        @block.gpsimd
        def _(pool):
            def low_squares(m, h):
                pool.wait_ge(v_sqhi, m + 1)
                nc.gpsimd.tensor_tensor(sq_lo[:, h % 2, :], sq[:, h % 2, :], sq_hi[:, h % 2, :].bitcast(F32),
                                        op=ALU.subtract).then_inc(g_sqlo, 1)

            def rms(u, part):
                if part == 0:
                    pool.wait_ge(d_ms, u * 16 + 16)
                    if due(u * 16):
                        pool.wait_ge(d_rs, u * 16)
                cols = slice(0, SKR // 2 + 1) if part == 0 else slice(SKR // 2 + 1, SK // SKR)
                n = cols.stop - cols.start
                nc.gpsimd.tensor_tensor(rk_sp[:, cols], ms_sp[:, cols], neg_half[0:HG * SKR, :].to_broadcast([HG * SKR, n]),
                                        op=ALU.pow).then_inc(g_rk, 1)

            def split_wo(i):
                pool.wait_ge(p_k, HEADS)
                pool.wait_ge(d_wo[i % 4], 16 * (i // 4 + 1))
                nc.gpsimd.tensor_copy(wo_first[0][:, i, :], wo_slots[i % 4]).then_inc(g_whi, 1)
                pool.wait_ge(g_whi, i + 1)
                nc.gpsimd.tensor_tensor(wo_first[1][:, i, :], wo_slots[i % 4], wo_first[0][:, i, :].bitcast(F32),
                                        op=ALU.subtract).then_inc(g_wlo, 1)

            def unit(u, b, j, par):
                for h in range(HG):
                    m = u * HG + h + LEAD
                    if real(m - 1, HEADS) and not early(m - 1):
                        low_squares(m - 1, (h + LEAD - 1) % HG)
                    if h == 0 and real(u + 1, UNITS):
                        rms(u + 1, 1)
                    if h == 3 and real(u + 2, UNITS):
                        rms(u + 2, 0)
                    if h == 1 and isinstance(u, int) and 0 <= u < H // 2:
                        query_factors(nc, rq_all, neg_half, G - 1, u).then_inc(g_rq, 1)
                    if isinstance(u, int) and (u, h) in WO_AT:
                        split_wo(WO_AT[u, h])

            pipeline(pool, unit)

        @block.tensor
        def _(pe):
            def keys(m, j, h, slot):
                if due(m - 1):
                    pe.wait_ge(v_klo, m - 1)
                n = 0
                for c in range(CC):
                    col = (j * HG + h) * D
                    for w, x in ((wk_hi, cT_hi), (wk_hi, cT_lo), (wk_lo, cT_hi)):
                        last = nc.tensor.matmul(psK[h % 2][:, 0:SKP], w[:, c, col:col + D], x[:, slot, c, :],
                                                start=(n == 0), stop=(n == 3 * CC - 1))
                        n += 1
                last.then_inc(p_k, 1)

            def squares(m, h, v_ms_count):
                pe.wait_ge(g_sqlo, m + 1)
                if h == 0:
                    if due(v_ms_count):
                        pe.wait_ge(v_ms, v_ms_count)
                for part in (sq_hi, sq_lo):
                    last = nc.tensor.matmul(psN[:, 0:SKP], sel[:, P - 1 - h:2 * P - 1 - h], part[:, h % 2, :],
                                            start=(h == 0 and part is sq_hi), stop=(h == HG - 1 and part is sq_lo))
                last.then_inc(p_ss, 1)

            def scores(n, u, j, h):
                if h == 0:
                    pe.wait_ge(v_q, u + 1)
                pe.wait_ge(v_klo, n + 1)
                if due(n):
                    pe.wait_ge(v_max, n)
                cols = slice(h * SQ, (h + 1) * SQ)
                for i, (w, x) in enumerate(((q_hi, k_hi), (q_hi, k_lo), (q_lo, k_hi))):
                    last = nc.tensor.matmul(psS[0:SQ, 0:SKP], w[:, j % 2, cols], x[:, j, h, :],
                                            start=(i == 0), stop=(i == 2))
                last.then_inc(p_s, 1)

            def transposes(n, h):
                pe.wait_ge(a_pr, n + 1)
                if due(n):
                    pe.wait_ge(v_pT, n)
                if isinstance(n, int) and n == 0:
                    pe.wait_ge(v_zero, 1)
                for i in range(3):
                    last = nc.tensor.transpose(psP[0:KW[i], i * SQ:(i + 1) * SQ],
                                               pr[:, h % 2, KO[i]:KO[i] + KW[i]], ident[0:SQ, 0:SQ])
                last.then_inc(p_t, 1)

            def gather(u, j, slot, c):
                pe.wait_ge(v_pT, u * HG + HG)
                if due(u):
                    pe.wait_ge(v_z if c else a_z, u)
                n = 0
                for i in range(3):
                    for w, x in ((cK_hi, pT_hi), (cK_hi, pT_lo), (cK_lo, pT_hi)):
                        last = nc.tensor.matmul(psZ[c][:, 0:UQ], w[0:KW[i], slot, i, c * P:(c + 1) * P],
                                                x[0:KW[i], j % 2, i, :], start=(n == 0), stop=(n == 8))
                        n += 1
                last.then_inc(p_z, 1)

            def values(u, j, heads):
                for h in heads:
                    if h == 0:
                        pe.wait_ge(a_z, u + 1)
                        pe.wait_ge(v_z, u + 1)
                        if due(u):
                            pe.wait_ge(a_o, u)
                    col = (j * HG + h) * D
                    for c in range(CC):
                        last = nc.tensor.matmul(psV[:, h * SQ:(h + 1) * SQ], wv_sb[:, c, col:col + D],
                                                z[:, c, h * SQ:(h + 1) * SQ], start=(c == 0), stop=(c == CC - 1))
                    if h == HG - 1:
                        last.then_inc(p_v, 1)

            def unit(u, b, j, par):
                for h in range(HG):
                    n = u * HG + h
                    m = n + LEAD
                    if real(n, HEADS):
                        scores(n, u, j, h)
                    if real(m, HEADS):
                        jm, hm = ahead(j, h + LEAD)
                        if jm == 0 and hm == 0:
                            if due(b + 1):
                                pe.wait_ge(v_cT, b + 1)
                        keys(m, jm, hm, 1 - par if j * HG + h + LEAD >= H else par)
                    if real(m - 2, HEADS):
                        hs = (h + LEAD - 2) % HG
                        squares(m - 2, hs, u + (h + LEAD - 2) // HG)
                    if real(n - 2, HEADS):
                        transposes(n - 2, (h - 2) % HG)
                    if h < 2 and real(u - 2, UNITS):
                        values(u - 2, (j - 2) % NG, (2 * h, 2 * h + 1))
                    if h >= 2 and real(u - 1, UNITS):
                        if j == 1 and h == 2:
                            pe.wait_ge(v_cK, b + 1)
                        gather(u - 1, (j - 1) % NG, par if j else 1 - par, h - 2)

            nc.tensor.matmul(psV[:, 0:3], ones[:], asums[:], start=True, stop=True).then_inc(p_sum, 1)
            pipeline(pe, unit)

        @block.scalar
        def _(act):
            def high_cT(b, slot):
                act.wait_ge(d_cT, b * 16)
                if due(b * H - H):
                    act.wait_ge(p_k, b * H - H)
                nc.scalar.activation(cT_hi[:, slot, :, 0:SK], cT_in[:], ACT.Copy).then_inc(a_cT, 1)

            def high_cK(b, slot):
                if due(b * 48):
                    act.wait_ge(d_cK, b * 48)
                if due((b - 1) * NG * CC):
                    act.wait_ge(p_z, (b - 1) * NG * CC)
                for i in range(3):
                    nc.scalar.activation(cK_hi[0:KW[i], slot, i, :], cK_in[0:KW[i], i, :], ACT.Copy).then_inc(a_cK, 1)

            def high_q(u, count, j):
                act.wait_ge(d_q[j % 2], count)
                if due(u * HG - HG):
                    act.wait_ge(p_s, u * HG - HG)
                nc.scalar.activation(q_hi[:, j % 2, :], q_in[:, j % 2, :], ACT.Copy).then_inc(a_q, 1)

            def high_k(m, j, h):
                act.wait_ge(p_k, m + 1)
                if due(m - H + 1):
                    act.wait_ge(p_s, m - H + 1)
                nc.scalar.activation(k_hi[:, j, h, :], psK[h % 2][:, 0:SKP], ACT.Copy)

            def square_k(m, h):
                if due(m - 1):
                    act.wait_ge(g_sqlo, m - 1)
                nc.scalar.activation(sq[:, h % 2, :], psK[h % 2][:, 0:SKP], ACT.Square).then_inc(a_k, 1)

            def exponential(n, j, h):
                act.wait_ge(v_nb, n + 1)
                if due(n - 1):
                    act.wait_ge(a_pr, n - 1)
                nc.scalar.activation(ex[:, h % 2, :], sc[:, h % 2, :], ACT.Exp, bias=nb[:, h % 2:h % 2 + 1],
                                     scale=rq[:, j % 2, h:h + 1], accum_out=rs[:, h % 2:h % 2 + 1]).then_inc(a_ex, 1)

            def normalise(n, h):
                act.wait_ge(v_ri, n + 1)
                if due(n - 1):
                    act.wait_ge(p_t, n - 1)
                nc.scalar.activation(pr[:, h % 2, :], ex[:, h % 2, :], ACT.Copy, scale=ri[:, h % 2:h % 2 + 1]
                                     ).then_inc(a_pr, 1)

            def high_pT(n, u, j, h):
                act.wait_ge(p_t, n + 1)
                if h == 0:
                    if due((u - 1) * CC):
                        act.wait_ge(p_z, (u - 1) * CC)
                nc.scalar.activation(pT_hi[0:KW[0], j % 2, :, h * SQ:(h + 1) * SQ],
                                     psP[0:KW[0], 0:3 * SQ].rearrange("p (i q) -> p i q", q=SQ),
                                     ACT.Copy).then_inc(a_pT, 1)

            def copy_z(u):
                act.wait_ge(p_z, u * CC + 1)
                if due(u):
                    act.wait_ge(p_v, u)
                nc.scalar.activation(z[:, 0, :], psZ[0][:, 0:UQ], ACT.Copy).then_inc(a_z, 1)

            def copy_o(u, count, j):
                act.wait_ge(p_v, u + 1)
                if due(count):
                    act.wait_ge(d_o[j % 2], count)
                nc.scalar.activation(o[:, j % 2, :], psV[:, 0:UQ], ACT.Copy).then_inc(a_o, 1)

            def load_w(k, piece, j):
                piece = piece if isinstance(piece, int) else act.snap(piece)
                src = w_ff.rearrange("w c p n -> (w c) p n")[bass.ds(piece, 1), :, j * DIM:(j + 1) * DIM]
                if due(k - 1):
                    act.wait_ge(v_wt, k - 1)
                if not isinstance(k, int):
                    apart(act, act_passed)
                act.dma_start(w_in[:, j % 2, :], src.rearrange("a p n -> p (a n)")).then_inc(d_w[j % 2], 16)

            def unit(u, b, j, par):
                if real(u - 8, CHUNKS):
                    load_w(u - 8, b - 2, j)
                for h in range(HG):
                    n = u * HG + h
                    m = n + LEAD
                    jm, hm = ahead(j, h + LEAD)
                    if real(n - 1, HEADS):
                        normalise(n - 1, (h - 1) % HG)
                    if j == 0 and h == 1 and real(b + 1, B) and not first_batch(b + 1):
                        high_cT(b + 1, 1 - par)
                    if j == 2 and h == 0 and real(b + 1, B):
                        high_cK(b + 1, 1 - par)
                    if h == 1 and real(u + 1, UNITS):
                        high_q(u + 1, (b * 2 + (j + 1) // 2 + 1) * 16, (j + 1) % NG)
                    if h == 2 and real(u - 2, UNITS):
                        copy_o(u - 2, (b * 2 + (j - 2) // 2) * 16, (j - 2) % NG)
                    if h == 3 and real(u - 1, UNITS):
                        copy_z(u - 1)
                    if real(m, HEADS):
                        high_k(m, jm, hm)
                    if real(n, HEADS):
                        exponential(n, j, h)
                    if real(m, HEADS):
                        square_k(m, hm)
                    if real(n - 2, HEADS):
                        high_pT(n - 2, u + (h - 2) // HG, (j + (h - 2) // HG) % NG, (h - 2) % HG)

            pipeline(act, unit)

        @block.vector
        def _(dve):
            nc.vector.memset(psP[:], 0.0).then_inc(v_zero, 1)
            dve.wait_ge(p_sum, 1)
            nc.vector.tensor_scalar(wsc[:], psV[:, 0:3], 1.0 / (DIM * FF), EPS, ALU.mult, ALU.max).then_inc(v_mean, 1)
            dve.wait_ge(v_mean, 1)
            for w in range(3):
                for i, factor in enumerate((0.5, -0.5)):
                    nc.vector.tensor_scalar(bounds[:, w * WC:(w + 1) * WC, i], wsc[:, w:w + 1].to_broadcast([P, WC]), factor,
                                            None, ALU.mult).then_inc(v_bounds, 1)
            nc.vector.tensor_scalar(w127[:], wsc[:], 1.0 / 127.0, None, ALU.mult).then_inc(v_bounds, 1)

            def load_bound(piece):
                if isinstance(piece, int):
                    dve.wait_ge(v_bounds, 7)
                nc.vector.tensor_copy(bound[:], bounds[:, bass.ds(piece, 1), :].rearrange("p a i -> p (a i)")
                                      ).then_inc(v_bound, 1)

            def round_w(k, piece, j):
                dve.wait_ge(d_w[j % 2], piece * 32 + (j // 2 * 16 + 16))
                dve.wait_ge(v_bound, piece + 1)
                if due(k):
                    dve.wait_ge(v_wt, k)
                if due(piece * 32 + j // 2 * 16):
                    dve.wait_ge(d_wt[j % 2], piece * 32 + j // 2 * 16)
                nc.vector.tensor_scalar(below[:], w_in[:, j % 2, :], bound[:, 1:2], None, ALU.is_lt).then_inc(v_below, 1)
                dve.wait_ge(v_below, k + 1)
                apart(dve, dve_passed)
                nc.vector.scalar_tensor_tensor(w_out[:, j % 2, :], w_in[:, j % 2, :], bound[:, 0:1], below[:], ALU.is_gt,
                                               ALU.subtract, saturate=False).then_inc(v_wt, 1)

            def low_cT(b, slot):
                dve.wait_ge(a_cT, b)
                nc.vector.tensor_tensor(cT_lo[:, slot, :, 0:SK], cT_in[:], cT_hi[:, slot, :, 0:SK].bitcast(F32),
                                        ALU.subtract).then_inc(v_cT, 1)

            def low_cK(b, slot):
                dve.wait_ge(a_cK, b * 3 + 3)
                for i in range(3):
                    last = nc.vector.tensor_tensor(cK_lo[0:KW[i], slot, i, :], cK_in[0:KW[i], i, :],
                                                   cK_hi[0:KW[i], slot, i, :].bitcast(F32), ALU.subtract)
                last.then_inc(v_cK, 1)

            def low_q(u, b, j):
                dve.wait_ge(a_q, u + 1)
                nc.vector.tensor_tensor(q_lo[:, j % 2, :], q_in[:, j % 2, :], q_hi[:, j % 2, :].bitcast(F32),
                                        ALU.subtract).then_inc(v_q, 1)
                nc.vector.tensor_copy(rq[:, j % 2, :], rq_all[:, bass.ds(b, 1), j * HG:(j + 1) * HG]
                                      .rearrange("p a h -> p (a h)")).then_inc(v_rq, 1)

            def low_k(m, j, h):
                dve.wait_ge(a_k, m + 1)
                nc.vector.tensor_tensor(k_lo[:, j, h, :], psK[h % 2][:, 0:SKP], k_hi[:, j, h, :].bitcast(F32),
                                        ALU.subtract).then_inc(v_klo, 1)

            def high_squares(m, h):
                if due(m - 1):
                    dve.wait_ge(p_ss, m - 1)
                nc.vector.tensor_copy(sq_hi[:, h % 2, :], sq[:, h % 2, :]).then_inc(v_sqhi, 1)
                if early(m):
                    dve.wait_ge(v_sqhi, m + 1)
                    nc.vector.tensor_tensor(sq_lo[:, h % 2, :], sq[:, h % 2, :], sq_hi[:, h % 2, :].bitcast(F32),
                                            ALU.subtract).then_inc(g_sqlo, 1)

            def mean_squares(u):
                dve.wait_ge(p_ss, u * HG + HG)
                if due(u * 16):
                    dve.wait_ge(d_ms, u * 16)
                nc.vector.tensor_scalar(ms[:], psN[0:HG, 0:SK], 1.0 / D, EPS, ALU.mult, ALU.add).then_inc(v_ms, 1)

            def low_pT(n, j, h):
                dve.wait_ge(a_pT, n + 1)
                nc.vector.tensor_tensor(pT_lo[0:KW[0], j % 2, :, h * SQ:(h + 1) * SQ],
                                        psP[0:KW[0], 0:3 * SQ].rearrange("p (i q) -> p i q", q=SQ),
                                        pT_hi[0:KW[0], j % 2, :, h * SQ:(h + 1) * SQ].bitcast(F32),
                                        ALU.subtract).then_inc(v_pT, 1)

            def invert_sum(n, h):
                k = slice(h % 2, h % 2 + 1)
                dve.wait_ge(a_ex, n + 1)
                if due(n - 1):
                    dve.wait_ge(a_pr, n - 1)
                nc.vector.reciprocal(ri[:, k], rs[:, k]).then_inc(v_ri, 1)

            def scale_scores(n, u, b, j, h):
                if h == 0:
                    dve.wait_ge(d_rb[j % 2], (b * 2 + j // 2 + 1) * 16)
                    dve.wait_ge(v_rq, u + 1)
                if due(n - 1):
                    dve.wait_ge(a_ex, n - 1)
                dve.wait_ge(p_s, n + 1)
                apart(dve, dve_passed)
                nc.vector.tensor_tensor_reduce(out=sc[:, h % 2, :], in0=psS[0:SQ, 0:SK], in1=rk[:, j % 2, h, :],
                                               scale=1.0, scalar=-3.0e38, op0=ALU.mult, op1=ALU.max,
                                               accum_out=mx[:, h % 2:h % 2 + 1]).then_inc(v_max, 1)

            def negate_max(n, j, h):
                k = slice(h % 2, h % 2 + 1)
                dve.wait_ge(v_max, n + 1)
                nc.vector.tensor_scalar(nb[:, k], mx[:, k], rq[:, j % 2, h:h + 1], -1.0, ALU.mult,
                                        ALU.mult).then_inc(v_nb, 1)

            def copy_z(u):
                dve.wait_ge(p_z, u * CC + 2)
                if due(u):
                    dve.wait_ge(p_v, u)
                nc.vector.tensor_copy(z[:, 1, :], psZ[1][:, 0:UQ]).then_inc(v_z, 1)

            def unit(u, b, j, par):
                for h in range(HG):
                    n = u * HG + h
                    m = n + LEAD
                    if real(n - 1, HEADS):
                        invert_sum(n - 1, (h - 1) % HG)
                    if h == 3 and real(u + 2, UNITS):
                        mean_squares(u + 2)
                    if real(n - 3, HEADS):
                        low_pT(n - 3, (j + (h - 3) // HG) % NG, (h - 3) % HG)
                    if h == 0 and real(u - 2, UNITS):
                        copy_z(u - 2)
                    if real(n, HEADS):
                        scale_scores(n, u, b, j, h)
                    if real(m - 1, HEADS):
                        low_k(m - 1, *ahead(j, h + LEAD - 1))
                    if real(n, HEADS):
                        negate_max(n, j, h)
                    if real(m - 1, HEADS):
                        high_squares(m - 1, (h + LEAD - 1) % HG)
                    if j == 0 and h == 2 and real(b + 1, B) and not first_batch(b + 1):
                        low_cT(b + 1, 1 - par)
                    if j == 2 and h == 1 and real(b + 1, B):
                        low_cK(b + 1, 1 - par)
                    if h == 2 and real(u + 1, UNITS):
                        low_q(u + 1, b + (j + 1) // NG, (j + 1) % NG)
                    if j == 0 and h == 1 and real(b - 2, 3 * WC):
                        load_bound(b - 2)
                    if h == 3 and real(u - 8, CHUNKS):
                        round_w(u - 8, b - 2, j)

            pipeline(dve, unit)


def feed_forward(nc, sbt, sem, passed, ident, neg_half, w127, o_in, d_stored, d_first, x, wo, d_wo, wo_first, had_in, o_dram,
                 wt_dram, out):
    HF = FF // 2
    with ExitStack() as ctx:
        sb = lambda name, shape, dt=F32: sbt(ctx, name, shape, dt)
        s = sem
        HALF = H // 2
        wo_hi, wo_lo = (sb(n, [P, HALF, DIM], F32R) for n in ("wo_hi", "wo_lo"))
        wt = sb("wt", [P, 3, WC, FF], FP8)
        stage = sb("stage3", [P, 2, FF])
        had = sb("had", [P, HC, HB], F32R)
        o_hi, o_lo = sb("o_hi", [P, H, TT], F32R), sb("o_lo", [P, H, TT], F32R)
        x_in, xn, xr = (sb(n, [P, DIM]) for n in ("x_in3", "xn3", "xr"))
        x1 = sb("x1", [P, 3, DIM])
        st, mv, ve, rstd = sb("st3", [P, 6]), sb("mv3", [P, 2]), sb("ve3", [P, 1]), sb("rstd3", [P, 1])
        xT_hi, xT_lo = sb("xT3_hi", [P, DC, TT], F32R), sb("xT3_lo", [P, DC, TT], F32R)
        mx4 = sb("mx4", [P, NB])
        mx, am, rc, sq = (sb(n, [P, 2]) for n in ("mx3", "am3", "rc3", "sq3"))
        al, ald = sb("al", [P, 2]), sb("ald", [P, 1])
        mag1, mag2 = sb("mag1", [P, DIM]), sb("mag2", [P, FF])
        q1, q1T = sb("q1", [P, DIM], BF16), sb("q1T", [P, DC, TT], BF16)
        q2, q2T = sb("q2", [P, FF], BF16), sb("q2T", [P, FC, TT], BF16)
        sil = sb("sil", [P, 2, DIM])
        hid = stage[:, 0, :].rearrange("p (n j) -> p n j", j=DIM)
        half_rot = stage[:, 1, :].rearrange("p (n j) -> p n j", j=DIM)
        hT_hi, hT_lo = sb("hT_hi", [P, FC, TT], F32R), sb("hT_lo", [P, FC, TT], F32R)
        y = sb("y", [P, DIM])
        ident_b = sb("ident_b", [P, P], BF16)
        warm = sb("warm3", [P, 1])
        psB = ctx.enter_context(nc.psum_tensor("psB", [P, NB, DIM], F32))
        psA = ctx.enter_context(nc.psum_tensor("psA", [P, DIM], F32))
        psF = ctx.enter_context(nc.psum_tensor("psF", [P, DIM], F32))
        psT = [ctx.enter_context(nc.psum_tensor(f"psT{i}", [P, DIM], F32)) for i in range(2)]
        psTb = [t[:].bitcast(BF16) for t in psT]

        d_o, d_x, d_out = s("d3_o"), s("d3_x"), s("d3_out")
        a_w, v_w, d_had, v_had, d_wt, v_ident, g_zero = s("a3_w"), s("v3_w"), s("d3_had"), s("v3_had"), s("d3_wt"), s("v3_ident"), s("g3_zero")
        a_o, v_o, g_o = s("a3_o"), s("v3_o"), s("g3_o")
        p_out, p_xT, p_rx, p_q1T, p_gu, p_hT, p_rh, p_q2T, p_down = (
            s(f"p3_{n}") for n in ("out", "xT", "rx", "q1T", "gu", "hT", "rh", "q2T", "down"))
        v_x1, v_st, v_ag, v_ve, g_rs, v_xn, v_xr = (s(n) for n in ("v3_x1", "v3_st", "v3_ag", "v3_ve", "g3_rs", "v3_xn", "v3_xr"))
        a_xT, v_xT = s("a3_xT"), s("v3_xT")
        v_mx4 = s("v3_mx4")
        v_scale = [s(f"v3_scale{i}") for i in range(2)]
        a_mag, v_q = ([s(f"{n}{i}") for i in range(2)] for n in ("a3_mag", "v3_q"))
        a_q1T, a_q2T, a_sil, v_h, g_pair0, v_pair1, v_r2, g_r2 = (s(n) for n in ("a3_q1T", "a3_q2T", "a3_sil", "v3_h", "g3_pair0", "v3_pair1",
                                                                                  "v3_r2", "g3_r2"))
        a_hT, v_hT, a_y, g_y, g_old = s("a3_hT"), s("v3_hT"), s("a3_y"), s("g3_y"), s("g3_old")

        PIECES = HALF // 2
        wo_v = wo.rearrange("(j h d) n -> j d h n", d=D, h=2)
        slots = [place[:, k * HF:(k + 1) * HF] for place in (stage[:, 0, :], mag2) for k in range(2)]
        NO, OH = 4, H // 4

        pool_passed, pe_passed, dve_passed = (passed[e] for e in ("pool", "pe", "dve"))
        block = ctx.enter_context(nc.Block())

        def real(t):
            return not isinstance(t, int) or 0 <= t < TILES

        def pipeline(eng, step, reach):
            step(-2)
            step(-1)
            with eng.Fori(0, TILES - reach) as i:
                step(i)
            for i in range(TILES - reach, TILES):
                step(i)

        @block.sync
        def _(sp):
            def load_o(t, tok):
                src = o_dram[:, :, bass.ds(tok, TT)].rearrange("h d t -> d h t")
                sp.wait_ge(v_o, NO + min(t, 2) - 1 if isinstance(t, int) else NO + 1)
                if due(t - 2):
                    sp.wait_ge(g_o, t - 2)
                sp.dma_start(o_in[:], src).then_inc(d_o, 16)

            def load_x(t, tok):
                src = x[bass.ds(tok, TT), :]
                sp.wait_ge(v_x1, t)
                sp.dma_start(x_in[:], src).then_inc(d_x, 16)

            def load(t, tok):
                load_o(t, tok)
                load_x(t, tok)

            def store(t, tok):
                dst = out[bass.ds(tok, TT), :]
                sp.wait_ge(g_y, t + 1 if isinstance(t, int) else sp.snap(t + 1))
                sp.dma_start(dst, y[:]).then_inc(d_out, 16)

            for i in range(PIECES):
                sp.dma_start(slots[i].rearrange("p (h n) -> p h n", h=2), wo_v[PIECES + i]).then_inc(d_wo[i], 16)
            sp.dma_start(x_in[:], x[0:TT, :]).then_inc(d_x, 16)
            sp.dma_start(stage[:, 1, 0:HC * HB].rearrange("p (c n) -> p c n", c=HC), had_in.rearrange("(c p) n -> p c n", p=P)
                         ).then_inc(d_had, 16)
            for i in range(2):
                sp.wait_ge(d_stored[i], 16 * B * NG // 2)
            load_o(1, TT)
            for w in range(3):
                sp.dma_start(wt[:, w, :, :].bitcast(BF16), wt_dram[w * WC:(w + 1) * WC].rearrange("c p n -> p c n")
                             ).then_inc(d_wt, 16)
            load_x(1, TT)
            for t in range(2, 4):
                load(t, t * TT)
            with sp.Fori(4, TILES - 1) as t:
                load(sp.snap(t), sp.snap(t * TT))
                store(t - 4, sp.snap((t - 4) * TT))
            load(TILES - 1, LAST_TOK)
            for t in range(TILES - 5, TILES):
                store(t, min(t * TT, LAST_TOK))
            sp.wait_ge(d_out, 16 * TILES)

        @block.gpsimd
        def _(pool):
            nc.gpsimd.memset(x1[:], 0.0).then_inc(g_zero, 1)
            pool.wait_ge(g_zero, 1)

            def inverse_deviation(t):
                pool.wait_ge(v_ve, t + 1)
                nc.gpsimd.tensor_tensor(rstd[:], ve[:], neg_half[:], op=ALU.pow).then_inc(g_rs, 1)

            def low_o(t):
                pool.wait_ge(a_o, t + NO)
                nc.gpsimd.tensor_tensor(o_lo[:], o_in[:], o_hi[:].bitcast(F32), op=ALU.subtract).then_inc(g_o, 1)

            def move_residuals(t):
                if due(t + 1):
                    pool.wait_ge(g_y, t + 1)
                pool.wait_ge(v_x1, min(t + 3, TILES) if isinstance(t, int) else t + 3)
                apart(pool, pool_passed)
                nc.gpsimd.tensor_copy(x1[:, 0, :], x1[:, 1, :]).then_inc(g_old, 1)
                pool.wait_ge(g_old, (t + 2) * 2 + 1)
                apart(pool, pool_passed)
                nc.gpsimd.tensor_copy(x1[:, 1, :], x1[:, 2, :]).then_inc(g_old, 1)

            def rotate_pair0(t):
                pool.wait_ge(v_h, t * NB + 2)
                if due(t * NB):
                    pool.wait_ge(p_hT, t * NB)
                src, dst = (r[:, 0:2, :].rearrange("p n (k j) -> p n k j", j=HB) for r in (hid, half_rot))
                for k, op in enumerate((ALU.add, ALU.subtract)):
                    nc.gpsimd.tensor_tensor(dst[:, :, k, :], src[:, :, 0, :], src[:, :, 1, :], op=op).then_inc(g_pair0, 1)
                pool.wait_ge(g_pair0, t * NB + 2)
                for b, op in enumerate((ALU.add, ALU.subtract)):
                    nc.gpsimd.tensor_tensor(hid[:, b, :], half_rot[:, 0, :], half_rot[:, 1, :], op=op).then_inc(g_pair0, 1)

            def rotate_across(t):
                pool.wait_ge(v_pair1, t * 6 + 6)
                pool.wait_ge(g_pair0, t * NB + NB)
                nc.gpsimd.tensor_tensor(half_rot[:, 2:4, :], hid[:, 0:2, :], hid[:, 2:4, :], op=ALU.subtract).then_inc(g_r2, 1)

            def result(t):
                pool.wait_ge(a_y, t + 1)
                pool.wait_ge(g_old, (t + 2) * 2)
                nc.gpsimd.tensor_tensor(y[:], y[:], x1[:, 0, :], op=ALU.add).then_inc(g_y, 1)

            def step(i):
                if real(i + 1):
                    rotate_pair0(i + 1)
                    rotate_across(i + 1)
                if real(i + 2):
                    inverse_deviation(i + 2)
                if real(i + 3) and not (isinstance(i, int) and i == -2):
                    low_o(i + 3)
                if real(i):
                    result(i)
                move_residuals(i)

            pipeline(pool, step, 3)

        @block.tensor
        def _(pe):
            def out_proj(t, heads):
                if heads[0] == 0:
                    if not (isinstance(t, int) and t == 0):
                        pe.wait_ge(v_o, NO + 1)
                    if due(t - 1):
                        pe.wait_ge(g_o, t - 1)
                    if due(t):
                        pe.wait_ge(v_xT, t)
                for h in heads:
                    if isinstance(t, int) and t == 0 and h % 2 == 0:
                        pe.wait_ge(v_o, h // OH + 1)
                        if h >= HALF:
                            pe.wait_ge(v_w, (h - HALF) // 2 + 1)
                    hi, lo = (a[:, h, :] if h < HALF else b[:, h - HALF, :] for a, b in zip(wo_first, (wo_hi, wo_lo)))
                    for i, (w, m) in enumerate(((o_hi, hi), (o_hi, lo), (o_lo, hi))):
                        last = nc.tensor.matmul(psA[:], w[:, h, :], m, start=(h == 0 and i == 0),
                                                stop=(h == H - 1 and i == 2))
                if heads[-1] == H - 1:
                    last.then_inc(p_out, 1)

            def norm_T(t):
                pe.wait_ge(v_xr, t * 2 + 2)
                for c in range(DC):
                    last = nc.tensor.transpose(psA[:, c * P:(c + 1) * P], xr[:, c * P:(c + 1) * P], ident[:])
                last.then_inc(p_xT, 1)

            def rotate_in(t):
                pe.wait_ge(v_xT, t + 1)
                if due(t):
                    pe.wait_ge(a_mag[0], t)
                if due(t - 1):
                    pe.wait_ge(a_y, t - 1)
                if isinstance(t, int) and t == 0:
                    pe.wait_ge(v_had, 1)
                for k in range(DIM // HB):
                    for c in range(HC):
                        for m in (xT_hi, xT_lo):
                            last = nc.tensor.matmul(psF[:, k * HB:(k + 1) * HB], m[:, k * HC + c, :], had[:, c, :],
                                                    start=(c == 0 and m is xT_hi), stop=(c == HC - 1 and m is xT_lo))
                last.then_inc(p_rx, 1)

            def q1_T(t):
                pe.wait_ge(v_q[0], t + 1)
                if due(t * NB):
                    pe.wait_ge(v_hT, t * NB)
                for c in range(DC):
                    last = nc.tensor.transpose(psTb[1][:, c * P:(c + 1) * P], q1[:, c * P:(c + 1) * P], ident_b[:])
                last.then_inc(p_q1T, 1)

            def gate_up(t):
                pe.wait_ge(a_q1T, t + 1)
                if isinstance(t, int) and t == 0:
                    pe.wait_ge(d_wt, 48)
                if due(2 * t):
                    pe.wait_ge(a_mag[1], 2 * t)
                for j in range(NB):
                    if due(t * NB + j - 1):
                        pe.wait_ge(v_h, t * NB + j - 1)
                    apart(pe, pe_passed)
                    for k in range(2):
                        for c in range(DC):
                            last = nc.tensor.matmul(psB[:, 2 * (j % 2) + k, :], q1T[:, c, :],
                                                    wt[:, k, c, j * DIM:(j + 1) * DIM], start=(c == 0), stop=(c == DC - 1))
                    last.then_inc(p_gu, 1)

            def hidden_T(t, n):
                if n % 2 == 0:
                    pe.wait_ge(g_r2 if n else v_r2, t + 1)
                if n < 2:
                    if due(t * 2):
                        pe.wait_ge(a_q2T, t * 2)
                    pe.wait_ge(a_q1T, t + 1)
                else:
                    pe.wait_ge(v_hT, t * NB + n - 1)
                for c in range(DC):
                    last = nc.tensor.transpose(psT[n % 2][:, c * P:(c + 1) * P], half_rot[:, n, c * P:(c + 1) * P], ident[:])
                last.then_inc(p_hT, 1)

            def rotate_hidden(t, n):
                pe.wait_ge(v_hT, t * NB + n + 1)
                if n == 0:
                    pe.wait_ge(v_h, t * NB + NB)
                for k in range(DIM // HB):
                    for c in range(HC):
                        for m in (hT_hi, hT_lo):
                            last = nc.tensor.matmul(psB[:, n, k * HB:(k + 1) * HB], m[:, n * DC + k * HC + c, :], had[:, c, :],
                                                    start=(c == 0 and m is hT_hi), stop=(c == HC - 1 and m is hT_lo))
                last.then_inc(p_rh, 1)

            def q2_T(t, quantised):
                pe.wait_ge(v_hT, t * NB + NB)
                pe.wait_ge(a_q1T, quantised)
                for k in range(2):
                    pe.wait_ge(v_q[1], 2 * t + k + 1)
                    for c in range(FC // 2):
                        i = k * FC // 2 + c
                        last = nc.tensor.transpose(psTb[k][:, c * P:(c + 1) * P], q2[:, i * P:(i + 1) * P], ident_b[:])
                    last.then_inc(p_q2T, 1)

            def down(t, k, rotated):
                if k == 0:
                    pe.wait_ge(a_mag[0], rotated)
                pe.wait_ge(a_q2T, 2 * t + k + 1)
                apart(pe, pe_passed)
                for i in range(k * FC // 2, (k + 1) * FC // 2):
                    last = nc.tensor.matmul(psF[:], q2T[:, i, :], wt[:, 2, i // WC, (i % WC) * DIM:(i % WC + 1) * DIM],
                                            start=(i == 0), stop=(i == FC - 1))
                if k == 1:
                    last.then_inc(p_down, 1)

            def step(i):
                front = i + 2 if not isinstance(i, int) else min(i + 2, TILES)
                if real(i + 2):
                    out_proj(i + 2, range(0, 6))
                if real(i + 1):
                    q1_T(i + 1)
                if real(i + 2):
                    out_proj(i + 2, range(6, 10))
                if real(i):
                    q2_T(i, front)
                if real(i + 1):
                    gate_up(i + 1)
                if real(i + 2):
                    out_proj(i + 2, range(10, H))
                if real(i):
                    down(i, 0, front)
                if real(i + 1):
                    hidden_T(i + 1, 0)
                    hidden_T(i + 1, 1)
                if real(i):
                    down(i, 1, front)
                if real(i + 1):
                    rotate_hidden(i + 1, 0)
                if real(i + 2):
                    norm_T(i + 2)
                if real(i + 1):
                    rotate_hidden(i + 1, 1)
                    hidden_T(i + 1, 2)
                    hidden_T(i + 1, 3)
                if real(i + 2):
                    rotate_in(i + 2)
                if real(i + 1):
                    rotate_hidden(i + 1, 2)
                    rotate_hidden(i + 1, 3)

            pe.wait_ge(v_ident, 1)
            pipeline(pe, step, 2)

        @block.scalar
        def _(act):
            def high_o(t):
                act.wait_ge(d_o, t * 16)
                act.wait_ge(v_o, NO + min(t, 2) - 1 if isinstance(t, int) else NO + 1)
                act.wait_ge(p_out, t)
                nc.scalar.activation(o_hi[:], o_in[:], ACT.Copy).then_inc(a_o, 1)

            def high_hT(t, n):
                act.wait_ge(p_hT, t * NB + n + 1)
                if n == 0:
                    if due(t * NB):
                        act.wait_ge(p_rh, t * NB)
                nc.scalar.activation(hT_hi[:, n * DC:(n + 1) * DC, :].rearrange("p c t -> p (c t)"),
                                     psT[n % 2][:], ACT.Copy).then_inc(a_hT, 1)

            def high_xT(t):
                act.wait_ge(p_xT, t + 1)
                if due(t):
                    act.wait_ge(p_rx, t)
                nc.scalar.activation(xT_hi[:].rearrange("p c t -> p (c t)"), psA[:], ACT.Copy).then_inc(a_xT, 1)

            def round1(t):
                act.wait_ge(v_scale[0], 5 * t + 4)
                if due(t):
                    act.wait_ge(v_q[0], t)
                nc.scalar.activation(mag1[:], psF[:], ACT.Copy, bias=MAGIC, scale=sq[:, 0:1]).then_inc(a_mag[0], 1)

            def round2(t):
                act.wait_ge(v_scale[1], 5 * t + 4)
                act.wait_ge(v_q[1], 2 * t)
                for k in range(2):
                    nc.scalar.activation(mag2[:, k * HF:(k + 1) * HF],
                                         psB[:, k * NB // 2:(k + 1) * NB // 2, :].rearrange("p n j -> p (n j)"), ACT.Copy,
                                         bias=MAGIC, scale=sq[:, 1:2]).then_inc(a_mag[1], 1)

            def copy_q2T(t, k):
                act.wait_ge(p_q2T, 2 * t + k + 1)
                if k == 0:
                    act.wait_ge(p_down, t)
                nc.scalar.activation(q2T[:, k * FC // 2:(k + 1) * FC // 2, :].rearrange("p c t -> p (c t)"),
                                     psTb[k][:, 0:FC // 2 * TT], ACT.Copy).then_inc(a_q2T, 1)

            def copy_q1T(t):
                act.wait_ge(p_q1T, t + 1)
                if due(t * NB):
                    act.wait_ge(p_gu, t * NB)
                nc.scalar.activation(q1T[:].rearrange("p c t -> p (c t)"), psTb[1][:, 0:DIM], ACT.Copy).then_inc(a_q1T, 1)

            def scale_down(t):
                act.wait_ge(p_down, t + 1)
                act.wait_ge(d_out, t * 16)
                act.wait_ge(v_scale[1], 5 * t + 5)
                nc.scalar.activation(y[:], psF[:], ACT.Copy, scale=ald[:]).then_inc(a_y, 1)

            def silus(t, blocks):
                act.wait_ge(v_scale[0], 5 * t + 5)
                for j in blocks:
                    act.wait_ge(p_gu, t * NB + j + 1)
                    if due(t * NB + j - 1):
                        act.wait_ge(v_h, t * NB + j - 1)
                    nc.scalar.activation(sil[:, j % 2, :], psB[:, 2 * (j % 2), :], ACT.Silu, scale=al[:, 0:1]
                                         ).then_inc(a_sil, 1)

            def step(i):
                if isinstance(i, int) and i == -2:
                    high_o(1)
                if real(i + 1):
                    round1(i + 1)
                if real(i):
                    round2(i)
                if real(i + 1):
                    copy_q1T(i + 1)
                if real(i):
                    copy_q2T(i, 0)
                if real(i + 1):
                    silus(i + 1, (0,))
                if real(i):
                    copy_q2T(i, 1)
                if real(i + 1):
                    silus(i + 1, range(1, NB))
                if real(i + 3) and not (isinstance(i, int) and i == -2):
                    high_o(i + 3)
                if real(i + 1):
                    high_hT(i + 1, 0)
                    high_hT(i + 1, 1)
                if real(i):
                    scale_down(i)
                if real(i + 2):
                    high_xT(i + 2)
                if real(i + 1):
                    high_hT(i + 1, 2)
                    high_hT(i + 1, 3)

            def high_wo(i):
                act.wait_ge(d_wo[i], 48)
                nc.scalar.activation(wo_hi[:, 2 * i:2 * i + 2, :].rearrange("p h n -> p (h n)"), slots[i], ACT.Copy
                                     ).then_inc(a_w, 1)

            act.wait_ge(d_first, 16)
            for k in range(NO):
                heads = slice(k * OH, (k + 1) * OH)
                nc.scalar.activation(o_hi[:, heads, :], o_in[:, heads, :], ACT.Copy).then_inc(a_o, 1)
            for i in range(PIECES):
                high_wo(i)
            nc.scalar.activation(warm[:], neg_half[:], ACT.Silu)
            pipeline(act, step, 3)

        @block.vector
        def _(dve):
            nc.vector.tensor_copy(ident_b[:], ident[:]).then_inc(v_ident, 1)
            for k in range(NO):
                heads = slice(k * OH, (k + 1) * OH)
                dve.wait_ge(a_o, k + 1)
                nc.vector.tensor_tensor(o_lo[:, heads, :], o_in[:, heads, :], o_hi[:, heads, :].bitcast(F32),
                                        ALU.subtract).then_inc(v_o, 1)
            for i in range(PIECES):
                dve.wait_ge(a_w, i + 1)
                heads = slice(2 * i, 2 * i + 2)
                nc.vector.tensor_tensor(wo_lo[:, heads, :].rearrange("p h n -> p (h n)"), slots[i],
                                        wo_hi[:, heads, :].rearrange("p h n -> p (h n)").bitcast(F32),
                                        ALU.subtract).then_inc(v_w, 1)
            dve.wait_ge(v_w, PIECES)
            dve.wait_ge(d_had, 16)
            nc.vector.tensor_copy(had[:].rearrange("p c n -> p (c n)"), stage[:, 1, 0:HC * HB]).then_inc(v_had, 1)

            def low_hT(t, n):
                dve.wait_ge(a_hT, t * NB + n + 1)
                nc.vector.tensor_tensor(hT_lo[:, n * DC:(n + 1) * DC, :].rearrange("p c t -> p (c t)"), psT[n % 2][:],
                                        hT_hi[:, n * DC:(n + 1) * DC, :].rearrange("p c t -> p (c t)").bitcast(F32),
                                        ALU.subtract).then_inc(v_hT, 1)

            def residual(t):
                dve.wait_ge(p_out, t + 1)
                dve.wait_ge(d_x, t * 16 + 16)
                dve.wait_ge(g_zero, 1)
                if due(t * 2):
                    dve.wait_ge(g_old, t * 2)
                if due(t):
                    dve.wait_ge(v_xn, t)
                nc.vector.tensor_tensor(x1[:, 2, :], psA[:], x_in[:], ALU.add).then_inc(v_x1, 1)
                dve.wait_ge(v_x1, t + 1)
                nc.vector.bn_stats(st[:], x1[:, 2, :]).then_inc(v_st, 1)
                dve.wait_ge(v_st, t + 1)
                apart(dve, dve_passed)
                nc.vector.bn_aggr(mv[:], st[:]).then_inc(v_ag, 1)
                dve.wait_ge(v_ag, t + 1)
                nc.vector.tensor_scalar(ve[:], mv[:, 1:2], EPS, None, ALU.add).then_inc(v_ve, 1)

            def norm(t):
                dve.wait_ge(g_rs, t + 1)
                if due(t * 2):
                    dve.wait_ge(v_xr, t * 2)
                nc.vector.tensor_scalar(xn[:], x1[:, 2, :], mv[:, 0:1], rstd[:], ALU.subtract, ALU.mult).then_inc(v_xn, 1)

            def rotate_halves(t):
                dve.wait_ge(v_xn, t + 1)
                if due(t):
                    dve.wait_ge(p_xT, t)
                for k, op in enumerate((ALU.add, ALU.subtract)):
                    nc.vector.tensor_tensor(xr[:, k * HB:(k + 1) * HB], xn[:, 0:HB], xn[:, HB:], op).then_inc(v_xr, 1)

            def low_xT(t):
                dve.wait_ge(a_xT, t + 1)
                nc.vector.tensor_tensor(xT_lo[:].rearrange("p c t -> p (c t)"), psA[:],
                                        xT_hi[:].rearrange("p c t -> p (c t)").bitcast(F32), ALU.subtract).then_inc(v_xT, 1)

            def scales(i, t, peaks, n, factor, weight):
                c = slice(i, i + 1)
                norm_n = float(n) ** -0.5
                if due(t * (i + 1)):
                    dve.wait_ge(a_mag[i], t * (i + 1))
                nc.vector.tensor_reduce(mx[:, c], peaks, axis=AX.X, op=ALU.max, apply_absolute_value=True).then_inc(v_scale[i], 1)
                dve.wait_ge(v_scale[i], 5 * t + 1)
                nc.vector.tensor_scalar(am[:, c], mx[:, c], norm_n, EPS, ALU.mult, ALU.max).then_inc(v_scale[i], 1)
                dve.wait_ge(v_scale[i], 5 * t + 2)
                nc.vector.reciprocal(rc[:, c], am[:, c]).then_inc(v_scale[i], 1)
                dve.wait_ge(v_scale[i], 5 * t + 3)
                nc.vector.tensor_scalar(sq[:, c], rc[:, c], 127.0 * norm_n, None, ALU.mult).then_inc(v_scale[i], 1)
                nc.vector.tensor_scalar(factor, weight, am[:, c], None, ALU.mult).then_inc(v_scale[i], 1)

            def peak(t, n):
                dve.wait_ge(p_rh, t * NB + n + 1)
                if due(5 * t - 4):
                    dve.wait_ge(v_scale[1], 5 * t - 4)
                nc.vector.tensor_reduce(mx4[:, n:n + 1], psB[:, n, :], axis=AX.X, op=ALU.max,
                                        apply_absolute_value=True).then_inc(v_mx4, 1)

            def scales1(t):
                dve.wait_ge(p_rx, t + 1)
                if due(t * NB):
                    dve.wait_ge(a_sil, t * NB)
                if due(t * NB):
                    dve.wait_ge(v_h, t * NB)
                scales(0, t, psF[:], DIM, al[:], w127[:, 0:2])

            def scales2(t):
                dve.wait_ge(v_mx4, t * NB + NB)
                dve.wait_ge(a_y, t)
                scales(1, t, mx4[:], FF, ald[:], w127[:, 2:3])

            def to_int(q, mag, count):
                nc.vector.tensor_scalar(q, mag, MAGIC, 127.0, ALU.subtract, ALU.min).then_inc(count, 1)

            def ints1(t):
                dve.wait_ge(a_mag[0], t + 1)
                if due(t):
                    dve.wait_ge(p_q1T, t)
                to_int(q1[:], mag1[:], v_q[0])

            def ints2(t):
                for k in range(2):
                    dve.wait_ge(a_mag[1], 2 * t + k + 1)
                    dve.wait_ge(p_q2T, 2 * t)
                    to_int(q2[:, k * HF:(k + 1) * HF], mag2[:, k * HF:(k + 1) * HF], v_q[1])

            def hidden(t, j):
                dve.wait_ge(a_sil, t * NB + j + 1)
                if j == 0:
                    if due(t):
                        dve.wait_ge(v_r2, t)
                    if due(t):
                        dve.wait_ge(g_r2, t)
                nc.vector.scalar_tensor_tensor(hid[:, j, :], psB[:, 2 * (j % 2) + 1, :], al[:, 1:2], sil[:, j % 2, :],
                                               ALU.mult, ALU.mult).then_inc(v_h, 1)

            def rotate_within(t, n):
                dve.wait_ge(v_h, t * NB + n + 1)
                if due(t * NB):
                    dve.wait_ge(p_hT, t * NB)
                for k, op in enumerate((ALU.add, ALU.subtract)):
                    nc.vector.tensor_tensor(half_rot[:, n, k * HB:(k + 1) * HB], hid[:, n, 0:HB], hid[:, n, HB:], op
                                            ).then_inc(v_pair1, 1)

            def rotate_pair1(t):
                dve.wait_ge(v_pair1, t * 6 + 4)
                for b, op in enumerate((ALU.add, ALU.subtract)):
                    nc.vector.tensor_tensor(hid[:, 2 + b, :], half_rot[:, 2, :], half_rot[:, 3, :], op).then_inc(v_pair1, 1)

            def rotate_across(t):
                dve.wait_ge(v_pair1, t * 6 + 6)
                dve.wait_ge(g_pair0, t * NB + NB)
                nc.vector.tensor_tensor(half_rot[:, 0:2, :], hid[:, 0:2, :], hid[:, 2:4, :], ALU.add).then_inc(v_r2, 1)

            def step(i):
                if real(i):
                    scales2(i)
                if real(i + 1):
                    ints1(i + 1)
                if real(i):
                    ints2(i)
                if real(i + 1):
                    for n in range(3):
                        hidden(i + 1, n)
                    rotate_within(i + 1, 2)
                    hidden(i + 1, 3)
                    rotate_within(i + 1, 3)
                    rotate_pair1(i + 1)
                    rotate_across(i + 1)
                if real(i + 2):
                    residual(i + 2)
                if real(i + 1):
                    low_hT(i + 1, 0)
                if real(i + 2):
                    norm(i + 2)
                    rotate_halves(i + 2)
                if real(i + 1):
                    low_hT(i + 1, 1)
                if real(i + 2):
                    low_xT(i + 2)
                if isinstance(i, int) and i == -2:
                    dve.wait_ge(a_o, NO + 1)
                    nc.vector.tensor_tensor(o_lo[:], o_in[:], o_hi[:].bitcast(F32), ALU.subtract).then_inc(v_o, 1)
                if real(i + 1):
                    low_hT(i + 1, 2)
                    low_hT(i + 1, 3)
                if real(i + 2):
                    scales1(i + 2)
                if real(i + 1):
                    for n in range(NB):
                        peak(i + 1, n)

            pipeline(dve, step, 2)


def kernel(x, ctx_1024, L0_xattn_Wq, L0_xattn_Wk, L0_xattn_Wv, L0_xattn_Wo, L0_xattn_gq, L0_xattn_gk,
           L0_ffn_w_gate, L0_ffn_w_up, L0_ffn_w_down):
    import numpy as np
    import concourse.bacc as bacc
    from concourse.bass_utils import run_bass_kernel_spmd

    x2 = np.asarray(x).reshape(T, DIM)
    ctx = np.asarray(ctx_1024)
    rows = lambda w: np.asarray(w).T.reshape(4, P, FF)
    down = np.asarray(L0_ffn_w_down).T.reshape(4, 4, P, DIM).transpose(0, 2, 1, 3).reshape(4, P, FF)
    had = np.ones((1, 1), np.float32)
    while had.shape[0] < HB:
        had = np.block([[had, had], [had, -had]])
    arrays = {
        "x": x2, "ctxT": ctx.transpose(0, 2, 1), "ctx_k": ctx, "wq": L0_xattn_Wq, "wk": L0_xattn_Wk, "wv": L0_xattn_Wv,
        "wo": L0_xattn_Wo, "gq": L0_xattn_gq, "gk": L0_xattn_gk,
        "w_ff": np.stack([rows(L0_ffn_w_gate), rows(L0_ffn_w_up), down]),
        "ident": np.eye(P, dtype=np.float32), "had": had,
    }
    arrays = {"in_" + k: np.ascontiguousarray(v) for k, v in arrays.items()}
    nc = bacc.Bacc("TRN2", target_bir_lowering=False, num_devices=1)
    args = [nc.dram_tensor(k, a.shape, F32, kind="ExternalInput").ap() for k, a in arrays.items()]
    out = nc.dram_tensor("out", [T, DIM], F32, kind="ExternalOutput").ap()
    build(nc, *args, out)
    r = run_bass_kernel_spmd(nc, [arrays], core_ids=[0])
    return r.results[0]["out"].reshape(B, SQ, DIM)
```
